# Optimizing a Trainium2 kernel written in Bass

```python
import numpy as np
import jax
import jax.numpy as jnp

def _softmax(x, axis=-1):
    return jax.nn.softmax(x, axis=axis)

def _gelu(x):
    return jax.nn.gelu(x, approximate=True)

def _silu(x):
    return jax.nn.silu(x)

def _sigmoid(x):
    return jax.nn.sigmoid(x)

def _layernorm(x, axis=-1, eps=1e-05):
    m = jnp.mean(x, axis=axis, keepdims=True)
    v = jnp.var(x, axis=axis, keepdims=True)
    return (x - m) / jnp.sqrt(v + eps)

def _scatter_add(tgt, idx, src, axis=0):
    return tgt.at[idx].add(src)

def _segment_sum(src, seg, n):
    return jax.ops.segment_sum(src, seg, n)
kernel_name = 'mk_gnn_preln_d2_gnn_r8_2f7fdb'

def setup_inputs(seed: int=0):
    np.random.seed(seed)
    _w = jnp.asarray

    def _rec_inputs():
        import jax
        import jax.numpy as jnp
        _gk = jax.random.key(seed)
        x = -0.0003713 + 1 * jax.random.normal(jax.random.fold_in(_gk, 1), (6250, 256), jnp.float32)
        src = jax.random.randint(jax.random.fold_in(_gk, 2), (100000,), 0, 6250, jnp.int32)
        dst = jax.random.randint(jax.random.fold_in(_gk, 3), (100000,), 0, 6250, jnp.int32)
        _o = jnp.argsort(dst, stable=True)
        src = src[_o]
        dst = dst[_o]
        edge_type_6 = jax.random.randint(jax.random.fold_in(_gk, 13), (100000,), 0, 6, jnp.int32)
        edge_type_64 = jax.random.randint(jax.random.fold_in(_gk, 14), (100000,), 0, 64, jnp.int32)
        return (x, src, dst, edge_type_6, edge_type_64)
    x, src, dst, edge_type_6, edge_type_64 = _rec_inputs()

    def _L0_gnn_setup():
        import jax, jax.numpy as jnp
        import numpy as np
        N_NODES = 6250
        N_EDGES = 62500
        IN_DIM = 256
        HID = 64
        HEADS = 4
        N_REL = 64
        key = jax.random.key(seed)
        ks = jax.random.split(key, 16)
        s = 0.02
        return {'node_features': jax.random.normal(ks[0], (N_NODES, IN_DIM), jnp.float32), 'edge_index': jax.random.randint(ks[1], (2, N_EDGES), 0, N_NODES, jnp.int32), 'edge_relations': jax.random.randint(ks[2], (N_EDGES,), 0, N_REL, jnp.int32), 'query_emb': jax.random.normal(ks[3], (IN_DIM,), jnp.float32), 'Wq': jax.random.normal(ks[4], (IN_DIM, HID * HEADS), jnp.float32) * s, 'bq': jnp.zeros((HID * HEADS,), jnp.float32), 'Wk': jax.random.normal(ks[5], (IN_DIM, HID * HEADS), jnp.float32) * s, 'bk': jnp.zeros((HID * HEADS,), jnp.float32), 'Wv': jax.random.normal(ks[6], (IN_DIM, HID * HEADS), jnp.float32) * s, 'bv': jnp.zeros((HID * HEADS,), jnp.float32), 'rel_w': jax.random.normal(ks[7], (N_REL, HID), jnp.float32) * s, 'Wo': jax.random.normal(ks[8], (HID * HEADS, IN_DIM), jnp.float32) * s, 'bo': jnp.zeros((IN_DIM,), jnp.float32), 'gamma': jnp.ones((IN_DIM,), jnp.float32), 'beta': jnp.zeros((IN_DIM,), jnp.float32)}
    _L0_gnn_all = _L0_gnn_setup()
    _L0_gnn_in = {k: v for k, v in _L0_gnn_all.items() if k in ('query_emb', 'Wq', 'bq', 'Wk', 'bk', 'Wv', 'bv', 'rel_w', 'Wo', 'bo', 'gamma', 'beta')}
    del _L0_gnn_all

    def _L1_gnn_setup():
        import jax, jax.numpy as jnp
        import numpy as np
        HIDDEN = 256
        NUM_REL = 6
        NUM_BASES = 30
        N_NODES = 6250
        N_EDGES = 100000

        def rgcn_gate_layer(x, src, dst, etype, basis, att, root, bias, gate_w, gate_b):
            N = x.shape[0]
            W = jnp.einsum('rb,bio->rio', att, basis)
            xw = jnp.einsum('nd,rde->rne', x, W)
            msg = xw[etype, src]
            g = jax.nn.sigmoid(msg @ gate_w + gate_b)
            gated = g * msg
            agg = jax.ops.segment_sum(gated, dst, num_segments=N)
            deg = jax.ops.segment_sum(jnp.ones((src.shape[0], 1), x.dtype), dst, num_segments=N)
            agg = agg / jnp.maximum(deg, 1.0)
            return agg + x @ root + bias
        key = jax.random.key(seed)
        ks = jax.random.split(key, 16)
        d = HIDDEN
        inp = {'x': jax.random.normal(ks[0], (N_NODES, d), jnp.float32), 'edge_src': jax.random.randint(ks[1], (N_EDGES,), 0, N_NODES, jnp.int32), 'edge_dst': jax.random.randint(ks[2], (N_EDGES,), 0, N_NODES, jnp.int32), 'edge_type': jax.random.randint(ks[3], (N_EDGES,), 0, NUM_REL, jnp.int32)}

        def glorot(k, shape):
            fan = shape[-2] + shape[-1]
            return jax.random.uniform(k, shape, jnp.float32, -np.sqrt(6.0 / fan), np.sqrt(6.0 / fan))
        for li, off in ((1, 4), (2, 10)):
            inp[f'basis{li}'] = glorot(ks[off + 0], (NUM_BASES, d, d))
            inp[f'att{li}'] = glorot(ks[off + 1], (NUM_REL, NUM_BASES))
            inp[f'root{li}'] = glorot(ks[off + 2], (d, d))
            inp[f'bias{li}'] = jnp.zeros((d,), jnp.float32)
            inp[f'gate_w{li}'] = glorot(ks[off + 3], (d, 1))
            inp[f'gate_b{li}'] = jnp.zeros((1,), jnp.float32)
        return inp
    _L1_gnn_all = _L1_gnn_setup()
    _L1_gnn_in = {k: v for k, v in _L1_gnn_all.items() if k in ('basis1', 'att1', 'root1', 'bias1', 'gate_w1', 'gate_b1', 'basis2', 'att2', 'root2', 'bias2', 'gate_w2', 'gate_b2')}
    del _L1_gnn_all
    return {'x': x, 'src': src, 'dst': dst, 'edge_type_6': edge_type_6, 'edge_type_64': edge_type_64, 'L0_gnn_query_emb': _L0_gnn_in['query_emb'], 'L0_gnn_Wq': _L0_gnn_in['Wq'], 'L0_gnn_bq': _L0_gnn_in['bq'], 'L0_gnn_Wk': _L0_gnn_in['Wk'], 'L0_gnn_bk': _L0_gnn_in['bk'], 'L0_gnn_Wv': _L0_gnn_in['Wv'], 'L0_gnn_bv': _L0_gnn_in['bv'], 'L0_gnn_rel_w': _L0_gnn_in['rel_w'], 'L0_gnn_Wo': _L0_gnn_in['Wo'], 'L0_gnn_bo': _L0_gnn_in['bo'], 'L0_gnn_gamma': _L0_gnn_in['gamma'], 'L0_gnn_beta': _L0_gnn_in['beta'], 'L1_gnn_basis1': _L1_gnn_in['basis1'], 'L1_gnn_att1': _L1_gnn_in['att1'], 'L1_gnn_root1': _L1_gnn_in['root1'], 'L1_gnn_bias1': _L1_gnn_in['bias1'], 'L1_gnn_gate_w1': _L1_gnn_in['gate_w1'], 'L1_gnn_gate_b1': _L1_gnn_in['gate_b1'], 'L1_gnn_basis2': _L1_gnn_in['basis2'], 'L1_gnn_att2': _L1_gnn_in['att2'], 'L1_gnn_root2': _L1_gnn_in['root2'], 'L1_gnn_bias2': _L1_gnn_in['bias2'], 'L1_gnn_gate_w2': _L1_gnn_in['gate_w2'], 'L1_gnn_gate_b2': _L1_gnn_in['gate_b2']}

def reference(x, src, dst, edge_type_6, edge_type_64, L0_gnn_query_emb, L0_gnn_Wq, L0_gnn_bq, L0_gnn_Wk, L0_gnn_bk, L0_gnn_Wv, L0_gnn_bv, L0_gnn_rel_w, L0_gnn_Wo, L0_gnn_bo, L0_gnn_gamma, L0_gnn_beta, L1_gnn_basis1, L1_gnn_att1, L1_gnn_root1, L1_gnn_bias1, L1_gnn_gate_w1, L1_gnn_gate_b1, L1_gnn_basis2, L1_gnn_att2, L1_gnn_root2, L1_gnn_bias2, L1_gnn_gate_w2, L1_gnn_gate_b2):
    import jax
    import jax.numpy as jnp

    def _L0_gnn_ref(node_features, edge_index, edge_relations, query_emb, Wq, bq, Wk, bk, Wv, bv, rel_w, Wo, bo, gamma, beta):
        import jax, jax.numpy as jnp
        import numpy as np
        N_NODES = 6250
        N_EDGES = 62500
        IN_DIM = 256
        HID = 64
        HEADS = 4
        N_REL = 64
        N = node_features.shape[0]
        D = rel_w.shape[1]
        H = Wq.shape[1] // D
        enh = node_features + 0.1 * query_emb[None, :]
        Q = (enh @ Wq + bq).reshape(N, H, D)
        K = (enh @ Wk + bk).reshape(N, H, D)
        V = (enh @ Wv + bv).reshape(N, H, D)
        src, dst = (edge_index[0], edge_index[1])
        rel = rel_w[edge_relations]
        mod_k = K[src] + 0.2 * rel[:, None, :]
        scores = jnp.einsum('ehd,ehd->eh', Q[dst], mod_k) / D ** 0.5
        seg_max = jax.ops.segment_max(scores, dst, num_segments=N)
        ex = jnp.exp(scores - seg_max[dst])
        denom = jax.ops.segment_sum(ex, dst, num_segments=N)
        w = ex / denom[dst]
        agg = jax.ops.segment_sum(w[:, :, None] * V[src], dst, num_segments=N)
        deg = jax.ops.segment_sum(jnp.ones((src.shape[0],), jnp.float32), dst, num_segments=N)
        msgs = jnp.where(deg[:, None, None] > 0, agg, V)
        out = msgs.reshape(N, H * D) @ Wo + bo
        x = out + node_features
        mu = jnp.mean(x, axis=-1, keepdims=True)
        var = jnp.var(x, axis=-1, keepdims=True)
        return (x - mu) / jnp.sqrt(var + 1e-05) * gamma + beta

    def _L1_gnn_ref(x, edge_src, edge_dst, edge_type, basis1, att1, root1, bias1, gate_w1, gate_b1, basis2, att2, root2, bias2, gate_w2, gate_b2):
        import jax, jax.numpy as jnp
        import numpy as np
        HIDDEN = 256
        NUM_REL = 6
        NUM_BASES = 30
        N_NODES = 6250
        N_EDGES = 100000

        def rgcn_gate_layer(x, src, dst, etype, basis, att, root, bias, gate_w, gate_b):
            N = x.shape[0]
            W = jnp.einsum('rb,bio->rio', att, basis)
            xw = jnp.einsum('nd,rde->rne', x, W)
            msg = xw[etype, src]
            g = jax.nn.sigmoid(msg @ gate_w + gate_b)
            gated = g * msg
            agg = jax.ops.segment_sum(gated, dst, num_segments=N)
            deg = jax.ops.segment_sum(jnp.ones((src.shape[0], 1), x.dtype), dst, num_segments=N)
            agg = agg / jnp.maximum(deg, 1.0)
            return agg + x @ root + bias
        h = jax.nn.relu(rgcn_gate_layer(x, edge_src, edge_dst, edge_type, basis1, att1, root1, bias1, gate_w1, gate_b1))
        out = rgcn_gate_layer(h, edge_src, edge_dst, edge_type, basis2, att2, root2, bias2, gate_w2, gate_b2)
        return out
    edge_index = jnp.stack([src, dst])
    h = jnp.maximum(_layernorm(x, axis=-1), 0.0)
    x = x + _L0_gnn_ref(h, edge_index, edge_type_64, L0_gnn_query_emb, L0_gnn_Wq, L0_gnn_bq, L0_gnn_Wk, L0_gnn_bk, L0_gnn_Wv, L0_gnn_bv, L0_gnn_rel_w, L0_gnn_Wo, L0_gnn_bo, L0_gnn_gamma, L0_gnn_beta)
    h = jnp.maximum(_layernorm(x, axis=-1), 0.0)
    x = x + _L1_gnn_ref(h, src, dst, edge_type_6, L1_gnn_basis1, L1_gnn_att1, L1_gnn_root1, L1_gnn_bias1, L1_gnn_gate_w1, L1_gnn_gate_b1, L1_gnn_basis2, L1_gnn_att2, L1_gnn_root2, L1_gnn_bias2, L1_gnn_gate_w2, L1_gnn_gate_b2)
    return x

_drawn_inputs = setup_inputs


def setup_inputs(seed=0):
    import zlib

    import numpy as np

    out = dict(_drawn_inputs(seed))
    spreads = {'L0_gnn_bq': (0.0, 2.0),
     'L0_gnn_bk': (0.0, 2.0),
     'L0_gnn_bv': (0.0, 0.29),
     'L0_gnn_bo': (0.0, 0.1),
     'L0_gnn_gamma': (1.0, 0.2),
     'L0_gnn_beta': (0.0, 0.1),
     'L1_gnn_bias1': (0.0, 0.1),
     'L1_gnn_bias2': (0.0, 0.1)}
    factors = {'L0_gnn_query_emb': 7.939, 'L0_gnn_Wq': 8.0, 'L0_gnn_Wk': 8.0, 'L0_gnn_rel_w': 200.0}
    for name, (base, spread) in spreads.items():
        noise = np.random.default_rng([zlib.crc32(name.encode()), seed]).standard_normal(out[name].shape)
        drawn = base * np.exp(spread * noise) if base else spread * noise
        out[name] = jnp.asarray(drawn.astype(out[name].dtype))
    for name, factor in factors.items():
        out[name] = (out[name] * factor).astype(out[name].dtype)
    return out
```

```python
import numpy as np
import concourse.bass as bass
from concourse import mybir
from contextlib import ExitStack

F32 = mybir.dt.float32
I32 = mybir.dt.int32
ALU = mybir.AluOpType
ACT = mybir.ActivationFunctionType
AX = mybir.AxisListType.X

P = 128
N, D = 6250, 256
E = 100000
HEADS, HD = 4, 64
NTYPE, NREL, NBASE = 64, 6, 30
TILES = -(-N // P)
PAIRS = -(-TILES // 2)
NT = 2 * PAIRS
ROWS = NT * P
LOADROWS = ROWS + 4 * P
CHUNKS = -(-E // P)
FULL = E // P
TAIL = E - FULL * P
QUAD = 4
BODY = 2 * QUAD
STEPS = -(-(CHUNKS + TILES - 1) // BODY) * BODY
TURNS = STEPS // BODY
SG = -(-STEPS // P)
SP_ = SG * P
AW = D + 4
BIG = 1e30
EPS = 1e-5
WP = 2048
WPIECES = (64 * 256) // WP
PAD_DST = N


class Steps:

    def __init__(self, eng, sem):
        self.eng, self.sem, self.base, self.k, self.i, self.per = eng, sem, 0, 0, None, 0

    def enter(self, i, per):
        self.base += self.k
        self.i, self.per, self.k = i, per, 0

    def leave(self, turns):
        assert self.k == self.per, (self.k, self.per)
        self.base += turns * self.per
        self.i, self.k = None, 0

    def __call__(self, ins):
        ins.then_inc(self.sem, 1)
        self.k += 1

    def settle(self):
        if self.i is None:
            self.eng.wait_ge(self.sem, self.base + self.k)
        else:
            self.eng.wait_ge(self.sem, self.i * self.per + (self.base + self.k))

    def then(self, ins):
        self(ins)
        self.settle()


def build(nc, x, src, dst, et6, et64, qe, Wq, bq, Wk, bk, Wv, bv, rel_w, Wo, bo, gamma, beta,
          basis1, att1, root1, bias1, gw1, gb1, basis2, att2, root2, bias2, gw2, gb2, out):
    dram = lambda name, shape, dt=F32: nc.dram_tensor(name, shape, dt, kind="Internal").ap()
    x_d = dram("x_padded", (LOADROWS, D))
    x1_d = dram("x_after_attention", (LOADROWS, D))
    k_d = dram("k_table", (ROWS, D))
    v_d = dram("v_table", (LOADROWS, D))
    g_d = dram("gated_table", (NREL * ROWS, D))
    rec_d = dram("edge_records", (CHUNKS, 4 * P), I32)
    row_d = dram("step_rows", (SP_, 2 * P))
    w_d = [dram(f"w_layer{l}", (4 * NREL, 64 * D)) for l in range(2)]

    ctx = ExitStack()
    with ctx:
        sb = lambda name, shape, dt=F32: ctx.enter_context(nc.sbuf_tensor(name, shape, dt))
        sem = lambda name: ctx.enter_context(nc.semaphore(name))
        pair_of = lambda name: [sem(f"{name}{b}") for b in range(2)]

        qr = sb("qr", [P, NT, D])
        acc = sb("acc", [P, NT, AW])
        sc = sb("sc", [P, SP_, HEADS])
        dl = sb("dl", [P, SP_])
        si = sb("si", [P, SP_], I32)
        ci = sb("ci", [P, SP_], I32)
        wbig = sb("wbig", [P, 2, NREL * D])
        wo = sb("wo", [P, 2, D])
        wroot = sb("wroot", [P, 2, D])
        wgate = sb("wgate", [P, 2, NREL])
        bqkv = sb("bqkv", [P, 3 * D])
        vecs = sb("vecs", [P, 6, D])
        gb = sb("gb", [P, 1])
        rel = sb("rel", [NTYPE, HD])
        ident = sb("ident", [P, P])
        iotaj = sb("iotaj", [P, P])
        npid = sb("npid", [P, 1])
        epsc = sb("epsc", [P, 1])
        ones = sb("ones", [1, P])
        att = sb("att", [4 * NBASE, 2, 4 * NREL])
        rsx = sb("rsx", [P, SG, P + 1])
        gmc = sb("gmc", [P, 2, SG, HEADS])
        trow = sb("trow", [1, SP_], I32)
        stage = sb("stage", [P, 2, QUAD], I32)
        gbuf = sb("gbuf", [P, BODY, AW])
        oh = sb("oh", [P, 2, QUAD, P])
        xt = sb("xt", [P, 2, 2, D])
        vt = sb("vt", [P, 2, 2, D])
        hh = sb("hh", [P, 2, D])
        mm = sb("mm", [P, 2, D])
        mT = sb("mT", [P, 2, 2, P])
        hT = sb("hT", [P, 2, 2, P])
        uu = sb("uu", [P, 2, D])
        kvo = sb("kvo", [P, 2, 2 * D])
        gout = sb("gout", [P, 2, NREL, D])
        st6 = sb("st6", [P, 2, 6])
        mv = sb("mv", [P, 2, 2])
        sd = sb("sd", [P, 2])
        rs = sb("rs", [P, 2])
        nm = sb("nm", [P, 2])
        den = sb("den", [P, 2, HEADS])
        zer = sb("zer", [P, 2, HEADS])
        gate = sb("gate", [P, 2, NREL])
        ps = ctx.enter_context(nc.psum_tensor("ps", [P, 8, 512], F32))

        accf = acc[:, :, :].rearrange("p t c -> p (t c)")
        qrf = qr[:, :, :].rearrange("p t c -> p (t c)")
        scf = sc[:, :, :].rearrange("p s h -> p (s h)")
        goutf = gout[:, :, :, :].rearrange("p a r c -> p (a r c)")
        psf = ps[:, :, :].rearrange("p b c -> p (b c)")

        o = [0]

        def cut(n):
            o[0] += n
            return slice(o[0] - n, o[0])
        recs = accf[:, cut(SG * 512)].bitcast(I32).rearrange("p (g c) -> p g c", g=SG)
        pdb = accf[:, cut(2 * CHUNKS)].rearrange("p (a c) -> p a c", a=2)
        iotac = accf[:, cut(CHUNKS)]
        junk = accf[:, cut(CHUNKS)]
        loc_row = accf[:, cut(SG * 256)].rearrange("p (g c) -> p g c", g=SG)
        key = accf[:, cut(SG * P)].rearrange("p (g c) -> p g c", g=SG)
        srcf = accf[:, cut(SG * P)].rearrange("p (g c) -> p g c", g=SG)
        combf = accf[:, cut(SG * P)].rearrange("p (g c) -> p g c", g=SG)
        assert o[0] <= NT * AW
        bas = [qrf[0:4 * NBASE, b * WP:(b + 1) * WP] for b in range(2)]
        wout = [qrf[0:4 * NREL, (2 + b) * WP:(3 + b) * WP] for b in range(2)]
        o[0] = 4 * WP
        pd = qrf[0:1, cut(2 * CHUNKS)].rearrange("p (a c) -> p a c", a=2)
        krow = qrf[0:1, cut(2 * SP_)].rearrange("p (a c) -> p a c", a=2)
        crow = qrf[0:1, cut(SP_ + 1)]
        assert o[0] <= NT * D
        lohi_i = gbuf[:, :, :].rearrange("p a c -> p (a c)")[0:1, 0:2 * CHUNKS].bitcast(I32)
        o[0] = 0
        lohi = scf[0:1, cut(2 * CHUNKS)]
        ncount = scf[0:1, cut(CHUNKS)]
        zrow = scf[0:1, cut(CHUNKS)]
        scol, cnt, dsel, tilec, inr = (sb(n, [P, SG]) for n in ("scol", "cnt", "dsel", "tilec", "inr"))
        chunk_i = sb("chunk_i", [P, SG], I32)
        zpad = kvo[:, 0, :]
        dpad = sb("dpad", [1, 2 * P], I32)
        sx = [accf[:, a * SG * 512:(a + 1) * SG * 512].rearrange("p (h g c) -> p h g c", h=HEADS, g=SG)
              for a in range(3)]
        ltrow = goutf[0:HEADS, 0:SP_]
        grow = goutf[0:HEADS, SP_:2 * SP_]
        carry = goutf[0:HEADS, 2 * SP_:3 * SP_ + 1]
        lcol = sb("lcol", [P, SG, HEADS])
        ccol = sb("ccol", [P, SG, HEADS])
        bcr = [accf[:, b * 1024:(b + 1) * 1024].rearrange("p (s c) -> p s c", s=QUAD) for b in range(2)]
        ohT = [accf[:, (2 + b) * 1024:(3 + b) * 1024].rearrange("p (s c) -> p s c", s=QUAD) for b in range(2)]

        made = {}

        def sig(stage, what):
            if (stage, what) not in made:
                made[stage, what] = ctx.enter_context(nc.semaphore(f"{stage}_{what}"))
            return made[stage, what]

        stage_ended = sem("stage_ended")
        ended = {}

        def barrier(eng, name):
            ended[name] = ended.get(name, 0) + 1
            eng.drain().then_inc(stage_ended, 1)
            eng.wait_ge(stage_ended, 5 * ended[name])

        block = ctx.enter_context(nc.Block())
        vrow = lambda v: v.rearrange("(a n) -> a n", a=1)
        kxn = lambda w: w.rearrange("(k p) n -> p k n", p=P)
        pairview = lambda t, r0: t[bass.ds(r0, 2 * P), :].rearrange("(a p) c -> p a c", p=P)
        PR = 2 * P
        HALF = PAIRS // 2
        assert PAIRS % 2 == 1
        H2 = CHUNKS // 2

        @block.sync
        def _(sp):
            for b in range(2):
                sp.sem_inc(sig("w", f"stored{b}"), 16)
            sp.sem_inc(sig("n1", "stored"), 32)
            sp.sem_inc(sig("n2", "x1stored"), 16)
            sp.sem_inc(sig("n2", "stored"), 32)
            sp.sem_inc(sig("n3", "stored"), 32)
            sp.sem_inc(sig("n4", "stored"), 16)
            copied, recorded = sig("pre", "copied"), sig("pre", "recorded")
            sp.dma_start(x_d[0:N, :], x[:, :]).then_inc(copied, 16)
            for j, a in enumerate((dst, src, et6, et64)):
                sp.dma_start(rec_d[0:FULL, j * P:(j + 1) * P], a[0:FULL * P].rearrange("(c e) -> c e", e=P)).then_inc(recorded, 16)
                sp.dma_start(rec_d[FULL:FULL + 1, j * P:j * P + TAIL], vrow(a[FULL * P:E])).then_inc(recorded, 16)
            sp.wait_ge(sig("pre", "pads"), 3)
            for j in range(4):
                sp.dma_start(rec_d[FULL:FULL + 1, j * P + TAIL:(j + 1) * P],
                             dpad[0:1, (0 if j == 0 else P):(0 if j == 0 else P) + P - TAIL]).then_inc(recorded, 16)
            n_copied = 16
            for t, r0 in ((x_d, N), (x1_d, ROWS), (v_d, ROWS)):
                for r in range(r0, LOADROWS, P):
                    m = min(P, LOADROWS - r)
                    sp.dma_start(t[r:r + m, :], zpad[0:m, 0:D]).then_inc(copied, 16)
                    n_copied += 16
            sp.wait_ge(recorded, 12 * 16)
            with nc.allow_non_contiguous_dma(reason="first and last destination of each chunk; transposed coefficients"):
                sp.dma_start(lohi_i[0:1, 0:CHUNKS], rec_d[:, 0:1].rearrange("c a -> a c")).then_inc(sig("pre", "lohi"), 16)
                sp.dma_start(lohi_i[0:1, CHUNKS:2 * CHUNKS], rec_d[:, P - 1:P].rearrange("c a -> a c")).then_inc(sig("pre", "lohi"), 16)
                sp.wait_ge(sig("pre", "att0"), 1)
                for l, a in enumerate((att1, att2)):
                    for q in range(4):
                        sp.dma_start(att[q * NBASE:(q + 1) * NBASE, l, q * NREL:(q + 1) * NREL],
                                     a.rearrange("r b -> b r")).then_inc(sig("pre", "att"), 16)
            for dstt, s in ((wbig[:, :, 0:D], kxn(Wq)), (wbig[:, :, D:2 * D], kxn(Wk)), (wbig[:, :, 2 * D:3 * D], kxn(Wv)),
                            (wo[:, :, :], kxn(Wo)), (rel[:, :], rel_w[:, :]),
                            (bqkv[:, 0:D], vrow(bq).to_broadcast([P, D])), (bqkv[:, D:2 * D], vrow(bk).to_broadcast([P, D])),
                            (bqkv[:, 2 * D:3 * D], vrow(bv).to_broadcast([P, D])), (vecs[:, 0, :], vrow(qe).to_broadcast([P, D])),
                            (vecs[:, 1, :], vrow(bo).to_broadcast([P, D])), (vecs[:, 2, :], vrow(gamma).to_broadcast([P, D])),
                            (vecs[:, 3, :], vrow(beta).to_broadcast([P, D]))):
                sp.dma_start(dstt, s).then_inc(sig("pre", "params"), 16)
            for l, bs in enumerate((basis1, basis2)):
                bq4 = bs.rearrange("b (q i) o -> q b (i o)", q=4)
                with sp.Fori(0, WPIECES // 2) as i:
                    for b in range(2):
                        piece = i * 2 + b
                        sp.wait_ge(sig("w", "product"), piece * 4 + (l * WPIECES * 4 + 1))
                        for q in range(4):
                            sp.dma_start(bas[b][q * NBASE:(q + 1) * NBASE, :],
                                         bq4[q][:, bass.ds(piece * WP, WP)]).then_inc(sig("w", f"basis{b}"), 16)
                    for b in range(2):
                        piece = i * 2 + b
                        sp.wait_ge(sig("w", "copied"), piece * 4 + (l * WPIECES * 4 + 4))
                        sp.dma_start(w_d[l][:, bass.ds(piece * WP, WP)], wout[b]).then_inc(sig("w", f"stored{b}"), 16)
            for b in range(2):
                sp.wait_ge(sig("w", f"stored{b}"), 16 + 16 * WPIECES)
            sp.wait_ge(sig("idx", "rows"), 1)
            sp.dma_start(row_d.rearrange("(g p) c -> p g c", p=P), loc_row).then_inc(sig("idx", "rows_stored"), 16)
            sp.wait_ge(sig("idx", "rows_stored"), 16)
            sp.wait_ge(copied, n_copied)
            barrier(sp, "sp")

            def store_kv(n):
                sp.wait_ge(sig("n1", "ready"), n + 1)
                for tb, off in ((k_d, 0), (v_d, D)):
                    sp.dma_start(pairview(tb, n * PR), kvo[:, :, off:off + D]).then_inc(sig("n1", "stored"), 16)

            for b in range(2):
                sp.dma_start(xt[:, b, :, :], pairview(x_d, PR * b)).then_inc(sig("n1", f"tile{b}"), 16)
            with sp.Fori(0, HALF) as i:
                for b in range(2):
                    n = i * 2 + b
                    store_kv(n)
                    sp.dma_start(xt[:, b, :, :], pairview(x_d, n * PR + 2 * PR)).then_inc(sig("n1", f"tile{b}"), 16)
            store_kv(PAIRS - 1)
            sp.wait_ge(sig("n1", "stored"), 32 + PAIRS * 32)
            for b in range(2):
                sp.wait_ge(sig("n1", f"tile{b}"), 16 * (HALF + 1))
            barrier(sp, "sp")

            def layer_params(l, root, bias, gw, gbv):
                loaded = sig(f"g{l}", "loaded")
                wl = w_d[l].rearrange("(q r) (i o) -> q r i o", q=4, o=D)
                for q in range(4):
                    sp.dma_start(wbig[(q % 2) * 64:(q % 2) * 64 + 64, q // 2, :].rearrange("i (r o) -> i r o", r=NREL),
                                 wl[q].rearrange("r i o -> i r o")).then_inc(loaded, 16)
                sp.dma_start(wroot[:, :, :], kxn(root)).then_inc(loaded, 16)
                sp.dma_start(vecs[:, 4, :], vrow(bias).to_broadcast([P, D])).then_inc(loaded, 16)
                sp.dma_start(vecs[:, 5, :], gw.rearrange("k a -> a k").to_broadcast([P, D])).then_inc(loaded, 16)
                sp.dma_start(gb[:, :], vrow(gbv).to_broadcast([P, 1])).then_inc(loaded, 16)
                sp.wait_ge(loaded, 8 * 16)

            layer_params(0, root1, bias1, gw1, gb1)
            with sp.Fori(0, TURNS) as i:
                for b in range(2):
                    sp.wait_ge(sig("a", "rowfree"), i * 2 + (b + 1))
                    sp.dma_start(bcr[b], row_d[bass.ds(i * BODY + b * QUAD, QUAD), :].rearrange("(a s) c -> a s c", a=1)
                                 .to_broadcast([P, QUAD, 2 * P])).then_inc(sig("a", f"row{b}"), 16)
            barrier(sp, "sp")
            barrier(sp, "sp")
            barrier(sp, "sp")

            def store_gated(tag, n):
                sp.wait_ge(sig(tag, "copiedA"), n * 3 + 5)
                sp.wait_ge(sig(tag, "copiedV"), n * 3 + 5)
                for a in range(2):
                    sp.dma_start(g_d.rearrange("(r n) c -> n r c", r=NREL)[bass.ds(n * PR + a * P, P), :, :],
                                 gout[:, a, :, :]).then_inc(sig(tag, "stored"), 16)

            def store_x1(n):
                sp.wait_ge(sig("n2", "x1"), n + 1)
                sp.dma_start(pairview(x1_d, n * PR), uu[:, :, :]).then_inc(sig("n2", "x1stored"), 16)

            def load_xv(b, r0):
                sp.dma_start(xt[:, b, :, :], pairview(x_d, r0)).then_inc(sig("n2", f"tile{b}"), 16)
                sp.dma_start(vt[:, b, :, :], pairview(v_d, r0)).then_inc(sig("n2", f"tile{b}"), 16)

            for b in range(2):
                load_xv(b, PR * b)
            with sp.Fori(0, HALF) as i:
                for b in range(2):
                    n = i * 2 + b
                    store_x1(n)
                    load_xv(b, n * PR + 2 * PR)
                    store_gated("n2", n)
            store_x1(PAIRS - 1)
            store_gated("n2", PAIRS - 1)
            sp.wait_ge(sig("n2", "x1stored"), 16 + 16 * PAIRS)
            sp.wait_ge(sig("n2", "stored"), 32 + 32 * PAIRS)
            for b in range(2):
                sp.wait_ge(sig("n2", f"tile{b}"), 32 * (HALF + 1))
            barrier(sp, "sp")
            layer_params(1, root2, bias2, gw2, gb2)
            barrier(sp, "sp")
            with sp.Fori(0, PAIRS) as i:
                store_gated("n3", i)
            sp.wait_ge(sig("n3", "stored"), 32 + 32 * PAIRS)
            barrier(sp, "sp")
            barrier(sp, "sp")
            for b in range(2):
                sp.dma_start(xt[:, b, :, :], pairview(x1_d, PR * b)).then_inc(sig("n4", f"tile{b}"), 16)
            with sp.Fori(0, HALF) as i:
                for b in range(2):
                    n = i * 2 + b
                    sp.wait_ge(sig("n4", "ready"), n + 1)
                    sp.dma_start(pairview(out, n * PR), hh[:, :, :]).then_inc(sig("n4", "stored"), 16)
                    sp.dma_start(xt[:, b, :, :], pairview(x1_d, n * PR + 2 * PR)).then_inc(sig("n4", f"tile{b}"), 16)
            sp.wait_ge(sig("n4", "ready"), PAIRS)
            last = N - (PAIRS - 1) * PR
            sp.dma_start(out[N - last:N, :], hh[0:last, 0, :]).then_inc(sig("n4", "stored"), 16)
            sp.wait_ge(sig("n4", "stored"), 16 + 16 * PAIRS)
            for b in range(2):
                sp.wait_ge(sig("n4", f"tile{b}"), 16 * (HALF + 1))

        @block.gpsimd
        def _(pool):
            seq = Steps(pool, sem("pool_steps"))
            seq(nc.gpsimd.memset(ident[:, :], 0.0))
            for t, pat, mult in ((iotaj[:, :], [[1, P]], 0), (npid[:, :], [[1, 1]], -1), (scol[:, :], [[P, SG]], 1), (iotac, [[1, CHUNKS]], 0)):
                seq(nc.gpsimd.iota(t, pat, base=0, channel_multiplier=mult, allow_small_or_imprecise_dtypes=True))
            seq.settle()
            pool.affine_select(out=ident[:, :], in_=ident[:, :], compare_op=ALU.not_equal, fill=1.0, base=0,
                               pattern=[[-1, P]], channel_multiplier=1).then_inc(sig("pre", "constants"), 1)
            pool.wait_ge(sig("idx", "chunks"), 1)
            for g in range(SG):
                pool.indirect_dma_start(out=recs[:, g, :], out_offset=None, in_=rec_d[:, :],
                                        in_offset=bass.IndirectOffsetOnAxis(ap=chunk_i[:, g:g + 1], axis=0)).then_inc(sig("idx", "records"), 16)
            pool.wait_ge(sig("idx", "records"), 16 * SG)
            barrier(pool, "pool")
            barrier(pool, "pool")

            def gather_loop(tag, table, index, free, unit):
                with pool.Fori(0, TURNS) as i:
                    for b in range(2):
                        pool.wait_ge(free, i * (2 * unit) + (b + 1) * unit)
                        pool.sem_inc(sig("pool", "go"), 1)
                        nc.gpsimd.tensor_copy(stage[:, b, :], index[:, bass.ds(i * BODY + b * QUAD, QUAD)]).then_inc(sig(tag, "staged"), 1)
                        pool.wait_ge(sig(tag, "staged"), i * 2 + (b + 1))
                        pool.sem_inc(sig("pool", "go"), 1)
                        for k in range(QUAD):
                            pool.indirect_dma_start(out=gbuf[:, b * QUAD + k, 0:D], out_offset=None, in_=table[:, :],
                                                    in_offset=bass.IndirectOffsetOnAxis(ap=stage[:, b, k:k + 1], axis=0)
                                                    ).then_inc(sig(tag, f"gathered{b}{k}"), 16)
                barrier(pool, "pool")

            gather_loop("a", k_d, si, sig("a", "scored"), 1)
            barrier(pool, "pool")
            gather_loop("b", v_d, si, sig("b", "added"), QUAD)
            barrier(pool, "pool")
            gather_loop("l1", g_d, ci, sig("l1", "added"), QUAD)
            barrier(pool, "pool")
            gather_loop("l2", g_d, ci, sig("l2", "added"), QUAD)

        @block.tensor
        def _(pe):
            product = nc.tensor.matmul
            pe.sem_inc(sig("w", "product"), 5)
            pe.sem_inc(sig("a", "expanded"), 2)
            pe.wait_ge(sig("pre", "att"), 16 * 8)
            for l in range(2):
                with pe.Fori(0, WPIECES // 2) as i:
                    for b in range(2):
                        pe.wait_ge(sig("w", f"basis{b}"), i * 64 + (l * 32 * WPIECES + 64))
                        for j in range(4):
                            pe.wait_ge(sig("w", "bankfree"), (i * 2 + b) * 4 + (l * WPIECES * 4 + j + 1))
                            product(ps[0:4 * NREL, j, :], att[:, l, :], bas[b][:, j * 512:(j + 1) * 512],
                                    start=True, stop=True).then_inc(sig("w", "product"), 1)
            pe.wait_ge(sig("idx", "pd"), 1)
            for a in range(2):
                for c in range(2):
                    last = product(ps[:, 4 + 2 * a + c, 0:H2], ones[:, :], pd[:, a, c * H2:(c + 1) * H2], start=True, stop=True)
            last.then_inc(sig("idx", "pd_everywhere"), 1)
            pe.wait_ge(sig("pre", "constants"), 1)
            pe.wait_ge(sig("idx", "rows"), 1)
            pe.wait_ge(sig("w", "copied"), 2 * 4 * WPIECES)
            for g in range(SG):
                nc.tensor.transpose(psf[0:1, g * P:(g + 1) * P], tilec[:, g:g + 1], ident[:, :])
                nc.tensor.transpose(psf[0:1, 1024 + g * P:1024 + (g + 1) * P], key[:, g, 0:1], ident[:, :])
                last = nc.tensor.transpose(psf[0:1, 2048 + g * P:2048 + (g + 1) * P], key[:, g, P - 1:P], ident[:, :])
            last.then_inc(sig("idx", "edges_T"), 1)
            pe.wait_ge(sig("idx", "crow"), 1)
            for g in range(SG):
                product(ps[:, 6, g:g + 1], crow[0:1, g * P:(g + 1) * P], ones[0:1, 0:1], start=True, stop=True)
                last = product(ps[:, 6, 8 + g:9 + g], crow[0:1, g * P + 1:(g + 1) * P + 1], ones[0:1, 0:1], start=True, stop=True)
            last.then_inc(sig("idx", "ccol"), 1)
            for a, v in enumerate((loc_row[:, :, 0:P], srcf, combf)):
                if a:
                    pe.wait_ge(sig("idx", "copied"), a)
                for g in range(SG):
                    last = nc.tensor.transpose(psf[:, g * P:(g + 1) * P], v[:, g, :], ident[:, :])
                last.then_inc(sig("idx", "transposed"), 1)
            barrier(pe, "pe")

            def transpose_pair(source, bank):
                for a in range(2):
                    for k in range(2):
                        last = nc.tensor.transpose(ps[:, bank, (a * 2 + k) * P:(a * 2 + k + 1) * P], source[:, a, k * P:(k + 1) * P], ident[:, :])
                return last

            with pe.Fori(0, PAIRS) as n:
                pe.wait_ge(sig("n1", "operand"), n + 1)
                transpose_pair(mm, 0).then_inc(sig("n1", "T"), 1)
                pe.wait_ge(sig("n1", "Tc"), n + 1)
                for a in range(2):
                    for c0, c1, bank in ((0, 512, 1 + 2 * a), (512, 768, 2 + 2 * a)):
                        for k in range(2):
                            last = product(ps[:, bank, 0:c1 - c0], mT[:, a, k, :], wbig[:, k, c0:c1], start=(k == 0), stop=(k == 1))
                last.then_inc(sig("n1", "qkv"), 1)
            barrier(pe, "pe")

            with pe.Fori(0, TURNS) as i:
                for b in range(2):
                    _, tile_of = nc.values_load_multi_w_load_instructions(
                        trow[0:1, bass.ds(i * BODY + b * QUAD, QUAD)], engines=(pe.engine,), min_val=0, max_val=TILES - 1,
                        skip_runtime_bounds_check_because="clamped when made")
                    pe.wait_ge(sig("a", "onehot"), i * 2 + (b + 1))
                    pe.wait_ge(sig("a", "scored"), i * 2 + (b + 1))
                    for k in range(QUAD):
                        product(ps[:, 2 * b + k // 2, (k % 2) * D:(k % 2 + 1) * D], ohT[b][:, k, 0:P],
                                qr[:, bass.ds(tile_of[k], 1), :].rearrange("p a c -> p (a c)"), start=True, stop=True)
                        last = product(ps[:, 4 + b, k * HD:(k + 1) * HD], ohT[b][0:NTYPE, k, P:2 * P], rel[:, :], start=True, stop=True)
                    last.then_inc(sig("a", "expanded"), 1)
            barrier(pe, "pe")

            for g in range(SG):
                if g >= 2:
                    pe.wait_ge(sig("m", "copied"), g - 1)
                for h in range(HEADS):
                    last = nc.tensor.transpose(ps[:, g % 2, h * P:(h + 1) * P], sc[:, g * P:(g + 1) * P, h], ident[:, :])
                last.then_inc(sig("m", "transposed"), 1)
            for r in range(2):
                pe.wait_ge(sig("m", "last"), r + 1)
                for g in range(SG):
                    nc.tensor.transpose(psf[0:HEADS, 1024 + g * P:1024 + (g + 1) * P], lcol[:, g, :], ident[:, :])
                    last = nc.tensor.transpose(psf[0:HEADS, 2048 + g * P:2048 + (g + 1) * P], gmc[:, r, g, :], ident[:, :])
                last.then_inc(sig("m", "last_T"), 1)
                pe.wait_ge(sig("m", "carry"), r + 1)
                for g in range(SG):
                    last = nc.tensor.transpose(ps[:, 7, g * HEADS:(g + 1) * HEADS], carry[:, g * P + r:(g + 1) * P + r], ident[0:HEADS, 0:HEADS])
                last.then_inc(sig("m", "carry_T"), 1)
            pe.wait_ge(sig("m", "exp"), 1)
            for g in range(SG):
                if g >= 2:
                    pe.wait_ge(sig("m", "back"), g - 1)
                for h in range(HEADS):
                    last = nc.tensor.transpose(ps[:, g % 2, h * P:(h + 1) * P], sx[0][:, h, g, :], ident[:, :])
                last.then_inc(sig("m", "back_T"), 1)
            barrier(pe, "pe")

            def seg_loop(tag):
                with pe.Fori(0, TURNS) as i:
                    for b in range(2):
                        pe.wait_ge(sig(tag, "onehot"), i * 2 + (b + 1))
                        for k in range(QUAD):
                            if tag != "b":
                                pe.wait_ge(sig(tag, f"gathered{b}{k}"), i * 16 + 16)
                            pe.wait_ge(sig(tag, "added"), i * BODY + (b * QUAD + k + 1))
                            product(ps[:, 4 * b + k, 0:AW], oh[:, b, k, :], gbuf[:, b * QUAD + k, :], start=True, stop=True
                                    ).then_inc(sig(tag, "sum"), 1)
                barrier(pe, "pe")

            def gated(tag, n):
                pe.wait_ge(sig(tag, "h"), n + 1)
                transpose_pair(hh, 0).then_inc(sig(tag, "hT"), 1)
                pe.wait_ge(sig(tag, "hTc"), n + 1)
                for a in range(2):
                    for k in range(2):
                        product(ps[:, 1, a * 8:a * 8 + NREL], hT[:, a, k, :], wgate[:, k, :], start=(k == 0), stop=(k == 1))
                for a in range(2):
                    for k in range(2):
                        last = product(ps[:, 2, a * D:(a + 1) * D], hT[:, a, k, :], wroot[:, k, :], start=(k == 0), stop=(k == 1))
                last.then_inc(sig(tag, "gate_root"), 1)
                for a in range(2):
                    for c in range(3):
                        j = a * 3 + c
                        if j % 2:
                            pe.wait_ge(sig(tag, "copiedA"), n * 3 + ((j + 3) // 2))
                        else:
                            pe.wait_ge(sig(tag, "copiedV"), n * 3 + (j // 2 + 1))
                        for k in range(2):
                            last = product(ps[:, 3 + c, :], hT[:, a, k, :], wbig[:, k, c * 512:(c + 1) * 512], start=(k == 0), stop=(k == 1))
                        last.then_inc(sig(tag, "xw"), 1)

            seg_loop("b")
            with pe.Fori(0, PAIRS) as n:
                pe.wait_ge(sig("n2", "operand"), n + 1)
                transpose_pair(mm, 6).then_inc(sig("n2", "T"), 1)
                pe.wait_ge(sig("n2", "Tc"), n + 1)
                for a in range(2):
                    for k in range(2):
                        last = product(ps[:, 7, a * D:(a + 1) * D], mT[:, a, k, :], wo[:, k, :], start=(k == 0), stop=(k == 1))
                last.then_inc(sig("n2", "o"), 1)
                gated("n2", n)
            barrier(pe, "pe")
            seg_loop("l1")
            with pe.Fori(0, PAIRS) as n:
                gated("n3", n)
            barrier(pe, "pe")
            seg_loop("l2")

        @block.scalar
        def _(act):
            A = nc.scalar.activation
            act.sem_inc(sig("w", "bankfree"), 4)
            act.sem_inc(sig("a", "rowfree"), 2)
            for tag in ("n2", "n3"):
                act.sem_inc(sig(tag, "copiedA"), 2)
            for l in range(2):
                with act.Fori(0, WPIECES // 2) as i:
                    for b in range(2):
                        act.wait_ge(sig("w", f"stored{b}"), i * 16 + (l * 8 * WPIECES + 16))
                        for j in range(4):
                            act.wait_ge(sig("w", "product"), (i * 2 + b) * 4 + (l * WPIECES * 4 + j + 6))
                            A(wout[b][:, j * 512:(j + 1) * 512], ps[0:4 * NREL, j, :], ACT.Copy).then_inc(sig("w", "copied"), 1)
                            act.wait_ge(sig("w", "copied"), (i * 2 + b) * 4 + (l * WPIECES * 4 + j + 1))
                            act.sem_inc(sig("w", "bankfree"), 1)
            barrier(act, "act")

            def normalise(stage, n, what, out3, in3, func):
                act.wait_ge(sig(stage, f"{what}_var"), n + 1)
                A(sd[:, :], mv[:, :, 1], ACT.Sqrt, bias=epsc[:, :]).then_inc(sig(stage, f"{what}_sd"), 1)
                act.wait_ge(sig(stage, f"{what}_scale"), n + 1)
                for a in range(2):
                    last = A(out3[:, a, :], in3[:, a, :], func, bias=nm[:, a:a + 1], scale=rs[:, a:a + 1])
                return last

            def n1_pair(n, b):
                normalise("n1", n, "x", hh, xt[:, b, :, :], ACT.Relu).then_inc(sig("n1", "h"), 1)
                act.wait_ge(sig("n1", "T"), n + 1)
                A(mT[:, :, :, :].rearrange("p a k c -> p (a k c)"), ps[:, 0, :], ACT.Copy).then_inc(sig("n1", "Tc"), 1)

            with act.Fori(0, HALF) as i:
                for b in range(2):
                    n1_pair(i * 2 + b, b)
            n1_pair(PAIRS - 1, 0)
            barrier(act, "act")

            with act.Fori(0, TURNS) as i:
                for b in range(2):
                    act.wait_ge(sig("a", f"row{b}"), i * 16 + 16)
                    act.wait_ge(sig("a", "expanded"), i * 2 + (b + 1))
                    A(ohT[b], bcr[b], ACT.Square, bias=npid[:, :]).then_inc(sig("a", "rowfree"), 1)
                    act.wait_ge(sig("a", "rowfree"), i * 2 + (b + 3))
                    A(ohT[b], ohT[b], ACT.Relu, bias=1.0, scale=-1.0).then_inc(sig("a", "onehot"), 1)
            barrier(act, "act")

            for g in range(SG):
                act.wait_ge(sig("m", "transposed"), g + 1)
                A(sx[0][:, :, g, :], ps[:, g % 2, :].rearrange("p (h c) -> p h c", h=HEADS), ACT.Copy).then_inc(sig("m", "copied"), 1)
            act.wait_ge(sig("m", "shifted"), 1)
            A(accf[:, 0:SG * 512], accf[:, 0:SG * 512], ACT.Exp).then_inc(sig("m", "exp"), 1)
            for g in range(SG):
                act.wait_ge(sig("m", "back_T"), g + 1)
                A(sc[:, g * P:(g + 1) * P, :].rearrange("p s h -> p h s"), ps[:, g % 2, :].rearrange("p (h c) -> p h c", h=HEADS),
                  ACT.Copy).then_inc(sig("m", "back"), 1)
            barrier(act, "act")
            barrier(act, "act")

            def gated(tag, n):
                act.wait_ge(sig(tag, "hT"), n + 1)
                A(hT[:, :, :, :].rearrange("p a k c -> p (a k c)"), ps[:, 0, :], ACT.Copy).then_inc(sig(tag, "hTc"), 1)
                act.wait_ge(sig(tag, "gate_root"), n + 1)
                A(gate[:, :, :], ps[:, 1, 0:16].rearrange("p (a r) -> p a r", a=2)[:, :, 0:NREL], ACT.Sigmoid, bias=gb[:, :]).then_inc(sig(tag, "gate"), 1)
                act.wait_ge(sig(tag, "gate"), n + 1)
                act.wait_ge(sig(tag, "stored"), n * 32 + 32)
                for j in (0, 2, 4):
                    a, c = j // 3, j % 3
                    act.wait_ge(sig(tag, "xw"), n * 6 + (j + 1))
                    for e in range(2):
                        r = 2 * c + e
                        last = A(gout[:, a, r, :], ps[:, 3 + c, e * D:(e + 1) * D], ACT.Copy, scale=gate[:, a, r:r + 1])
                    last.then_inc(sig(tag, "copiedA"), 1)

            def n2_pair(n, b):
                act.wait_ge(sig("n2", "T"), n + 1)
                A(mT[:, :, :, :].rearrange("p a k c -> p (a k c)"), ps[:, 6, :], ACT.Copy).then_inc(sig("n2", "Tc"), 1)
                normalise("n2", n, "x", hh, xt[:, b, :, :], ACT.Relu).then_inc(sig("n2", "h0"), 1)
                normalise("n2", n, "u", vt[:, b, :, :], uu, ACT.Identity).then_inc(sig("n2", "un"), 1)
                normalise("n2", n, "y", hh, uu, ACT.Relu).then_inc(sig("n2", "h"), 1)
                gated("n2", n)

            with act.Fori(0, HALF) as i:
                for b in range(2):
                    n2_pair(i * 2 + b, b)
            n2_pair(PAIRS - 1, 0)
            barrier(act, "act")
            barrier(act, "act")
            with act.Fori(0, PAIRS) as n:
                gated("n3", n)
            barrier(act, "act")
            barrier(act, "act")

        @block.vector
        def _(dve):
            V = nc.vector
            seq = Steps(dve, sem("dve_steps"))
            dve.sem_inc(sig("a", "scored"), 2)
            for tag in ("b", "l1", "l2"):
                dve.sem_inc(sig(tag, "added"), BODY)
            for tag in ("n2", "n3"):
                dve.sem_inc(sig(tag, "copiedV"), 2)
            V.memset(att[:, :, :], 0.0).then_inc(sig("pre", "att0"), 1)
            V.memset(zpad, 0.0).then_inc(sig("pre", "pads"), 1)
            V.memset(dpad[:, 0:P], PAD_DST).then_inc(sig("pre", "pads"), 1)
            V.memset(dpad[:, P:2 * P], 0).then_inc(sig("pre", "pads"), 1)
            seq(V.memset(epsc[:, :], EPS))
            seq(V.memset(ones[:, :], 1.0))
            seq(V.memset(zrow, 0.0))
            dve.wait_ge(sig("pre", "lohi"), 32)
            seq.then(V.tensor_scalar(lohi_i, lohi_i, 7, None, ALU.arith_shift_right))
            seq.then(V.tensor_copy(lohi, lohi_i))
            lo, hi = lohi[:, 0:CHUNKS], lohi[:, CHUNKS:2 * CHUNKS]
            seq.then(V.scalar_tensor_tensor(ncount, hi, 1.0, lo, ALU.add, ALU.subtract))
            seq.then(V.tensor_tensor_scan(hi, ncount, zrow, 0.0, ALU.add, ALU.add))
            seq.then(V.tensor_tensor(pd[:, 0, :], hi, ncount, ALU.subtract))
            V.tensor_tensor(pd[:, 1, :], lo, pd[:, 0, :], ALU.subtract).then_inc(sig("idx", "pd"), 1)
            dve.wait_ge(sig("idx", "pd_everywhere"), 1)
            seq.then(V.tensor_copy(pdb[:, :, :].rearrange("p a (c n) -> p a c n", c=2), ps[:, 4:8, 0:H2].rearrange("p (a c) n -> p a c n", a=2)))
            dve.wait_ge(sig("pre", "constants"), 1)
            for g in range(SG):
                seq.then(V.tensor_scalar(junk, pdb[:, 0, :], scol[:, g:g + 1], None, ALU.is_le, ALU.add, accum_out=cnt[:, g:g + 1]))
            seq.then(V.tensor_scalar(cnt[:, :], cnt[:, :], -1.0, None, ALU.add))
            for g in range(SG):
                seq.then(V.scalar_tensor_tensor(junk, iotac, cnt[:, g:g + 1], pdb[:, 1, :], ALU.is_equal, ALU.mult, accum_out=dsel[:, g:g + 1]))
            V.tensor_copy(chunk_i[:, :], cnt[:, :]).then_inc(sig("idx", "chunks"), 1)
            seq.then(V.tensor_tensor(dsel[:, :], dsel[:, :], scol[:, :], ALU.add))
            seq.then(V.tensor_scalar(tilec[:, :], dsel[:, :], float(TILES - 1), None, ALU.min))
            seq.then(V.tensor_scalar(inr[:, :], dsel[:, :], float(P), None, ALU.mult))
            dve.wait_ge(sig("idx", "records"), 16 * SG)
            seq.then(V.tensor_copy(srcf, recs[:, :, 0:P]))
            seq.then(V.tensor_tensor(loc_row[:, :, 0:P], srcf, inr[:, :, None].to_broadcast([P, SG, P]), ALU.subtract))
            seq.then(V.tensor_scalar(key, loc_row[:, :, 0:P], 0.0, None, ALU.is_ge))
            seq.then(V.scalar_tensor_tensor(key, loc_row[:, :, 0:P], float(P), key, ALU.is_lt, ALU.mult))
            seq.then(V.scalar_tensor_tensor(key, srcf, 1.0, key, ALU.add, ALU.mult))
            seq.then(V.tensor_copy(combf, recs[:, :, 2 * P:3 * P]))
            seq.then(V.tensor_copy(srcf, recs[:, :, P:2 * P]))
            seq.then(V.scalar_tensor_tensor(combf, combf, float(ROWS), srcf, ALU.mult, ALU.add))
            V.tensor_copy(loc_row[:, :, P:2 * P], recs[:, :, 3 * P:4 * P]).then_inc(sig("idx", "rows"), 1)
            seq.then(V.tensor_tensor(rsx[:, :, 1:P], key[:, :, 1:P], key[:, :, 0:P - 1], ALU.not_equal))
            seq.then(V.tensor_scalar(rsx[:, :, 1:P], rsx[:, :, 1:P], -BIG, None, ALU.mult))
            dve.wait_ge(sig("idx", "edges_T"), 1)
            seq(V.tensor_copy(trow[:, :], psf[0:1, 0:SP_]))
            seq.then(V.tensor_copy(krow, psf[0:1, 1024:3072].rearrange("p (a c) -> p a c", a=2)[:, :, 0:SP_]))
            seq(V.memset(crow[:, 0:1], -BIG))
            seq(V.memset(crow[:, SP_:SP_ + 1], -BIG))
            seq.then(V.tensor_tensor(crow[:, 1:SP_], krow[:, 0, 1:SP_], krow[:, 1, 0:SP_ - 1], ALU.not_equal))
            V.tensor_scalar(crow[:, 1:SP_], crow[:, 1:SP_], -BIG, None, ALU.mult).then_inc(sig("idx", "crow"), 1)
            dve.wait_ge(sig("idx", "ccol"), 1)
            seq(V.tensor_copy(rsx[:, :, 0:1], ps[:, 6, 0:SG][:, :, None]))
            seq.then(V.tensor_copy(rsx[:, :, P:P + 1], ps[:, 6, 8:8 + SG][:, :, None]))
            for r in range(2):
                seq.then(V.tensor_reduce(inr[:, :], rsx[:, :, r:P + r], AX, ALU.min))
                seq.then(V.tensor_copy(gmc[:, r, :, :], inr[:, :, None].to_broadcast([P, SG, HEADS])))
            for a, t in enumerate((dl, si, ci)):
                dve.wait_ge(sig("idx", "transposed"), a + 1)
                V.tensor_copy(t[:, :], psf[:, 0:SP_]).then_inc(sig("idx", "copied"), 1)
            dve.wait_ge(sig("pre", "params"), 16 * 12)
            for t, f in ((wbig[:, :, 0:D], HD ** -0.5), (bqkv[:, 0:D], HD ** -0.5), (rel[:, :], 0.2), (vecs[:, 0, :], 0.1)):
                seq(V.tensor_scalar(t, t, f, None, ALU.mult))
            seq.settle()
            barrier(dve, "dve")

            def moments(stage, n, what, in3):
                for a in range(2):
                    seq(V.bn_stats(st6[:, a, :], in3[:, a, :]))
                seq.settle()
                dve.sem_inc(sig("dve", "go"), 1)
                seq(V.bn_aggr(mv[:, 0, :], st6[:, 0, :]))
                V.bn_aggr(mv[:, 1, :], st6[:, 1, :]).then_inc(sig(stage, f"{what}_var"), 1)
                dve.wait_ge(sig(stage, f"{what}_sd"), n + 1)
                seq.then(V.reciprocal(rs[:, :], sd[:, :]))
                V.scalar_tensor_tensor(nm[:, :], mv[:, :, 0], -1.0, rs[:, :], ALU.mult, ALU.mult).then_inc(sig(stage, f"{what}_scale"), 1)

            bc2 = lambda v: v[:, None, :].to_broadcast([P, 2, D])

            def n1_pair(i, n, b):
                dve.wait_ge(sig("n1", f"tile{b}"), i * 16 + 16)
                moments("n1", n, "x", xt[:, b, :, :])
                dve.wait_ge(sig("n1", "h"), n + 1)
                V.tensor_tensor(mm[:, :, :], hh[:, :, :], bc2(vecs[:, 0, :]), ALU.add).then_inc(sig("n1", "operand"), 1)
                dve.wait_ge(sig("n1", "qkv"), n + 1)
                dve.wait_ge(sig("n1", "stored"), n * 32 + 32)
                seq(V.tensor_tensor(qr[:, bass.ds(n * 2, 2), :], ps[:, 1:4:2, 0:D], bc2(bqkv[:, 0:D]), ALU.add))
                seq(V.tensor_tensor(kvo[:, :, 0:D], ps[:, 1:4:2, D:2 * D], bc2(bqkv[:, D:2 * D]), ALU.add))
                V.tensor_tensor(kvo[:, :, D:2 * D], ps[:, 2:5:2, 0:D], bc2(bqkv[:, 2 * D:3 * D]), ALU.add).then_inc(sig("n1", "ready"), 1)

            with dve.Fori(0, HALF) as i:
                seq.enter(i, 12)
                for b in range(2):
                    n1_pair(i, i * 2 + b, b)
            seq.leave(HALF)
            n1_pair(HALF, PAIRS - 1, 0)
            seq.settle()
            barrier(dve, "dve")

            seq.then(V.memset(sc[:, STEPS:SP_, :], 0.0))
            with dve.Fori(0, TURNS) as i:
                seq.enter(i, 4)
                for b in range(2):
                    kk = gbuf[:, b * QUAD:(b + 1) * QUAD, 0:D]
                    for k in range(QUAD):
                        dve.wait_ge(sig("a", f"gathered{b}{k}"), i * 16 + 16)
                    dve.wait_ge(sig("a", "expanded"), i * 2 + (b + 3))
                    k4 = kk.rearrange("p k (h d) -> p k h d", h=HEADS)
                    seq.then(V.tensor_tensor(k4, k4, ps[:, 4 + b, 0:QUAD * HD].rearrange("p (k d) -> p k d", k=QUAD)[:, :, None, :]
                                             .to_broadcast([P, QUAD, HEADS, HD]), ALU.add))
                    seq.then(V.tensor_tensor(kk, kk, psf[:, b * 1024:(b + 1) * 1024].rearrange("p (k c) -> p k c", k=QUAD), ALU.mult))
                    V.tensor_reduce(sc[:, bass.ds(i * BODY + b * QUAD, QUAD), :], k4, AX, ALU.add).then_inc(sig("a", "scored"), 1)
            seq.leave(TURNS)
            dve.wait_ge(sig("a", "scored"), 2 + 2 * TURNS)
            barrier(dve, "dve")

            def scans(r, carried):
                for g in range(SG):
                    for h in range(HEADS):
                        first = ccol[:, g, h:h + 1] if carried else -BIG
                        if r == 0:
                            seq(V.tensor_tensor_scan(sx[1][:, h, g, :], rsx[:, g, 0:P], sx[0][:, h, g, :], first, ALU.add, ALU.max))
                        else:
                            seq(V.tensor_tensor_scan(sx[2][:, h, g, ::-1], rsx[:, g, P:0:-1], sx[1][:, h, g, ::-1], first, ALU.add, ALU.max))
                seq.settle()

            dve.wait_ge(sig("m", "copied"), SG)
            for r in range(2):
                scans(r, False)
                end = P - 1 if r == 0 else 0
                V.tensor_copy(lcol[:, :, :], sx[1 + r][:, :, :, end].rearrange("p h g -> p g h")).then_inc(sig("m", "last"), 1)
                dve.wait_ge(sig("m", "last_T"), r + 1)
                seq(V.tensor_copy(ltrow, psf[0:HEADS, 1024:1024 + SP_]))
                seq(V.tensor_copy(grow, psf[0:HEADS, 2048:2048 + SP_]))
                seq.then(V.memset(carry[:, (0 if r == 0 else SP_):(1 if r == 0 else SP_ + 1)], -BIG))
                if r == 0:
                    V.tensor_tensor_scan(carry[:, 1:SP_ + 1], grow, ltrow, -BIG, ALU.add, ALU.max).then_inc(sig("m", "carry"), 1)
                else:
                    V.tensor_tensor_scan(carry[:, 0:SP_][:, ::-1], grow[:, ::-1], ltrow[:, ::-1], -BIG, ALU.add, ALU.max).then_inc(sig("m", "carry"), 1)
                dve.wait_ge(sig("m", "carry_T"), r + 1)
                seq.then(V.tensor_copy(ccol[:, :, :], ps[:, 7, 0:SG * HEADS].rearrange("p (g h) -> p g h", h=HEADS)))
                scans(r, True)
            V.tensor_tensor(accf[:, 0:SG * 512], accf[:, 0:SG * 512], accf[:, 2 * SG * 512:3 * SG * 512], ALU.subtract).then_inc(sig("m", "shifted"), 1)
            barrier(dve, "dve")

            def seg_loop(tag):
                seq.then(V.memset(accf, 0.0))
                if tag == "l1":
                    seq.then(V.memset(gbuf[:, :, D:AW], 1.0))
                added, total = sig(tag, "added"), sig(tag, "sum")

                def make(i, b):
                    at = bass.ds(i * BODY + b * QUAD, QUAD)
                    hot = V.tensor_tensor(oh[:, b, :, :], iotaj[:, None, :].to_broadcast([P, QUAD, P]),
                                          dl[:, at][:, :, None].to_broadcast([P, QUAD, P]), ALU.is_equal)
                    if tag != "b":
                        hot.then_inc(sig(tag, "onehot"), 1)
                        return
                    for k in range(QUAD):
                        dve.wait_ge(sig(tag, f"gathered{b}{k}"), i * 16 + 16)
                    v4 = gbuf[:, b * QUAD:(b + 1) * QUAD, 0:D].rearrange("p k (h d) -> p k h d", h=HEADS)
                    V.tensor_tensor(v4, v4, sc[:, at, :][:, :, :, None].to_broadcast([P, QUAD, HEADS, HD]), ALU.mult)
                    V.tensor_copy(gbuf[:, b * QUAD:(b + 1) * QUAD, D:AW], sc[:, at, :]).then_inc(sig(tag, "onehot"), 1)

                def add(i, b):
                    _, tile_of = nc.values_load_multi_w_load_instructions(
                        trow[0:1, bass.ds(i * BODY + b * QUAD, QUAD)], engines=(dve.engine,), min_val=0, max_val=TILES - 1,
                        skip_runtime_bounds_check_because="clamped when made")
                    for k in range(QUAD):
                        at = acc[:, bass.ds(tile_of[k], 1), :].rearrange("p a c -> p (a c)")
                        dve.wait_ge(total, i * BODY + (b * QUAD + k + 1))
                        dve.wait_ge(added, i * BODY + (BODY + b * QUAD + k))
                        V.tensor_tensor(at, ps[:, 4 * b + k, 0:AW], at, ALU.add).then_inc(added, 1)

                make(0, 0)
                with dve.Fori(0, TURNS - 1) as i:
                    make(i, 1)
                    add(i, 0)
                    make(i + 1, 0)
                    add(i, 1)
                make(TURNS - 1, 1)
                add(TURNS - 1, 0)
                add(TURNS - 1, 1)
                dve.wait_ge(added, BODY + STEPS)
                barrier(dve, "dve")

            def gate_columns(l):
                dve.wait_ge(sig(f"g{l}", "loaded"), 8 * 16)
                for k in range(2):
                    w6 = wbig[:, k, :].rearrange("p (r o) -> p r o", r=NREL)
                    seq.then(V.tensor_tensor(gout[:, 0, :, :], w6, vecs[:, 5, :][:, None, :].to_broadcast([P, NREL, D]), ALU.mult))
                    seq.then(V.tensor_reduce(wgate[:, k, :], gout[:, 0, :, :], AX, ALU.add))

            def gated(tag, n):
                dve.wait_ge(sig(tag, "gate_root"), n + 1)
                seq(V.tensor_tensor(qr[:, bass.ds(n * 2, 2), :], ps[:, 2, :].rearrange("p (a c) -> p a c", a=2), bc2(vecs[:, 4, :]), ALU.add))
                dve.wait_ge(sig(tag, "gate"), n + 1)
                dve.wait_ge(sig(tag, "stored"), n * 32 + 32)
                for j in (1, 3, 5):
                    a, c = j // 3, j % 3
                    dve.wait_ge(sig(tag, "xw"), n * 6 + (j + 1))
                    V.tensor_tensor(gout[:, a, 2 * c:2 * c + 2, :], ps[:, 3 + c, :].rearrange("p (e o) -> p e o", e=2),
                                    gate[:, a, 2 * c:2 * c + 2][:, :, None].to_broadcast([P, 2, D]), ALU.mult).then_inc(sig(tag, "copiedV"), 1)

            seg_loop("b")
            gate_columns(0)

            def n2_pair(i, n, b):
                x2, v2 = xt[:, b, :, :], vt[:, b, :, :]
                a2 = acc[:, bass.ds(n * 2, 2), 0:D].rearrange("p a (h d) -> p a h d", h=HEADS)
                w2 = acc[:, bass.ds(n * 2, 2), D:AW]
                wide = lambda t: t[:, :, :, None].to_broadcast([P, 2, HEADS, HD])
                dve.wait_ge(sig("n2", f"tile{b}"), i * 32 + 32)
                seq(V.tensor_scalar(zer[:, :, :], w2, 0.0, None, ALU.is_equal))
                seq.then(V.tensor_scalar(den[:, :, :], w2, 1e-30, None, ALU.max))
                seq.then(V.reciprocal(den[:, :, :], den[:, :, :]))
                m4 = mm[:, :, :].rearrange("p a (h d) -> p a h d", h=HEADS)
                v4 = v2.rearrange("p a (h d) -> p a h d", h=HEADS)
                seq(V.tensor_tensor(m4, a2, wide(den[:, :, :]), ALU.mult))
                seq.then(V.tensor_tensor(v4, v4, wide(zer[:, :, :]), ALU.mult))
                V.tensor_tensor(mm[:, :, :], mm[:, :, :], v2, ALU.add).then_inc(sig("n2", "operand"), 1)
                moments("n2", n, "x", x2)
                dve.wait_ge(sig("n2", "o"), n + 1)
                dve.wait_ge(sig("n2", "x1stored"), n * 16 + 16)
                seq.then(V.tensor_tensor(uu[:, :, :], ps[:, 7, :].rearrange("p (a c) -> p a c", a=2), bc2(vecs[:, 1, :]), ALU.add))
                dve.wait_ge(sig("n2", "h0"), n + 1)
                seq.then(V.tensor_tensor(uu[:, :, :], uu[:, :, :], hh[:, :, :], ALU.add))
                moments("n2", n, "u", uu)
                dve.wait_ge(sig("n2", "un"), n + 1)
                seq.then(V.tensor_tensor(v2, v2, bc2(vecs[:, 2, :]), ALU.mult))
                seq.then(V.tensor_tensor(v2, v2, bc2(vecs[:, 3, :]), ALU.add))
                V.tensor_tensor(uu[:, :, :], x2, v2, ALU.add).then_inc(sig("n2", "x1"), 1)
                dve.wait_ge(sig("n2", "x1"), n + 1)
                moments("n2", n, "y", uu)
                gated("n2", n)

            with dve.Fori(0, HALF) as i:
                seq.enter(i, 2 * 22)
                for b in range(2):
                    n2_pair(i, i * 2 + b, b)
            seq.leave(HALF)
            n2_pair(HALF, PAIRS - 1, 0)
            seq.settle()
            dve.wait_ge(sig("n2", "copiedV"), 2 + 3 * PAIRS)
            barrier(dve, "dve")
            seg_loop("l1")
            gate_columns(1)

            def mean_plus_root(n):
                seq.then(V.tensor_scalar(den[:, :, 0:1], acc[:, bass.ds(n * 2, 2), D:D + 1], 1.0, None, ALU.max))
                seq.then(V.reciprocal(den[:, :, 1:2], den[:, :, 0:1]))
                for a in range(2):
                    at = bass.ds(n * 2 + a, 1)
                    seq(V.scalar_tensor_tensor(hh[:, a, :], acc[:, at, 0:D].rearrange("p a c -> p (a c)"), den[:, a, 1:2],
                                               qr[:, at, :].rearrange("p a c -> p (a c)"), ALU.mult, ALU.add))
                seq.settle()

            with dve.Fori(0, PAIRS) as n:
                seq.enter(n, 5)
                mean_plus_root(n)
                V.tensor_scalar(hh[:, :, :], hh[:, :, :], 0.0, None, ALU.max).then_inc(sig("n3", "h"), 1)
                gated("n3", n)
            seq.leave(PAIRS)
            dve.wait_ge(sig("n3", "copiedV"), 2 + 3 * PAIRS)
            barrier(dve, "dve")
            seg_loop("l2")

            def n4_pair(i, n, b):
                dve.wait_ge(sig("n4", f"tile{b}"), i * 16 + 16)
                dve.wait_ge(sig("n4", "stored"), n * 16 + 16)
                mean_plus_root(n)
                V.tensor_tensor(hh[:, :, :], hh[:, :, :], xt[:, b, :, :], ALU.add).then_inc(sig("n4", "ready"), 1)

            with dve.Fori(0, HALF) as i:
                seq.enter(i, 8)
                for b in range(2):
                    n4_pair(i, i * 2 + b, b)
            seq.leave(HALF)
            n4_pair(HALF, PAIRS - 1, 0)


_INS = ['x', 'src', 'dst', 'edge_type_6', 'edge_type_64'] + ['L0_gnn_' + n for n in (
    'query_emb', 'Wq', 'bq', 'Wk', 'bk', 'Wv', 'bv', 'rel_w', 'Wo', 'bo', 'gamma', 'beta')] + [
    'L1_gnn_' + n for n in ('basis1', 'att1', 'root1', 'bias1', 'gate_w1', 'gate_b1',
                            'basis2', 'att2', 'root2', 'bias2', 'gate_w2', 'gate_b2')]


def kernel(**inputs):
    import numpy as _np
    import concourse.bacc as _bacc
    from concourse import mybir as _mybir
    from concourse.bass_utils import run_bass_kernel_spmd as _run

    nc = _bacc.Bacc("TRN2", target_bir_lowering=False, num_devices=1)
    arrays, args = {}, []
    for name in _INS:
        a = _np.ascontiguousarray(inputs[name])
        arrays[f"in_{name}"] = a
        args.append(nc.dram_tensor(f"in_{name}", a.shape, _mybir.dt.from_np(a.dtype), kind="ExternalInput").ap())
    o = nc.dram_tensor("out", (N, D), _mybir.dt.float32, kind="ExternalOutput").ap()
    build(nc, *args, o)
    r = _run(nc, [arrays], core_ids=[0])
    return r.results[0]["out"]
```

```python
import numpy as np
import concourse.bass as bass
from concourse import mybir
from contextlib import ExitStack

F32 = mybir.dt.float32
I32 = mybir.dt.int32
ALU = mybir.AluOpType
ACT = mybir.ActivationFunctionType
AX = mybir.AxisListType.X

P = 128
N, D = 6250, 256
E = 100000
HEADS, HD = 4, 64
NTYPE, NREL, NBASE = 64, 6, 30
TILES = -(-N // P)
PAIRS = -(-TILES // 2)
NT = 2 * PAIRS
ROWS = NT * P
LOADROWS = ROWS + 4 * P
CHUNKS = -(-E // P)
FULL = E // P
TAIL = E - FULL * P
QUAD = 4
RING = 4
BODY = RING * QUAD
STEPS = -(-(CHUNKS + TILES - 1) // BODY) * BODY
TURNS = STEPS // BODY
SG = -(-STEPS // P)
SP_ = SG * P
AW = D + 4
BIG = 1e30
EPS = 1e-5
WP = 2048
WPIECES = (64 * 256) // WP
PAD_DST = N


class Steps:

    def __init__(self, eng, sem):
        self.eng, self.sem, self.base, self.k, self.i, self.per = eng, sem, 0, 0, None, 0

    def enter(self, i, per):
        self.base += self.k
        self.i, self.per, self.k = i, per, 0

    def leave(self, turns):
        assert self.k == self.per, (self.k, self.per)
        self.base += turns * self.per
        self.i, self.k = None, 0

    def __call__(self, ins):
        ins.then_inc(self.sem, 1)
        self.k += 1

    def settle(self):
        if self.i is None:
            self.eng.wait_ge(self.sem, self.base + self.k)
        else:
            self.eng.wait_ge(self.sem, self.i * self.per + (self.base + self.k))

    def then(self, ins):
        self(ins)
        self.settle()


def build(nc, x, src, dst, et6, et64, qe, Wq, bq, Wk, bk, Wv, bv, rel_w, Wo, bo, gamma, beta,
          basis1, att1, root1, bias1, gw1, gb1, basis2, att2, root2, bias2, gw2, gb2, out):
    dram = lambda name, shape, dt=F32: nc.dram_tensor(name, shape, dt, kind="Internal").ap()
    x_d = dram("x_padded", (LOADROWS, D))
    x1_d = dram("x_after_attention", (LOADROWS, D))
    k_d = dram("k_table", (ROWS, D))
    v_d = dram("v_table", (LOADROWS, D))
    g_d = dram("gated_table", (NREL * ROWS, D))
    rec_d = dram("edge_records", (CHUNKS, 4 * P), I32)
    row_d = dram("step_rows", (SP_, 2 * P))
    w_d = [dram(f"w_layer{l}", (4 * NREL, 64 * D)) for l in range(2)]

    ctx = ExitStack()
    with ctx:
        sb = lambda name, shape, dt=F32: ctx.enter_context(nc.sbuf_tensor(name, shape, dt))
        sem = lambda name: ctx.enter_context(nc.semaphore(name))
        pair_of = lambda name: [sem(f"{name}{b}") for b in range(2)]

        qr = sb("qr", [P, NT, D])
        acc = sb("acc", [P, NT, AW])
        sc = sb("sc", [P, SP_, HEADS])
        dl = sb("dl", [P, SP_])
        si = sb("si", [P, SP_], I32)
        ci = sb("ci", [P, SP_], I32)
        wbig = sb("wbig", [P, 2, NREL * D])
        wo = sb("wo", [P, 2, D])
        wroot = sb("wroot", [P, 2, D])
        wgate = sb("wgate", [P, 2, NREL])
        bqkv = sb("bqkv", [P, 3 * D])
        vecs = sb("vecs", [P, 6, D])
        gb = sb("gb", [P, 1])
        rel = sb("rel", [NTYPE, HD])
        ident = sb("ident", [P, P])
        iotaj = sb("iotaj", [P, P])
        npid = sb("npid", [P, 1])
        epsc = sb("epsc", [P, 1])
        ones = sb("ones", [1, P])
        att = sb("att", [4 * NBASE, 2, 4 * NREL])
        rsx = sb("rsx", [P, SG, P + 1])
        gmc = sb("gmc", [P, 2, SG, HEADS])
        trow = sb("trow", [1, SP_], I32)
        stage = sb("stage", [P, RING, QUAD], I32)
        shared = sb("shared", [P, BODY * AW])
        gbuf = shared[:, :].rearrange("p (s c) -> p s c", s=BODY)
        gout = shared[:, 0:2 * NREL * D].rearrange("p (a r c) -> p a r c", a=2, r=NREL)
        kvo = shared[:, 2 * NREL * D:2 * NREL * D + 4 * D].rearrange("p (a c) -> p a c", a=2)
        oh = sb("oh", [P, 2, QUAD, P])
        xt = sb("xt", [P, 2, 2, D])
        vt = sb("vt", [P, 2, 2, D])
        hh = sb("hh", [P, 2, D])
        mm = sb("mm", [P, 2, D])
        h0 = sb("h0", [P, 2, D])
        mTs = [sb(f"mT{b}", [P, 2, 2, P]) for b in range(2)]
        hTs = [sb(f"hT{b}", [P, 2, 2, P]) for b in range(2)]
        uu = sb("uu", [P, 2, D])
        st6 = sb("st6", [P, 2, 6])
        mv = sb("mv", [P, 2, 2])
        sd = sb("sd", [P, 2])
        rs = sb("rs", [P, 2])
        nm = sb("nm", [P, 2])
        den = sb("den", [P, 2, HEADS])
        zer = sb("zer", [P, 2, HEADS])
        gate = sb("gate", [P, 2, NREL])
        ps = ctx.enter_context(nc.psum_tensor("ps", [P, 8, 512], F32))

        accf = acc[:, :, :].rearrange("p t c -> p (t c)")
        qrf = qr[:, :, :].rearrange("p t c -> p (t c)")
        scf = sc[:, :, :].rearrange("p s h -> p (s h)")
        goutf = shared[:, 0:2 * NREL * D]
        psf = ps[:, :, :].rearrange("p b c -> p (b c)")

        o = [0]

        def cut(n):
            o[0] += n
            return slice(o[0] - n, o[0])
        recs = accf[:, cut(SG * 512)].bitcast(I32).rearrange("p (g c) -> p g c", g=SG)
        pdb = accf[:, cut(2 * CHUNKS)].rearrange("p (a c) -> p a c", a=2)
        iotac = accf[:, cut(CHUNKS)]
        junk = accf[:, cut(CHUNKS)]
        loc_row = accf[:, cut(SG * 256)].rearrange("p (g c) -> p g c", g=SG)
        key = accf[:, cut(SG * P)].rearrange("p (g c) -> p g c", g=SG)
        srcf = accf[:, cut(SG * P)].rearrange("p (g c) -> p g c", g=SG)
        combf = accf[:, cut(SG * P)].rearrange("p (g c) -> p g c", g=SG)
        assert o[0] <= NT * AW
        bas = [qrf[0:4 * NBASE, b * WP:(b + 1) * WP] for b in range(2)]
        wout = [qrf[0:4 * NREL, (2 + b) * WP:(3 + b) * WP] for b in range(2)]
        o[0] = 4 * WP
        pd = qrf[0:1, cut(2 * CHUNKS)].rearrange("p (a c) -> p a c", a=2)
        krow = qrf[0:1, cut(2 * SP_)].rearrange("p (a c) -> p a c", a=2)
        crow = qrf[0:1, cut(SP_ + 1)]
        assert o[0] <= NT * D
        lohi_i = shared[0:1, 0:2 * CHUNKS].bitcast(I32)
        o[0] = 0
        lohi = scf[0:1, cut(2 * CHUNKS)]
        ncount = scf[0:1, cut(CHUNKS)]
        zrow = scf[0:1, cut(CHUNKS)]
        scol, cnt, dsel, tilec, inr = (sb(n, [P, SG]) for n in ("scol", "cnt", "dsel", "tilec", "inr"))
        chunk_i = sb("chunk_i", [P, SG], I32)
        zpad = kvo[:, 0, :]
        dpad = sb("dpad", [1, 2 * P], I32)
        sx = [accf[:, a * SG * 512:(a + 1) * SG * 512].rearrange("p (h g c) -> p h g c", h=HEADS, g=SG)
              for a in range(3)]
        ltrow = goutf[0:HEADS, 0:SP_]
        grow = goutf[0:HEADS, SP_:2 * SP_]
        carry = goutf[0:HEADS, 2 * SP_:3 * SP_ + 1]
        lcol = sb("lcol", [P, SG, HEADS])
        ccol = sb("ccol", [P, SG, HEADS])
        bcr = [accf[:, b * 1024:(b + 1) * 1024].rearrange("p (s c) -> p s c", s=QUAD) for b in range(2)]
        ohT = [accf[:, (2 + b) * 1024:(3 + b) * 1024].rearrange("p (s c) -> p s c", s=QUAD) for b in range(2)]

        made = {}

        def sig(stage, what):
            if (stage, what) not in made:
                made[stage, what] = ctx.enter_context(nc.semaphore(f"{stage}_{what}"))
            return made[stage, what]

        stage_ended = sem("stage_ended")
        ended = {}

        def barrier(eng, name):
            ended[name] = ended.get(name, 0) + 1
            eng.drain().then_inc(stage_ended, 1)
            eng.wait_ge(stage_ended, 5 * ended[name])

        block = ctx.enter_context(nc.Block())
        vrow = lambda v: v.rearrange("(a n) -> a n", a=1)
        kxn = lambda w: w.rearrange("(k p) n -> p k n", p=P)
        pairview = lambda t, r0: t[bass.ds(r0, 2 * P), :].rearrange("(a p) c -> p a c", p=P)
        PR = 2 * P
        HALF = PAIRS // 2
        assert PAIRS % 2 == 1
        H2 = CHUNKS // 2

        @block.sync
        def _(sp):
            for b in range(2):
                sp.sem_inc(sig("w", f"stored{b}"), 16)
            sp.sem_inc(sig("n1", "stored"), 32)
            sp.sem_inc(sig("n2", "x1stored"), 16)
            sp.sem_inc(sig("n2", "stored"), 32)
            sp.sem_inc(sig("n3", "stored"), 32)
            sp.sem_inc(sig("n4", "stored"), 16)
            copied, recorded = sig("pre", "copied"), sig("pre", "recorded")
            sp.dma_start(x_d[0:N, :], x[:, :]).then_inc(copied, 16)
            for j, a in enumerate((dst, src, et6, et64)):
                sp.dma_start(rec_d[0:FULL, j * P:(j + 1) * P], a[0:FULL * P].rearrange("(c e) -> c e", e=P)).then_inc(recorded, 16)
                sp.dma_start(rec_d[FULL:FULL + 1, j * P:j * P + TAIL], vrow(a[FULL * P:E])).then_inc(recorded, 16)
            sp.wait_ge(sig("pre", "pads"), 3)
            for j in range(4):
                sp.dma_start(rec_d[FULL:FULL + 1, j * P + TAIL:(j + 1) * P],
                             dpad[0:1, (0 if j == 0 else P):(0 if j == 0 else P) + P - TAIL]).then_inc(recorded, 16)
            n_copied = 16
            for t, r0 in ((x_d, N), (x1_d, ROWS), (v_d, ROWS)):
                for r in range(r0, LOADROWS, P):
                    m = min(P, LOADROWS - r)
                    sp.dma_start(t[r:r + m, :], zpad[0:m, 0:D]).then_inc(copied, 16)
                    n_copied += 16
            sp.wait_ge(recorded, 12 * 16)
            with nc.allow_non_contiguous_dma(reason="first and last destination of each chunk; transposed coefficients"):
                sp.dma_start(lohi_i[0:1, 0:CHUNKS], rec_d[:, 0:1].rearrange("c a -> a c")).then_inc(sig("pre", "lohi"), 16)
                sp.dma_start(lohi_i[0:1, CHUNKS:2 * CHUNKS], rec_d[:, P - 1:P].rearrange("c a -> a c")).then_inc(sig("pre", "lohi"), 16)
                sp.wait_ge(sig("pre", "att0"), 1)
                for l, a in enumerate((att1, att2)):
                    for q in range(4):
                        sp.dma_start(att[q * NBASE:(q + 1) * NBASE, l, q * NREL:(q + 1) * NREL],
                                     a.rearrange("r b -> b r")).then_inc(sig("pre", "att"), 16)
            for dstt, s in ((wbig[:, :, 0:D], kxn(Wq)), (wbig[:, :, D:2 * D], kxn(Wk)), (wbig[:, :, 2 * D:3 * D], kxn(Wv)),
                            (wo[:, :, :], kxn(Wo)), (rel[:, :], rel_w[:, :]),
                            (bqkv[:, 0:D], vrow(bq).to_broadcast([P, D])), (bqkv[:, D:2 * D], vrow(bk).to_broadcast([P, D])),
                            (bqkv[:, 2 * D:3 * D], vrow(bv).to_broadcast([P, D])), (vecs[:, 0, :], vrow(qe).to_broadcast([P, D])),
                            (vecs[:, 1, :], vrow(bo).to_broadcast([P, D])), (vecs[:, 2, :], vrow(gamma).to_broadcast([P, D])),
                            (vecs[:, 3, :], vrow(beta).to_broadcast([P, D]))):
                sp.dma_start(dstt, s).then_inc(sig("pre", "params"), 16)
            for l, bs in enumerate((basis1, basis2)):
                bq4 = bs.rearrange("b (q i) o -> q b (i o)", q=4)
                with sp.Fori(0, WPIECES // 2) as i:
                    for b in range(2):
                        piece = i * 2 + b
                        sp.wait_ge(sig("w", "product"), piece * 4 + (l * WPIECES * 4 + 1))
                        for q in range(4):
                            sp.dma_start(bas[b][q * NBASE:(q + 1) * NBASE, :],
                                         bq4[q][:, bass.ds(piece * WP, WP)]).then_inc(sig("w", f"basis{b}"), 16)
                    for b in range(2):
                        piece = i * 2 + b
                        sp.wait_ge(sig("w", "copied"), piece * 4 + (l * WPIECES * 4 + 4))
                        sp.dma_start(w_d[l][:, bass.ds(piece * WP, WP)], wout[b]).then_inc(sig("w", f"stored{b}"), 16)
            for b in range(2):
                sp.wait_ge(sig("w", f"stored{b}"), 16 + 16 * WPIECES)
            sp.wait_ge(sig("idx", "rows"), 1)
            sp.dma_start(row_d.rearrange("(g p) c -> p g c", p=P), loc_row).then_inc(sig("idx", "rows_stored"), 16)
            sp.wait_ge(sig("idx", "rows_stored"), 16)
            sp.wait_ge(copied, n_copied)
            barrier(sp, "sp")

            def store_kv(n):
                sp.wait_ge(sig("n1", "used"), n * 2 + 4)
                for tb, off in ((k_d, 0), (v_d, D)):
                    sp.dma_start(pairview(tb, n * PR), kvo[:, :, off:off + D]).then_inc(sig("n1", "stored"), 16)

            for b in range(2):
                sp.dma_start(xt[:, b, :, :], pairview(x_d, PR * b)).then_inc(sig("n1", f"tile{b}"), 16)
            with sp.Fori(0, HALF) as i:
                for b in range(2):
                    n = i * 2 + b
                    store_kv(n)
                    sp.dma_start(xt[:, b, :, :], pairview(x_d, n * PR + 2 * PR)).then_inc(sig("n1", f"tile{b}"), 16)
            store_kv(PAIRS - 1)
            sp.wait_ge(sig("n1", "stored"), 32 + PAIRS * 32)
            for b in range(2):
                sp.wait_ge(sig("n1", f"tile{b}"), 16 * (HALF + 1))
            barrier(sp, "sp")

            def layer_params(l, root, bias, gw, gbv):
                loaded = sig(f"g{l}", "loaded")
                wl = w_d[l].rearrange("(q r) (i o) -> q r i o", q=4, o=D)
                for q in range(4):
                    sp.dma_start(wbig[(q % 2) * 64:(q % 2) * 64 + 64, q // 2, :].rearrange("i (r o) -> i r o", r=NREL),
                                 wl[q].rearrange("r i o -> i r o")).then_inc(loaded, 16)
                sp.dma_start(wroot[:, :, :], kxn(root)).then_inc(loaded, 16)
                sp.dma_start(vecs[:, 4, :], vrow(bias).to_broadcast([P, D])).then_inc(loaded, 16)
                sp.dma_start(vecs[:, 5, :], gw.rearrange("k a -> a k").to_broadcast([P, D])).then_inc(loaded, 16)
                sp.dma_start(gb[:, :], vrow(gbv).to_broadcast([P, 1])).then_inc(loaded, 16)
                sp.wait_ge(loaded, 8 * 16)

            layer_params(0, root1, bias1, gw1, gb1)
            with sp.Fori(0, TURNS) as i:
                for u in range(RING):
                    b = u % 2
                    sp.wait_ge(sig("a", "rowfree"), i * RING + (u + 1))
                    sp.dma_start(bcr[b], row_d[bass.ds(i * BODY + u * QUAD, QUAD), :].rearrange("(a s) c -> a s c", a=1)
                                 .to_broadcast([P, QUAD, 2 * P])).then_inc(sig("a", f"row{b}"), 16)
            barrier(sp, "sp")
            barrier(sp, "sp")
            barrier(sp, "sp")

            def store_gated(tag, n):
                sp.wait_ge(sig(tag, "copiedA"), n * 3 + 5)
                sp.wait_ge(sig(tag, "copiedV"), n * 3 + 5)
                for a in range(2):
                    sp.dma_start(g_d.rearrange("(r n) c -> n r c", r=NREL)[bass.ds(n * PR + a * P, P), :, :],
                                 gout[:, a, :, :]).then_inc(sig(tag, "stored"), 16)

            def store_x1(n):
                sp.wait_ge(sig("n2", "x1"), n + 1)
                sp.dma_start(pairview(x1_d, n * PR), uu[:, :, :]).then_inc(sig("n2", "x1stored"), 16)

            def load_xv(b, r0):
                sp.dma_start(xt[:, b, :, :], pairview(x_d, r0)).then_inc(sig("n2", f"tile{b}"), 16)
                sp.dma_start(vt[:, b, :, :], pairview(v_d, r0)).then_inc(sig("n2", f"tile{b}"), 16)

            for b in range(2):
                load_xv(b, PR * b)
            with sp.Fori(0, HALF) as i:
                for b in range(2):
                    n = i * 2 + b
                    store_x1(n)
                    load_xv(b, n * PR + 2 * PR)
                    store_gated("n2", n)
            store_x1(PAIRS - 1)
            store_gated("n2", PAIRS - 1)
            sp.wait_ge(sig("n2", "x1stored"), 16 + 16 * PAIRS)
            sp.wait_ge(sig("n2", "stored"), 32 + 32 * PAIRS)
            for b in range(2):
                sp.wait_ge(sig("n2", f"tile{b}"), 32 * (HALF + 1))
            barrier(sp, "sp")
            layer_params(1, root2, bias2, gw2, gb2)
            barrier(sp, "sp")
            with sp.Fori(0, PAIRS) as i:
                store_gated("n3", i)
            sp.wait_ge(sig("n3", "stored"), 32 + 32 * PAIRS)
            barrier(sp, "sp")
            barrier(sp, "sp")
            for b in range(2):
                sp.dma_start(xt[:, b, :, :], pairview(x1_d, PR * b)).then_inc(sig("n4", f"tile{b}"), 16)
            with sp.Fori(0, HALF) as i:
                for b in range(2):
                    n = i * 2 + b
                    sp.wait_ge(sig("n4", "ready"), n + 1)
                    sp.dma_start(pairview(out, n * PR), hh[:, :, :]).then_inc(sig("n4", "stored"), 16)
                    sp.dma_start(xt[:, b, :, :], pairview(x1_d, n * PR + 2 * PR)).then_inc(sig("n4", f"tile{b}"), 16)
            sp.wait_ge(sig("n4", "ready"), PAIRS)
            last = N - (PAIRS - 1) * PR
            sp.dma_start(out[N - last:N, :], hh[0:last, 0, :]).then_inc(sig("n4", "stored"), 16)
            sp.wait_ge(sig("n4", "stored"), 16 + 16 * PAIRS)
            for b in range(2):
                sp.wait_ge(sig("n4", f"tile{b}"), 16 * (HALF + 1))

        @block.gpsimd
        def _(pool):
            seq = Steps(pool, sem("pool_steps"))
            seq(nc.gpsimd.memset(ident[:, :], 0.0))
            for t, pat, mult in ((iotaj[:, :], [[1, P]], 0), (npid[:, :], [[1, 1]], -1), (scol[:, :], [[P, SG]], 1), (iotac, [[1, CHUNKS]], 0)):
                seq(nc.gpsimd.iota(t, pat, base=0, channel_multiplier=mult, allow_small_or_imprecise_dtypes=True))
            seq.settle()
            pool.affine_select(out=ident[:, :], in_=ident[:, :], compare_op=ALU.not_equal, fill=1.0, base=0,
                               pattern=[[-1, P]], channel_multiplier=1).then_inc(sig("pre", "constants"), 1)
            pool.wait_ge(sig("idx", "chunks"), 1)
            for g in range(SG):
                pool.indirect_dma_start(out=recs[:, g, :], out_offset=None, in_=rec_d[:, :],
                                        in_offset=bass.IndirectOffsetOnAxis(ap=chunk_i[:, g:g + 1], axis=0)).then_inc(sig("idx", "records"), 16)
            pool.wait_ge(sig("idx", "records"), 16 * SG)
            barrier(pool, "pool")
            barrier(pool, "pool")

            def gather_loop(tag, table):
                with pool.Fori(0, TURNS) as i:
                    for u in range(RING):
                        pool.wait_ge(sig(tag, "staged"), i * RING + (u + 1))
                        pool.sem_inc(sig("pool", "go"), 1)
                        for k in range(QUAD):
                            pool.indirect_dma_start(out=gbuf[:, u * QUAD + k, 0:D], out_offset=None, in_=table[:, :],
                                                    in_offset=bass.IndirectOffsetOnAxis(ap=stage[:, u, k:k + 1], axis=0)
                                                    ).then_inc(sig(tag, f"gathered{u}"), 16)
                barrier(pool, "pool")

            gather_loop("a", k_d)
            barrier(pool, "pool")
            gather_loop("b", v_d)
            barrier(pool, "pool")
            gather_loop("l1", g_d)
            barrier(pool, "pool")
            gather_loop("l2", g_d)

        @block.tensor
        def _(pe):
            product = nc.tensor.matmul
            pe.sem_inc(sig("w", "product"), 5)
            pe.sem_inc(sig("a", "expanded"), 2)
            pe.wait_ge(sig("pre", "att"), 16 * 8)
            for l in range(2):
                with pe.Fori(0, WPIECES // 2) as i:
                    for b in range(2):
                        pe.wait_ge(sig("w", f"basis{b}"), i * 64 + (l * 32 * WPIECES + 64))
                        for j in range(4):
                            pe.wait_ge(sig("w", "bankfree"), (i * 2 + b) * 4 + (l * WPIECES * 4 + j + 1))
                            product(ps[0:4 * NREL, j, :], att[:, l, :], bas[b][:, j * 512:(j + 1) * 512],
                                    start=True, stop=True).then_inc(sig("w", "product"), 1)
            pe.wait_ge(sig("idx", "pd"), 1)
            for a in range(2):
                for c in range(2):
                    last = product(ps[:, 4 + 2 * a + c, 0:H2], ones[:, :], pd[:, a, c * H2:(c + 1) * H2], start=True, stop=True)
            last.then_inc(sig("idx", "pd_everywhere"), 1)
            pe.wait_ge(sig("pre", "constants"), 1)
            pe.wait_ge(sig("idx", "rows"), 1)
            pe.wait_ge(sig("w", "copied"), 2 * 4 * WPIECES)
            for g in range(SG):
                nc.tensor.transpose(psf[0:1, g * P:(g + 1) * P], tilec[:, g:g + 1], ident[:, :])
                nc.tensor.transpose(psf[0:1, 1024 + g * P:1024 + (g + 1) * P], key[:, g, 0:1], ident[:, :])
                last = nc.tensor.transpose(psf[0:1, 2048 + g * P:2048 + (g + 1) * P], key[:, g, P - 1:P], ident[:, :])
            last.then_inc(sig("idx", "edges_T"), 1)
            pe.wait_ge(sig("idx", "crow"), 1)
            for g in range(SG):
                product(ps[:, 6, g:g + 1], crow[0:1, g * P:(g + 1) * P], ones[0:1, 0:1], start=True, stop=True)
                last = product(ps[:, 6, 8 + g:9 + g], crow[0:1, g * P + 1:(g + 1) * P + 1], ones[0:1, 0:1], start=True, stop=True)
            last.then_inc(sig("idx", "ccol"), 1)
            for a, v in enumerate((loc_row[:, :, 0:P], srcf, combf)):
                if a:
                    pe.wait_ge(sig("idx", "copied"), a)
                for g in range(SG):
                    last = nc.tensor.transpose(psf[:, g * P:(g + 1) * P], v[:, g, :], ident[:, :])
                last.then_inc(sig("idx", "transposed"), 1)
            barrier(pe, "pe")

            def transpose_pair(source, bank):
                for a in range(2):
                    for k in range(2):
                        last = nc.tensor.transpose(ps[:, bank, (a * 2 + k) * P:(a * 2 + k + 1) * P], source[:, a, k * P:(k + 1) * P], ident[:, :])
                return last

            def n1_transpose(m, b):
                pe.wait_ge(sig("n1", "operand"), m + 1)
                transpose_pair(mm, 0).then_inc(sig("n1", "T"), 1)

            def n1_product(n, b):
                pe.wait_ge(sig("n1", "Tc"), n + 1)
                for a in range(2):
                    pe.wait_ge(sig("n1", "used"), n * 2 + (a + 1))
                    for c0, c1, bank in ((0, 512, 1 + 2 * a), (512, 768, 2 + 2 * a)):
                        for k in range(2):
                            last = product(ps[:, bank, 0:c1 - c0], mTs[b][:, a, k, :], wbig[:, k, c0:c1], start=(k == 0), stop=(k == 1))
                    last.then_inc(sig("n1", "qkv"), 1)

            n1_transpose(0, 0)
            with pe.Fori(0, HALF) as i:
                for b in range(2):
                    n = i * 2 + b
                    pe.wait_ge(sig("n1", "Tc"), n + 1)
                    n1_transpose(n + 1, 1 - b)
                    n1_product(n, b)
            n1_product(PAIRS - 1, 0)
            barrier(pe, "pe")

            with pe.Fori(0, TURNS) as i:
                for u in range(RING):
                    b = u % 2
                    _, tile_of = nc.values_load_multi_w_load_instructions(
                        trow[0:1, bass.ds(i * BODY + u * QUAD, QUAD)], engines=(pe.engine,), min_val=0, max_val=TILES - 1,
                        skip_runtime_bounds_check_because="clamped when made")
                    pe.wait_ge(sig("a", "onehot"), i * RING + (u + 1))
                    pe.wait_ge(sig("a", "scored"), i * RING + (u + 1))
                    for k in range(QUAD):
                        product(ps[:, 2 * b + k // 2, (k % 2) * D:(k % 2 + 1) * D], ohT[b][:, k, 0:P],
                                qr[:, bass.ds(tile_of[k], 1), :].rearrange("p a c -> p (a c)"), start=True, stop=True)
                        last = product(ps[:, 4 + b, k * HD:(k + 1) * HD], ohT[b][0:NTYPE, k, P:2 * P], rel[:, :], start=True, stop=True)
                    last.then_inc(sig("a", "expanded"), 1)
            barrier(pe, "pe")

            for g in range(SG):
                if g >= 2:
                    pe.wait_ge(sig("m", "copied"), g - 1)
                for h in range(HEADS):
                    last = nc.tensor.transpose(ps[:, g % 2, h * P:(h + 1) * P], sc[:, g * P:(g + 1) * P, h], ident[:, :])
                last.then_inc(sig("m", "transposed"), 1)
            for r in range(2):
                pe.wait_ge(sig("m", "last"), r + 1)
                for g in range(SG):
                    nc.tensor.transpose(psf[0:HEADS, 1024 + g * P:1024 + (g + 1) * P], lcol[:, g, :], ident[:, :])
                    last = nc.tensor.transpose(psf[0:HEADS, 2048 + g * P:2048 + (g + 1) * P], gmc[:, r, g, :], ident[:, :])
                last.then_inc(sig("m", "last_T"), 1)
                pe.wait_ge(sig("m", "carry"), r + 1)
                for g in range(SG):
                    last = nc.tensor.transpose(ps[:, 7, g * HEADS:(g + 1) * HEADS], carry[:, g * P + r:(g + 1) * P + r], ident[0:HEADS, 0:HEADS])
                last.then_inc(sig("m", "carry_T"), 1)
            pe.wait_ge(sig("m", "exp"), 1)
            for g in range(SG):
                if g >= 2:
                    pe.wait_ge(sig("m", "back"), g - 1)
                for h in range(HEADS):
                    last = nc.tensor.transpose(ps[:, g % 2, h * P:(h + 1) * P], sx[0][:, h, g, :], ident[:, :])
                last.then_inc(sig("m", "back_T"), 1)
            barrier(pe, "pe")

            def seg_loop(tag):
                if tag != "b":
                    pe.wait_ge(sig(tag, "ones"), 1)
                with pe.Fori(0, TURNS) as i:
                    for u in range(RING):
                        pe.wait_ge(sig(tag, "onehot"), i * RING + (u + 1))
                        if tag == "b":
                            pe.wait_ge(sig(tag, "weighted"), i * RING + (u + 1))
                        if tag != "b":
                            pe.wait_ge(sig(tag, f"gathered{u}"), i * 64 + 64)
                        for k in range(QUAD):
                            pe.wait_ge(sig(tag, "added"), i * BODY + (u * QUAD + k + 1))
                            product(ps[:, 4 * (u % 2) + k, 0:AW], oh[:, u % 2, k, :], gbuf[:, u * QUAD + k, :], start=True, stop=True
                                    ).then_inc(sig(tag, "sum"), 1)
                barrier(pe, "pe")

            def h_transpose(tag, m):
                pe.wait_ge(sig(tag, "h"), m + 1)
                transpose_pair(hh, 0).then_inc(sig(tag, "hT"), 1)

            def gated(tag, n, b, between=None):
                pe.wait_ge(sig(tag, "hTc"), n + 1)
                pe.wait_ge(sig(tag, "rootused"), n + 1)
                for a in range(2):
                    for k in range(2):
                        last = product(ps[:, 1, a * 8:a * 8 + NREL], hTs[b][:, a, k, :], wgate[:, k, :], start=(k == 0), stop=(k == 1))
                last.then_inc(sig(tag, "gate_in"), 1)
                for a in range(2):
                    for k in range(2):
                        last = product(ps[:, 2, a * D:(a + 1) * D], hTs[b][:, a, k, :], wroot[:, k, :], start=(k == 0), stop=(k == 1))
                last.then_inc(sig(tag, "root"), 1)
                for j in range(6):
                    a, c = j // 3, j % 3
                    if j % 2:
                        pe.wait_ge(sig(tag, "copiedA"), n * 3 + ((j + 3) // 2))
                    else:
                        pe.wait_ge(sig(tag, "copiedV"), n * 3 + (j // 2 + 1))
                    for k in range(2):
                        last = product(ps[:, 3 + c, :], hTs[b][:, a, k, :], wbig[:, k, c * 512:(c + 1) * 512], start=(k == 0), stop=(k == 1))
                    last.then_inc(sig(tag, "xw"), 1)
                    if j == 3 and between:
                        between()

            seg_loop("b")
            def n2_out(m, b):
                pe.wait_ge(sig("n2", "operand"), m + 1)
                transpose_pair(mm, 6).then_inc(sig("n2", "T"), 1)
                pe.wait_ge(sig("n2", "Tc"), m + 1)
                for a in range(2):
                    for k in range(2):
                        last = product(ps[:, 7, a * D:(a + 1) * D], mTs[0][:, a, k, :], wo[:, k, :], start=(k == 0), stop=(k == 1))
                last.then_inc(sig("n2", "o"), 1)

            n2_out(0, 0)
            h_transpose("n2", 0)
            with pe.Fori(0, HALF) as i:
                for b in range(2):
                    n = i * 2 + b
                    n2_out(n + 1, 1 - b)
                    gated("n2", n, b)
                    h_transpose("n2", n + 1)
            gated("n2", PAIRS - 1, 0)
            barrier(pe, "pe")
            seg_loop("l1")
            h_transpose("n3", 0)
            with pe.Fori(0, HALF) as i:
                for b in range(2):
                    n = i * 2 + b
                    gated("n3", n, b, lambda: h_transpose("n3", n + 1))
            gated("n3", PAIRS - 1, 0)
            barrier(pe, "pe")
            seg_loop("l2")

        @block.scalar
        def _(act):
            A = nc.scalar.activation
            act.sem_inc(sig("w", "bankfree"), 4)
            act.sem_inc(sig("a", "rowfree"), 2)
            for tag in ("n2", "n3"):
                act.sem_inc(sig(tag, "copiedA"), 2)
            for l in range(2):
                with act.Fori(0, WPIECES // 2) as i:
                    for b in range(2):
                        act.wait_ge(sig("w", f"stored{b}"), i * 16 + (l * 8 * WPIECES + 16))
                        for j in range(4):
                            act.wait_ge(sig("w", "product"), (i * 2 + b) * 4 + (l * WPIECES * 4 + j + 6))
                            A(wout[b][:, j * 512:(j + 1) * 512], ps[0:4 * NREL, j, :], ACT.Copy).then_inc(sig("w", "copied"), 1)
                            act.wait_ge(sig("w", "copied"), (i * 2 + b) * 4 + (l * WPIECES * 4 + j + 1))
                            act.sem_inc(sig("w", "bankfree"), 1)
            barrier(act, "act")

            def normalise(stage, n, what, out3, in3, func):
                act.wait_ge(sig(stage, f"{what}_var"), n + 1)
                A(sd[:, :], mv[:, :, 1], ACT.Sqrt, bias=epsc[:, :]).then_inc(sig(stage, f"{what}_sd"), 1)
                act.wait_ge(sig(stage, f"{what}_scale"), n + 1)
                for a in range(2):
                    last = A(out3[:, a, :], in3[:, a, :], func, bias=nm[:, a:a + 1], scale=rs[:, a:a + 1])
                return last

            def n1_pair(m, b):
                normalise("n1", m, "x", hh, xt[:, b, :, :], ACT.Relu).then_inc(sig("n1", "h"), 1)
                act.wait_ge(sig("n1", "T"), m + 1)
                if b is not None:
                    A(mTs[b][:, :, :, :].rearrange("p a k c -> p (a k c)"), ps[:, 0, :], ACT.Copy).then_inc(sig("n1", "Tc"), 1)

            with act.Fori(0, HALF) as i:
                for b in range(2):
                    n = i * 2 + b
                    n1_pair(n, b)
            n1_pair(PAIRS - 1, 0)
            barrier(act, "act")

            def stage_indices(tag, index, done, unit, i, u):
                if u >= 2:
                    act.wait_ge(done, i * (RING * unit) + (u - 1) * unit)
                nc.scalar.activation(stage[:, u % RING, :], index[:, bass.ds(i * BODY + u * QUAD, QUAD)], ACT.Copy).then_inc(sig(tag, "staged"), 1)

            for u in range(2):
                stage_indices("a", si, None, 1, 0, u)
            with act.Fori(0, TURNS) as i:
                for u in range(RING):
                    b = u % 2
                    stage_indices("a", si, sig("a", "scored"), 1, i, u + 2)
                    act.wait_ge(sig("a", f"row{b}"), i * 32 + (u // 2 + 1) * 16)
                    act.wait_ge(sig("a", "expanded"), i * RING + (u + 1))
                    A(ohT[b], bcr[b], ACT.Square, bias=npid[:, :]).then_inc(sig("a", "rowfree"), 1)
                    act.wait_ge(sig("a", "rowfree"), i * RING + (u + 3))
                    A(ohT[b], ohT[b], ACT.Relu, bias=1.0, scale=-1.0).then_inc(sig("a", "onehot"), 1)
            barrier(act, "act")

            for g in range(SG):
                act.wait_ge(sig("m", "transposed"), g + 1)
                A(sx[0][:, :, g, :], ps[:, g % 2, :].rearrange("p (h c) -> p h c", h=HEADS), ACT.Copy).then_inc(sig("m", "copied"), 1)
            act.wait_ge(sig("m", "shifted"), 1)
            A(accf[:, 0:SG * 512], accf[:, 0:SG * 512], ACT.Exp).then_inc(sig("m", "exp"), 1)
            for g in range(SG):
                act.wait_ge(sig("m", "back_T"), g + 1)
                A(sc[:, g * P:(g + 1) * P, :].rearrange("p s h -> p h s"), ps[:, g % 2, :].rearrange("p (h c) -> p h c", h=HEADS),
                  ACT.Copy).then_inc(sig("m", "back"), 1)
            barrier(act, "act")

            def seg_loop(tag, index):
                added, total = sig(tag, "added"), sig(tag, "sum")
                for u in range(2):
                    stage_indices(tag, index, None, QUAD, 0, u)
                with act.Fori(0, TURNS) as i:
                    for u in range(RING):
                        stage_indices(tag, index, added, QUAD, i, u + 2)
                        act.wait_ge(added, i * BODY + (u + 1) * QUAD)
                        for k in range(QUAD):
                            last = A(oh[:, u % 2, k, :], iotaj[:, :], ACT.Square, scale=-1.0, bias=dl[:, bass.ds(i * BODY + u * QUAD + k, 1)])
                        last.then_inc(sig(tag, "squared"), 1)
                        act.wait_ge(sig(tag, "squared"), i * RING + (u + 1))
                        A(oh[:, u % 2, :, :], oh[:, u % 2, :, :], ACT.Relu, bias=1.0, scale=-1.0).then_inc(sig(tag, "onehot"), 1)
                barrier(act, "act")

            seg_loop("b", si)

            def h_copy(tag, b):
                A(hTs[b][:, :, :, :].rearrange("p a k c -> p (a k c)"), ps[:, 0, :], ACT.Copy).then_inc(sig(tag, "hTc"), 1)

            def gate_of(tag, n):
                act.wait_ge(sig(tag, "gate_in"), n + 1)
                act.wait_ge(sig(tag, "copiedV"), n * 3 + 2)
                act.wait_ge(sig(tag, "copiedA"), n * 3 + 2)
                A(gate[:, :, :], ps[:, 1, 0:16].rearrange("p (a r) -> p a r", a=2)[:, :, 0:NREL], ACT.Sigmoid, bias=gb[:, :]).then_inc(sig(tag, "gate"), 1)
                act.wait_ge(sig(tag, "gate"), n + 1)
                act.wait_ge(sig(tag, "stored"), n * 32 + 32)

            def scaled(tag, n, j):
                a, c = j // 3, j % 3
                act.wait_ge(sig(tag, "xw"), n * 6 + (j + 1))
                for e in range(2):
                    r = 2 * c + e
                    last = A(gout[:, a, r, :], ps[:, 3 + c, e * D:(e + 1) * D], ACT.Copy, scale=gate[:, a, r:r + 1])
                last.then_inc(sig(tag, "copiedA"), 1)

            def n2_first(m, b):
                act.wait_ge(sig("n2", "T"), m + 1)
                A(mTs[0][:, :, :, :].rearrange("p a k c -> p (a k c)"), ps[:, 6, :], ACT.Copy).then_inc(sig("n2", "Tc"), 1)
                normalise("n2", m, "x", h0, xt[:, b, :, :], ACT.Relu).then_inc(sig("n2", "h0"), 1)

            def n2_middle(m, b):
                normalise("n2", m, "u", vt[:, b, :, :], uu, ACT.Identity).then_inc(sig("n2", "un"), 1)

            def n2_last(m, b):
                normalise("n2", m, "y", hh, uu, ACT.Relu).then_inc(sig("n2", "h"), 1)
                act.wait_ge(sig("n2", "hT"), m + 1)
                h_copy("n2", b)

            n2_first(0, 0)
            n2_middle(0, 0)
            n2_last(0, 0)
            with act.Fori(0, HALF) as i:
                for b in range(2):
                    n = i * 2 + b
                    n2_first(n + 1, 1 - b)
                    gate_of("n2", n)
                    scaled("n2", n, 0)
                    n2_middle(n + 1, 1 - b)
                    scaled("n2", n, 2)
                    scaled("n2", n, 4)
                    n2_last(n + 1, 1 - b)
            gate_of("n2", PAIRS - 1)
            for j in (0, 2, 4):
                scaled("n2", PAIRS - 1, j)
            barrier(act, "act")
            seg_loop("l1", ci)
            act.wait_ge(sig("n3", "hT"), 1)
            h_copy("n3", 0)
            with act.Fori(0, HALF) as i:
                for b in range(2):
                    n = i * 2 + b
                    gate_of("n3", n)
                    scaled("n3", n, 0)
                    scaled("n3", n, 2)
                    act.wait_ge(sig("n3", "hT"), n + 2)
                    h_copy("n3", 1 - b)
                    scaled("n3", n, 4)
            gate_of("n3", PAIRS - 1)
            for j in (0, 2, 4):
                scaled("n3", PAIRS - 1, j)
            barrier(act, "act")
            seg_loop("l2", ci)

        @block.vector
        def _(dve):
            V = nc.vector
            seq = Steps(dve, sem("dve_steps"))
            dve.sem_inc(sig("a", "scored"), 2)
            for tag in ("b", "l1", "l2"):
                dve.sem_inc(sig(tag, "added"), 2 * QUAD)
            dve.sem_inc(sig("n1", "used"), 2)
            for tag in ("n2", "n3"):
                dve.sem_inc(sig(tag, "rootused"), 1)
                dve.sem_inc(sig(tag, "copiedV"), 2)
            V.memset(att[:, :, :], 0.0).then_inc(sig("pre", "att0"), 1)
            V.memset(zpad, 0.0).then_inc(sig("pre", "pads"), 1)
            V.memset(dpad[:, 0:P], PAD_DST).then_inc(sig("pre", "pads"), 1)
            V.memset(dpad[:, P:2 * P], 0).then_inc(sig("pre", "pads"), 1)
            seq(V.memset(epsc[:, :], EPS))
            seq(V.memset(ones[:, :], 1.0))
            seq(V.memset(zrow, 0.0))
            dve.wait_ge(sig("pre", "lohi"), 32)
            seq.then(V.tensor_scalar(lohi_i, lohi_i, 7, None, ALU.arith_shift_right))
            seq.then(V.tensor_copy(lohi, lohi_i))
            lo, hi = lohi[:, 0:CHUNKS], lohi[:, CHUNKS:2 * CHUNKS]
            seq.then(V.scalar_tensor_tensor(ncount, hi, 1.0, lo, ALU.add, ALU.subtract))
            seq.then(V.tensor_tensor_scan(hi, ncount, zrow, 0.0, ALU.add, ALU.add))
            seq.then(V.tensor_tensor(pd[:, 0, :], hi, ncount, ALU.subtract))
            V.tensor_tensor(pd[:, 1, :], lo, pd[:, 0, :], ALU.subtract).then_inc(sig("idx", "pd"), 1)
            dve.wait_ge(sig("idx", "pd_everywhere"), 1)
            seq.then(V.tensor_copy(pdb[:, :, :].rearrange("p a (c n) -> p a c n", c=2), ps[:, 4:8, 0:H2].rearrange("p (a c) n -> p a c n", a=2)))
            dve.wait_ge(sig("pre", "constants"), 1)
            for g in range(SG):
                seq.then(V.tensor_scalar(junk, pdb[:, 0, :], scol[:, g:g + 1], None, ALU.is_le, ALU.add, accum_out=cnt[:, g:g + 1]))
            seq.then(V.tensor_scalar(cnt[:, :], cnt[:, :], -1.0, None, ALU.add))
            for g in range(SG):
                seq.then(V.scalar_tensor_tensor(junk, iotac, cnt[:, g:g + 1], pdb[:, 1, :], ALU.is_equal, ALU.mult, accum_out=dsel[:, g:g + 1]))
            V.tensor_copy(chunk_i[:, :], cnt[:, :]).then_inc(sig("idx", "chunks"), 1)
            seq.then(V.tensor_tensor(dsel[:, :], dsel[:, :], scol[:, :], ALU.add))
            seq.then(V.tensor_scalar(tilec[:, :], dsel[:, :], float(TILES - 1), None, ALU.min))
            seq.then(V.tensor_scalar(inr[:, :], dsel[:, :], float(P), None, ALU.mult))
            dve.wait_ge(sig("idx", "records"), 16 * SG)
            seq.then(V.tensor_copy(srcf, recs[:, :, 0:P]))
            seq.then(V.tensor_tensor(loc_row[:, :, 0:P], srcf, inr[:, :, None].to_broadcast([P, SG, P]), ALU.subtract))
            seq.then(V.tensor_scalar(key, loc_row[:, :, 0:P], 0.0, None, ALU.is_ge))
            seq.then(V.scalar_tensor_tensor(key, loc_row[:, :, 0:P], float(P), key, ALU.is_lt, ALU.mult))
            seq.then(V.scalar_tensor_tensor(key, srcf, 1.0, key, ALU.add, ALU.mult))
            seq.then(V.tensor_copy(combf, recs[:, :, 2 * P:3 * P]))
            seq.then(V.tensor_copy(srcf, recs[:, :, P:2 * P]))
            seq.then(V.scalar_tensor_tensor(combf, combf, float(ROWS), srcf, ALU.mult, ALU.add))
            V.tensor_copy(loc_row[:, :, P:2 * P], recs[:, :, 3 * P:4 * P]).then_inc(sig("idx", "rows"), 1)
            seq.then(V.tensor_tensor(rsx[:, :, 1:P], key[:, :, 1:P], key[:, :, 0:P - 1], ALU.not_equal))
            seq.then(V.tensor_scalar(rsx[:, :, 1:P], rsx[:, :, 1:P], -BIG, None, ALU.mult))
            dve.wait_ge(sig("idx", "edges_T"), 1)
            seq(V.tensor_copy(trow[:, :], psf[0:1, 0:SP_]))
            seq.then(V.tensor_copy(krow, psf[0:1, 1024:3072].rearrange("p (a c) -> p a c", a=2)[:, :, 0:SP_]))
            seq(V.memset(crow[:, 0:1], -BIG))
            seq(V.memset(crow[:, SP_:SP_ + 1], -BIG))
            seq.then(V.tensor_tensor(crow[:, 1:SP_], krow[:, 0, 1:SP_], krow[:, 1, 0:SP_ - 1], ALU.not_equal))
            V.tensor_scalar(crow[:, 1:SP_], crow[:, 1:SP_], -BIG, None, ALU.mult).then_inc(sig("idx", "crow"), 1)
            dve.wait_ge(sig("idx", "ccol"), 1)
            seq(V.tensor_copy(rsx[:, :, 0:1], ps[:, 6, 0:SG][:, :, None]))
            seq.then(V.tensor_copy(rsx[:, :, P:P + 1], ps[:, 6, 8:8 + SG][:, :, None]))
            for r in range(2):
                seq.then(V.tensor_reduce(inr[:, :], rsx[:, :, r:P + r], AX, ALU.min))
                seq.then(V.tensor_copy(gmc[:, r, :, :], inr[:, :, None].to_broadcast([P, SG, HEADS])))
            for a, t in enumerate((dl, si, ci)):
                dve.wait_ge(sig("idx", "transposed"), a + 1)
                V.tensor_copy(t[:, :], psf[:, 0:SP_]).then_inc(sig("idx", "copied"), 1)
            dve.wait_ge(sig("pre", "params"), 16 * 12)
            for t, f in ((wbig[:, :, 0:D], HD ** -0.5), (bqkv[:, 0:D], HD ** -0.5), (rel[:, :], 0.2), (vecs[:, 0, :], 0.1)):
                seq(V.tensor_scalar(t, t, f, None, ALU.mult))
            seq.settle()
            barrier(dve, "dve")

            def moments(stage, n, what, in3):
                for a in range(2):
                    seq(V.bn_stats(st6[:, a, :], in3[:, a, :]))
                seq.settle()
                dve.sem_inc(sig("dve", "go"), 1)
                seq(V.bn_aggr(mv[:, 0, :], st6[:, 0, :]))
                V.bn_aggr(mv[:, 1, :], st6[:, 1, :]).then_inc(sig(stage, f"{what}_var"), 1)
                dve.wait_ge(sig(stage, f"{what}_sd"), n + 1)
                seq.then(V.reciprocal(rs[:, :], sd[:, :]))
                V.scalar_tensor_tensor(nm[:, :], mv[:, :, 0], -1.0, rs[:, :], ALU.mult, ALU.mult).then_inc(sig(stage, f"{what}_scale"), 1)

            bc2 = lambda v: v[:, None, :].to_broadcast([P, 2, D])

            def n1_operand(i, m, b):
                dve.wait_ge(sig("n1", f"tile{b}"), i * 16 + 16)
                moments("n1", m, "x", xt[:, b, :, :])
                dve.wait_ge(sig("n1", "h"), m + 1)
                if not isinstance(m, int) or m:
                    dve.wait_ge(sig("n1", "T"), m)
                V.tensor_tensor(mm[:, :, :], hh[:, :, :], bc2(vecs[:, 0, :]), ALU.add).then_inc(sig("n1", "operand"), 1)

            def n1_finish(n):
                dve.wait_ge(sig("n1", "stored"), n * 32 + 32)
                for a in range(2):
                    dve.wait_ge(sig("n1", "qkv"), n * 2 + (a + 1))
                    seq(V.tensor_tensor(qr[:, bass.ds(n * 2 + a, 1), :].rearrange("p a c -> p (a c)"), ps[:, 1 + 2 * a, 0:D], bqkv[:, 0:D], ALU.add))
                    seq(V.tensor_tensor(kvo[:, a, 0:D], ps[:, 1 + 2 * a, D:2 * D], bqkv[:, D:2 * D], ALU.add))
                    V.tensor_tensor(kvo[:, a, D:2 * D], ps[:, 2 + 2 * a, 0:D], bqkv[:, 2 * D:3 * D], ALU.add).then_inc(sig("n1", "used"), 1)

            n1_operand(0, 0, 0)
            with dve.Fori(0, HALF) as i:
                seq.enter(i, 2 * 8)
                for b in range(2):
                    n = i * 2 + b
                    n1_operand(i + b, n + 1, 1 - b)
                    n1_finish(n)
            seq.leave(HALF)
            n1_finish(PAIRS - 1)
            seq.settle()
            dve.wait_ge(sig("n1", "used"), 2 + 2 * PAIRS)
            barrier(dve, "dve")

            seq.then(V.memset(sc[:, STEPS:SP_, :], 0.0))
            with dve.Fori(0, TURNS) as i:
                seq.enter(i, 2 * RING)
                for u in range(RING):
                    b = u % 2
                    kk = gbuf[:, u * QUAD:(u + 1) * QUAD, 0:D]
                    dve.wait_ge(sig("a", f"gathered{u}"), i * 64 + 64)
                    dve.wait_ge(sig("a", "expanded"), i * RING + (u + 3))
                    k4 = kk.rearrange("p k (h d) -> p k h d", h=HEADS)
                    seq.then(V.tensor_tensor(k4, k4, ps[:, 4 + b, 0:QUAD * HD].rearrange("p (k d) -> p k d", k=QUAD)[:, :, None, :]
                                             .to_broadcast([P, QUAD, HEADS, HD]), ALU.add))
                    seq.then(V.tensor_tensor(kk, kk, psf[:, b * 1024:(b + 1) * 1024].rearrange("p (k c) -> p k c", k=QUAD), ALU.mult))
                    V.tensor_reduce(sc[:, bass.ds(i * BODY + u * QUAD, QUAD), :], k4, AX, ALU.add).then_inc(sig("a", "scored"), 1)
            seq.leave(TURNS)
            dve.wait_ge(sig("a", "scored"), 2 + RING * TURNS)
            barrier(dve, "dve")

            def scans(r, carried):
                for g in range(SG):
                    for h in range(HEADS):
                        first = ccol[:, g, h:h + 1] if carried else -BIG
                        if r == 0:
                            seq(V.tensor_tensor_scan(sx[1][:, h, g, :], rsx[:, g, 0:P], sx[0][:, h, g, :], first, ALU.add, ALU.max))
                        else:
                            seq(V.tensor_tensor_scan(sx[2][:, h, g, ::-1], rsx[:, g, P:0:-1], sx[1][:, h, g, ::-1], first, ALU.add, ALU.max))
                seq.settle()

            dve.wait_ge(sig("m", "copied"), SG)
            for r in range(2):
                scans(r, False)
                end = P - 1 if r == 0 else 0
                V.tensor_copy(lcol[:, :, :], sx[1 + r][:, :, :, end].rearrange("p h g -> p g h")).then_inc(sig("m", "last"), 1)
                dve.wait_ge(sig("m", "last_T"), r + 1)
                seq(V.tensor_copy(ltrow, psf[0:HEADS, 1024:1024 + SP_]))
                seq(V.tensor_copy(grow, psf[0:HEADS, 2048:2048 + SP_]))
                seq.then(V.memset(carry[:, (0 if r == 0 else SP_):(1 if r == 0 else SP_ + 1)], -BIG))
                if r == 0:
                    V.tensor_tensor_scan(carry[:, 1:SP_ + 1], grow, ltrow, -BIG, ALU.add, ALU.max).then_inc(sig("m", "carry"), 1)
                else:
                    V.tensor_tensor_scan(carry[:, 0:SP_][:, ::-1], grow[:, ::-1], ltrow[:, ::-1], -BIG, ALU.add, ALU.max).then_inc(sig("m", "carry"), 1)
                dve.wait_ge(sig("m", "carry_T"), r + 1)
                seq.then(V.tensor_copy(ccol[:, :, :], ps[:, 7, 0:SG * HEADS].rearrange("p (g h) -> p g h", h=HEADS)))
                scans(r, True)
            V.tensor_tensor(accf[:, 0:SG * 512], accf[:, 0:SG * 512], accf[:, 2 * SG * 512:3 * SG * 512], ALU.subtract).then_inc(sig("m", "shifted"), 1)
            barrier(dve, "dve")

            def seg_loop(tag):
                if tag != "b":
                    V.memset(gbuf[:, :, D:AW], 1.0).then_inc(sig(tag, "ones"), 1)
                seq.then(V.memset(accf, 0.0))
                added, total = sig(tag, "added"), sig(tag, "sum")

                def weight(i, u):
                    at = bass.ds(i * BODY + u * QUAD, QUAD)
                    dve.wait_ge(sig(tag, f"gathered{u}"), i * 64 + 64)
                    v4 = gbuf[:, u * QUAD:(u + 1) * QUAD, 0:D].rearrange("p k (h d) -> p k h d", h=HEADS)
                    V.tensor_tensor(v4, v4, sc[:, at, :][:, :, :, None].to_broadcast([P, QUAD, HEADS, HD]), ALU.mult)
                    V.tensor_copy(gbuf[:, u * QUAD:(u + 1) * QUAD, D:AW], sc[:, at, :]).then_inc(sig(tag, "weighted"), 1)

                def add(i, u):
                    _, tile_of = nc.values_load_multi_w_load_instructions(
                        trow[0:1, bass.ds(i * BODY + u * QUAD, QUAD)], engines=(dve.engine,), min_val=0, max_val=TILES - 1,
                        skip_runtime_bounds_check_because="clamped when made")
                    for k in range(QUAD):
                        at = acc[:, bass.ds(tile_of[k], 1), :].rearrange("p a c -> p (a c)")
                        dve.wait_ge(total, i * BODY + (u * QUAD + k + 1))
                        dve.wait_ge(added, i * BODY + (2 * QUAD + u * QUAD + k))
                        V.tensor_tensor(at, ps[:, 4 * (u % 2) + k, 0:AW], at, ALU.add).then_inc(added, 1)

                def turn(i, last):
                    for u in range(RING):
                        if tag == "b" and not (last and u == RING - 1):
                            weight(i + (u + 1) // RING, (u + 1) % RING)
                        add(i, u)

                if tag == "b":
                    weight(0, 0)
                with dve.Fori(0, TURNS - 1) as i:
                    turn(i, False)
                turn(TURNS - 1, True)
                dve.wait_ge(added, 2 * QUAD + STEPS)
                barrier(dve, "dve")

            def gate_columns(l):
                dve.wait_ge(sig(f"g{l}", "loaded"), 8 * 16)
                for k in range(2):
                    w6 = wbig[:, k, :].rearrange("p (r o) -> p r o", r=NREL)
                    seq.then(V.tensor_tensor(gout[:, 0, :, :], w6, vecs[:, 5, :][:, None, :].to_broadcast([P, NREL, D]), ALU.mult))
                    seq.then(V.tensor_reduce(wgate[:, k, :], gout[:, 0, :, :], AX, ALU.add))

            def root_of(tag, n):
                dve.wait_ge(sig(tag, "root"), n + 1)
                dve.wait_ge(sig(tag, "gate"), n + 1)
                V.tensor_tensor(qr[:, bass.ds(n * 2, 2), :], ps[:, 2, :].rearrange("p (a c) -> p a c", a=2), bc2(vecs[:, 4, :]), ALU.add).then_inc(sig(tag, "rootused"), 1)
                dve.wait_ge(sig(tag, "stored"), n * 32 + 32)

            def scaled(tag, n, j):
                a, c = j // 3, j % 3
                dve.wait_ge(sig(tag, "xw"), n * 6 + (j + 1))
                V.tensor_tensor(gout[:, a, 2 * c:2 * c + 2, :], ps[:, 3 + c, :].rearrange("p (e o) -> p e o", e=2),
                                gate[:, a, 2 * c:2 * c + 2][:, :, None].to_broadcast([P, 2, D]), ALU.mult).then_inc(sig(tag, "copiedV"), 1)

            seg_loop("b")
            gate_columns(0)

            def n2_messages(i, n, b):
                x2, v2 = xt[:, b, :, :], vt[:, b, :, :]
                a2 = acc[:, bass.ds(n * 2, 2), 0:D].rearrange("p a (h d) -> p a h d", h=HEADS)
                w2 = acc[:, bass.ds(n * 2, 2), D:AW]
                wide = lambda t: t[:, :, :, None].to_broadcast([P, 2, HEADS, HD])
                dve.wait_ge(sig("n2", f"tile{b}"), i * 32 + 32)
                seq(V.tensor_scalar(zer[:, :, :], w2, 0.0, None, ALU.is_equal))
                seq.then(V.tensor_scalar(den[:, :, :], w2, 1e-30, None, ALU.max))
                seq.then(V.reciprocal(den[:, :, :], den[:, :, :]))
                m4 = mm[:, :, :].rearrange("p a (h d) -> p a h d", h=HEADS)
                v4 = v2.rearrange("p a (h d) -> p a h d", h=HEADS)
                seq(V.tensor_tensor(m4, a2, wide(den[:, :, :]), ALU.mult))
                seq.then(V.tensor_tensor(v4, v4, wide(zer[:, :, :]), ALU.mult))
                V.tensor_tensor(mm[:, :, :], mm[:, :, :], v2, ALU.add).then_inc(sig("n2", "operand"), 1)
                moments("n2", n, "x", x2)

            def n2_residual(n):
                dve.wait_ge(sig("n2", "o"), n + 1)
                dve.wait_ge(sig("n2", "x1stored"), n * 16 + 16)
                seq.then(V.tensor_tensor(uu[:, :, :], ps[:, 7, :].rearrange("p (a c) -> p a c", a=2), bc2(vecs[:, 1, :]), ALU.add))
                dve.wait_ge(sig("n2", "h0"), n + 1)
                seq.then(V.tensor_tensor(uu[:, :, :], uu[:, :, :], h0[:, :, :], ALU.add))
                moments("n2", n, "u", uu)

            def n2_norm(n, b):
                x2, v2 = xt[:, b, :, :], vt[:, b, :, :]
                dve.wait_ge(sig("n2", "un"), n + 1)
                seq.then(V.tensor_tensor(v2, v2, bc2(vecs[:, 2, :]), ALU.mult))
                seq.then(V.tensor_tensor(v2, v2, bc2(vecs[:, 3, :]), ALU.add))
                V.tensor_tensor(uu[:, :, :], x2, v2, ALU.add).then_inc(sig("n2", "x1"), 1)
                dve.wait_ge(sig("n2", "x1"), n + 1)
                moments("n2", n, "y", uu)

            n2_messages(0, 0, 0)
            n2_residual(0)
            n2_norm(0, 0)
            with dve.Fori(0, HALF) as i:
                seq.enter(i, 2 * 21)
                for b in range(2):
                    n = i * 2 + b
                    n2_messages(i + b, n + 1, 1 - b)
                    root_of("n2", n)
                    n2_residual(n + 1)
                    scaled("n2", n, 1)
                    n2_norm(n + 1, 1 - b)
                    scaled("n2", n, 3)
                    scaled("n2", n, 5)
            seq.leave(HALF)
            root_of("n2", PAIRS - 1)
            for j in (1, 3, 5):
                scaled("n2", PAIRS - 1, j)
            seq.settle()
            dve.wait_ge(sig("n2", "copiedV"), 2 + 3 * PAIRS)
            barrier(dve, "dve")
            seg_loop("l1")
            gate_columns(1)

            def mean_plus_root(n):
                seq.then(V.tensor_scalar(den[:, :, 0:1], acc[:, bass.ds(n * 2, 2), D:D + 1], 1.0, None, ALU.max))
                seq.then(V.reciprocal(den[:, :, 1:2], den[:, :, 0:1]))
                for a in range(2):
                    at = bass.ds(n * 2 + a, 1)
                    seq(V.scalar_tensor_tensor(hh[:, a, :], acc[:, at, 0:D].rearrange("p a c -> p (a c)"), den[:, a, 1:2],
                                               qr[:, at, :].rearrange("p a c -> p (a c)"), ALU.mult, ALU.add))
                seq.settle()

            def n3_h(m):
                if isinstance(m, int):
                    mean_plus_root(m)
                else:
                    dve.wait_ge(sig("n3", "hT"), m)
                    mean_plus_root(m)
                V.tensor_scalar(hh[:, :, :], hh[:, :, :], 0.0, None, ALU.max).then_inc(sig("n3", "h"), 1)

            n3_h(0)
            with dve.Fori(0, PAIRS - 1) as n:
                seq.enter(n, 4)
                n3_h(n + 1)
                root_of("n3", n)
                for j in (1, 3, 5):
                    scaled("n3", n, j)
            seq.leave(PAIRS - 1)
            root_of("n3", PAIRS - 1)
            for j in (1, 3, 5):
                scaled("n3", PAIRS - 1, j)
            dve.wait_ge(sig("n3", "copiedV"), 2 + 3 * PAIRS)
            barrier(dve, "dve")
            seg_loop("l2")

            def n4_pair(i, n, b):
                dve.wait_ge(sig("n4", f"tile{b}"), i * 16 + 16)
                dve.wait_ge(sig("n4", "stored"), n * 16 + 16)
                mean_plus_root(n)
                V.tensor_tensor(hh[:, :, :], hh[:, :, :], xt[:, b, :, :], ALU.add).then_inc(sig("n4", "ready"), 1)

            with dve.Fori(0, HALF) as i:
                seq.enter(i, 8)
                for b in range(2):
                    n4_pair(i, i * 2 + b, b)
            seq.leave(HALF)
            n4_pair(HALF, PAIRS - 1, 0)


_INS = ['x', 'src', 'dst', 'edge_type_6', 'edge_type_64'] + ['L0_gnn_' + n for n in (
    'query_emb', 'Wq', 'bq', 'Wk', 'bk', 'Wv', 'bv', 'rel_w', 'Wo', 'bo', 'gamma', 'beta')] + [
    'L1_gnn_' + n for n in ('basis1', 'att1', 'root1', 'bias1', 'gate_w1', 'gate_b1',
                            'basis2', 'att2', 'root2', 'bias2', 'gate_w2', 'gate_b2')]


def kernel(**inputs):
    import numpy as _np
    import concourse.bacc as _bacc
    from concourse import mybir as _mybir
    from concourse.bass_utils import run_bass_kernel_spmd as _run

    nc = _bacc.Bacc("TRN2", target_bir_lowering=False, num_devices=1)
    arrays, args = {}, []
    for name in _INS:
        a = _np.ascontiguousarray(inputs[name])
        arrays[f"in_{name}"] = a
        args.append(nc.dram_tensor(f"in_{name}", a.shape, _mybir.dt.from_np(a.dtype), kind="ExternalInput").ap())
    o = nc.dram_tensor("out", (N, D), _mybir.dt.float32, kind="ExternalOutput").ap()
    build(nc, *args, o)
    r = _run(nc, [arrays], core_ids=[0])
    return r.results[0]["out"]
```

```python
import numpy as np
import concourse.bass as bass
from concourse import mybir
from contextlib import ExitStack

F32 = mybir.dt.float32
I32 = mybir.dt.int32
ALU = mybir.AluOpType
ACT = mybir.ActivationFunctionType
AX = mybir.AxisListType.X

P = 128
N, D = 6250, 256
E = 100000
HEADS, HD = 4, 64
NTYPE, NREL, NBASE = 64, 6, 30
TILES = -(-N // P)
PAIRS = -(-TILES // 2)
NT = 2 * PAIRS
ROWS = NT * P
LOADROWS = ROWS + 4 * P
CHUNKS = -(-E // P)
FULL = E // P
TAIL = E - FULL * P
QUAD = 4
RING = 4
BODY = RING * QUAD
STEPS = -(-(CHUNKS + TILES - 1) // BODY) * BODY
TURNS = STEPS // BODY
SG = -(-STEPS // P)
SP_ = SG * P
AW = D + 4
BIG = 1e30
EPS = 1e-5
WP = 512
WTURNS = (64 * D) // WP // 2
PAD_DST = N


class Steps:

    def __init__(self, eng, sem):
        self.eng, self.sem, self.base, self.k, self.i, self.per = eng, sem, 0, 0, None, 0

    def enter(self, i, per):
        self.base += self.k
        self.i, self.per, self.k = i, per, 0

    def leave(self, turns):
        assert self.k == self.per, (self.k, self.per)
        self.base += turns * self.per
        self.i, self.k = None, 0

    def __call__(self, ins):
        ins.then_inc(self.sem, 1)
        self.k += 1

    def settle(self):
        if self.i is None:
            self.eng.wait_ge(self.sem, self.base + self.k)
        else:
            self.eng.wait_ge(self.sem, self.i * self.per + (self.base + self.k))

    def then(self, ins):
        self(ins)
        self.settle()


def build(nc, x, src, dst, et6, et64, qe, Wq, bq, Wk, bk, Wv, bv, rel_w, Wo, bo, gamma, beta,
          basis1, att1, root1, bias1, gw1, gb1, basis2, att2, root2, bias2, gw2, gb2, out):
    dram = lambda name, shape, dt=F32: nc.dram_tensor(name, shape, dt, kind="Internal").ap()
    x_d = dram("x_padded", (LOADROWS, D))
    x1_d = dram("x_after_attention", (LOADROWS, D))
    k_d = dram("k_table", (ROWS, D))
    v_d = dram("v_table", (LOADROWS, D))
    g_d = dram("gated_table", (NREL * ROWS, D))
    rec_d = dram("edge_records", (CHUNKS, 4 * P), I32)
    row_d = dram("step_rows", (SP_, 2 * P))
    w_d = [dram(f"w_layer{l}", (4 * NREL, 64 * D)) for l in range(2)]

    ctx = ExitStack()
    with ctx:
        sb = lambda name, shape, dt=F32: ctx.enter_context(nc.sbuf_tensor(name, shape, dt))
        sem = lambda name: ctx.enter_context(nc.semaphore(name))

        qr = sb("qr", [P, NT, D])
        acc = sb("acc", [P, NT, AW])
        sc = sb("sc", [P, SP_, HEADS])
        dl = sb("dl", [P, SP_])
        si = sb("si", [P, SP_], I32)
        ci = sb("ci", [P, SP_], I32)
        wbig = sb("wbig", [P, 2, NREL * D])
        wo = sb("wo", [P, 2, D])
        wroot = sb("wroot", [P, 2, D + NREL])
        bqkv = sb("bqkv", [P, 3 * D])
        vecs = sb("vecs", [P, 5, D])
        gb = sb("gb", [P, 1])
        rel = sb("rel", [NTYPE, HD])
        qcol = sb("qcol", [P, 2])
        ident = sb("ident", [P, P])
        iotaj = sb("iotaj", [P, P])
        npid = sb("npid", [P, 1])
        epsc = sb("epsc", [P, 1])
        ones = sb("ones", [1, P])
        att = sb("att", [4 * NBASE, 2, 4 * NREL])
        rsx = sb("rsx", [P, SG, P + 1])
        gmc = sb("gmc", [P, 2, SG, HEADS])
        trow = sb("trow", [1, SP_], I32)
        stage = sb("stage", [P, RING, QUAD], I32)
        shared = sb("shared", [P, BODY * AW])
        gbuf = shared[:, :].rearrange("p (s c) -> p s c", s=BODY)
        gout = shared[:, 0:2 * NREL * D].rearrange("p (a r c) -> p a r c", a=2, r=NREL)
        kvo = shared[:, 2 * NREL * D:2 * NREL * D + 4 * D].rearrange("p (a c) -> p a c", a=2)
        oh = sb("oh", [P, 2, QUAD, P])
        xt = sb("xt", [P, 2, 2, D])
        vt = sb("vt", [P, 2, 2, D])
        hh = sb("hh", [P, 2, D])
        mm = sb("mm", [P, 2, D])
        h0 = sb("h0", [P, 2, D])
        mTs = [sb(f"mT{b}", [P, 2, 2, P]) for b in range(2)]
        hTs = [sb(f"hT{b}", [P, 2, 2, P]) for b in range(2)]
        uu = sb("uu", [P, 2, D])
        st6 = sb("st6", [P, 2, 6])
        mv = sb("mv", [P, 2, 2])
        sd = sb("sd", [P, 2])
        rs = sb("rs", [P, 2])
        nm = sb("nm", [P, 2])
        den = sb("den", [P, 2, HEADS])
        zer = sb("zer", [P, 2, HEADS])
        inv = sb("inv", [P, NT])
        gate = sb("gate", [P, 2, NREL])
        ps = ctx.enter_context(nc.psum_tensor("ps", [P, 8, 512], F32))

        accf = acc[:, :, :].rearrange("p t c -> p (t c)")
        qrf = qr[:, :, :].rearrange("p t c -> p (t c)")
        scf = sc[:, :, :].rearrange("p s h -> p (s h)")
        psf = ps[:, :, :].rearrange("p b c -> p (b c)")

        o = [0]

        def cut(n):
            o[0] += n
            return slice(o[0] - n, o[0])
        recs = accf[:, cut(SG * 512)].bitcast(I32).rearrange("p (g c) -> p g c", g=SG)
        pdb = accf[:, cut(2 * CHUNKS)].rearrange("p (a c) -> p a c", a=2)
        iotac = accf[:, cut(CHUNKS)]
        junk = accf[:, cut(CHUNKS)]
        loc_row = accf[:, cut(SG * 256)].rearrange("p (g c) -> p g c", g=SG)
        key = accf[:, cut(SG * P)].rearrange("p (g c) -> p g c", g=SG)
        srcf = accf[:, cut(SG * P)].rearrange("p (g c) -> p g c", g=SG)
        combf = accf[:, cut(SG * P)].rearrange("p (g c) -> p g c", g=SG)
        assert o[0] <= NT * AW
        bas = [accf[0:4 * NBASE, (12 + b) * WP:(13 + b) * WP] for b in range(2)]
        wout = [accf[0:4 * NREL, (14 + b) * WP:(15 + b) * WP] for b in range(2)]
        o[0] = 0
        pd = qrf[0:1, cut(2 * CHUNKS)].rearrange("p (a c) -> p a c", a=2)
        krow = qrf[0:1, cut(2 * SP_)].rearrange("p (a c) -> p a c", a=2)
        crow = qrf[0:1, cut(SP_ + 1)]
        assert o[0] <= NT * D
        lohi_i = shared[0:1, 0:2 * CHUNKS].bitcast(I32)
        o[0] = 0
        lohi = scf[0:1, cut(2 * CHUNKS)]
        ncount = scf[0:1, cut(CHUNKS)]
        zrow = scf[0:1, cut(CHUNKS)]
        scol, cnt, dsel, tilec, inr = (sb(n, [P, SG]) for n in ("scol", "cnt", "dsel", "tilec", "inr"))
        chunk_i = sb("chunk_i", [P, SG], I32)
        zpad = kvo[:, 0, :]
        dpad = sb("dpad", [1, 2 * P], I32)
        sx = [accf[:, a * SG * 512:(a + 1) * SG * 512].rearrange("p (h g c) -> p h g c", h=HEADS, g=SG)
              for a in range(3)]
        ltrow, grow, carry = (flat[0:HEADS, 0:n] for flat, n in (
            (oh[:, :, :, :].rearrange("p b k c -> p (b k c)"), SP_), (xt[:, :, :, :].rearrange("p b a c -> p (b a c)"), SP_),
            (vt[:, :, :, :].rearrange("p b a c -> p (b a c)"), SP_ + 1)))
        lcol = sb("lcol", [P, SG, HEADS])
        ccol = sb("ccol", [P, SG, HEADS])
        bcr = [accf[:, b * 1024:(b + 1) * 1024].rearrange("p (s c) -> p s c", s=QUAD) for b in range(2)]
        ohT = [accf[:, (2 + b) * 1024:(3 + b) * 1024].rearrange("p (s c) -> p s c", s=QUAD) for b in range(RING)]

        made = {}

        def sig(stage, what):
            if (stage, what) not in made:
                made[stage, what] = ctx.enter_context(nc.semaphore(f"{stage}_{what}"))
            return made[stage, what]

        stage_ended = sem("stage_ended")
        ended = {}

        def end_stage(eng, name):
            ended[name] = ended.get(name, 0) + 1
            eng.drain().then_inc(stage_ended, 1)

        def barrier(eng, name):
            end_stage(eng, name)
            eng.wait_ge(stage_ended, 5 * ended[name])

        block = ctx.enter_context(nc.Block())
        vrow = lambda v: v.rearrange("(a n) -> a n", a=1)
        kxn = lambda w: w.rearrange("(k p) n -> p k n", p=P)
        pairview = lambda t, r0: t[bass.ds(r0, 2 * P), :].rearrange("(a p) c -> p a c", p=P)
        PR = 2 * P
        HALF = PAIRS // 2
        assert PAIRS % 2 == 1
        H2 = CHUNKS // 2

        @block.sync
        def _(sp):
            sp.sem_inc(sig("n1", "stored0"), 32)
            sp.sem_inc(sig("n1", "stored1"), 32)
            sp.sem_inc(sig("n2", "x1stored"), 16)
            sp.sem_inc(sig("n2", "stored0"), 16)
            sp.sem_inc(sig("n2", "stored1"), 16)
            sp.sem_inc(sig("n3", "stored0"), 16)
            sp.sem_inc(sig("n3", "stored1"), 16)
            sp.sem_inc(sig("l2", "residual"), 1)
            copied, recorded = sig("pre", "copied"), sig("pre", "recorded")
            for j, a in enumerate((dst, src, et6, et64)):
                sp.dma_start(rec_d[0:FULL, j * P:(j + 1) * P], a[0:FULL * P].rearrange("(c e) -> c e", e=P)).then_inc(recorded, 16)
                sp.dma_start(rec_d[FULL:FULL + 1, j * P:j * P + TAIL], vrow(a[FULL * P:E])).then_inc(recorded, 16)
            sp.wait_ge(sig("pre", "pads"), 3)
            for j in range(4):
                sp.dma_start(rec_d[FULL:FULL + 1, j * P + TAIL:(j + 1) * P],
                             dpad[0:1, (0 if j == 0 else P):(0 if j == 0 else P) + P - TAIL]).then_inc(recorded, 16)
            sp.wait_ge(recorded, 12 * 16)
            with nc.allow_non_contiguous_dma(reason="first and last destination of each chunk; transposed coefficients"):
                sp.dma_start(lohi_i[0:1, 0:CHUNKS], rec_d[:, 0:1].rearrange("c a -> a c")).then_inc(sig("pre", "lohi"), 16)
                sp.dma_start(lohi_i[0:1, CHUNKS:2 * CHUNKS], rec_d[:, P - 1:P].rearrange("c a -> a c")).then_inc(sig("pre", "lohi"), 16)
                sp.wait_ge(sig("pre", "att0"), 1)
                for l, a in enumerate((att1, att2)):
                    for q in range(4):
                        sp.dma_start(att[q * NBASE:(q + 1) * NBASE, l, q * NREL:(q + 1) * NREL],
                                     a.rearrange("r b -> b r")).then_inc(sig("pre", "att"), 16)
            sp.dma_start(x_d[0:N, :], x[:, :]).then_inc(copied, 16)
            n_copied = 16
            for t, r0 in ((x_d, N), (x1_d, ROWS), (v_d, ROWS)):
                for r in range(r0, LOADROWS, P):
                    m = min(P, LOADROWS - r)
                    sp.dma_start(t[r:r + m, :], zpad[0:m, 0:D]).then_inc(copied, 16)
                    n_copied += 16
            with nc.allow_non_contiguous_dma(reason="a vector over partitions"):
                sp.dma_start(qcol[:, :], qe.rearrange("(k p) -> p k", p=P)).then_inc(sig("pre", "params"), 16)
            for dstt, s in ((wbig[:, :, 0:D], kxn(Wq)), (wbig[:, :, D:2 * D], kxn(Wk)), (wbig[:, :, 2 * D:3 * D], kxn(Wv)),
                            (wo[:, :, :], kxn(Wo)), (rel[:, :], rel_w[:, :]),
                            (bqkv[:, 0:D], vrow(bq).to_broadcast([P, D])), (bqkv[:, D:2 * D], vrow(bk).to_broadcast([P, D])),
                            (bqkv[:, 2 * D:3 * D], vrow(bv).to_broadcast([P, D])),
                            (vecs[:, 0, :], vrow(bo).to_broadcast([P, D])), (vecs[:, 1, :], vrow(gamma).to_broadcast([P, D])),
                            (vecs[:, 2, :], vrow(beta).to_broadcast([P, D]))):
                sp.dma_start(dstt, s).then_inc(sig("pre", "params"), 16)
            sp.wait_ge(sig("idx", "rows"), 1)
            sp.dma_start(row_d.rearrange("(g p) c -> p g c", p=P), loc_row).then_inc(sig("idx", "rows_stored"), 16)
            sp.wait_ge(sig("idx", "rows_stored"), 16)
            sp.wait_ge(copied, n_copied)
            for b in range(2):
                sp.dma_start(xt[:, b, :, :], pairview(x_d, PR * b)).then_inc(sig("n1", f"tile{b}"), 16)
            barrier(sp, "sp")

            def store_kv(n, between=None):
                for a in range(2):
                    if a and between:
                        between()
                    sp.wait_ge(sig("n1", "used"), n * 2 + (a + 3))
                    sp.sem_inc(sig("sp", "go"), 1)
                    for tb, off in ((k_d, 0), (v_d, D)):
                        sp.dma_start(tb[bass.ds(n * PR + a * P, P), :], kvo[:, a, off:off + D]).then_inc(sig("n1", f"stored{a}"), 16)

            def load_x(n, b):
                sp.wait_ge(sig("n1", "h"), n - 1)
                sp.sem_inc(sig("sp", "go"), 1)
                sp.dma_start(xt[:, b, :, :], pairview(x_d, n * PR)).then_inc(sig("n1", f"tile{b}"), 16)

            load_x(2, 0)
            with sp.Fori(0, HALF - 1) as i:
                for b in range(2):
                    n = i * 2 + b
                    store_kv(n, lambda: load_x(n + 3, 1 - b))
            for n in range(PAIRS - 3, PAIRS):
                store_kv(n)
            for a in range(2):
                sp.wait_ge(sig("n1", f"stored{a}"), 32 + PAIRS * 32)
            for b in range(2):
                sp.wait_ge(sig("n1", f"tile{b}"), 16 * (HALF + 1 - b))
            barrier(sp, "sp")

            def layer_params(l, root, bias, gw, gbv):
                loaded = sig(f"g{l}", "loaded")
                wl = w_d[l].rearrange("(q r) (i o) -> q r i o", q=4, o=D)
                for q in range(4):
                    sp.dma_start(wbig[(q % 2) * 64:(q % 2) * 64 + 64, q // 2, :].rearrange("i (r o) -> i r o", r=NREL),
                                 wl[q].rearrange("r i o -> i r o")).then_inc(loaded, 16)
                sp.dma_start(wroot[:, :, 0:D], kxn(root)).then_inc(loaded, 16)
                sp.dma_start(vecs[:, 3, :], vrow(bias).to_broadcast([P, D])).then_inc(loaded, 16)
                sp.dma_start(vecs[:, 4, :], gw.rearrange("k a -> a k").to_broadcast([P, D])).then_inc(loaded, 16)
                sp.dma_start(gb[:, :], vrow(gbv).to_broadcast([P, 1])).then_inc(loaded, 16)
                sp.wait_ge(loaded, 8 * 16)

            bases = [bs.rearrange("b (q i) o -> q b (i o)", q=4) for bs in (basis1, basis2)]

            def load_pieces(l, turn):
                for b in range(2):
                    sp.wait_ge(sig("w", "product"), turn * 2 + (l * 2 * WTURNS + b + 1))
                    for q in range(4):
                        sp.dma_start(bas[b][q * NBASE:(q + 1) * NBASE, :],
                                     bases[l][q][:, bass.ds((turn * 2 + b) * WP, WP)]).then_inc(sig("w", f"basis{b}"), 16)

            load_pieces(0, 0)
            def rows(i):
                for u in range(RING):
                    sp.wait_ge(sig("a", "rowfree"), i * RING + (u + 1))
                    sp.dma_start(bcr[u % 2], row_d[bass.ds(i * BODY + u * QUAD, QUAD), :].rearrange("(a s) c -> a s c", a=1)
                                 .to_broadcast([P, QUAD, 2 * P])).then_inc(sig("a", f"row{u % 2}"), 16)

            for l in range(2):
                with sp.Fori(l * WTURNS, (l + 1) * WTURNS - 1) as i:
                    rows(i)
                    load_pieces(l, i - (l * WTURNS - 1))
                rows((l + 1) * WTURNS - 1)
                if l == 0:
                    load_pieces(1, 0)
            with sp.Fori(2 * WTURNS, TURNS) as i:
                rows(i)
            barrier(sp, "sp")
            barrier(sp, "sp")
            layer_params(0, root1, bias1, gw1, gb1)
            barrier(sp, "sp")

            def store_gated(tag, n):
                for a in range(2):
                    sp.wait_ge(sig(tag, "copiedA"), n * 3 + (4, 5)[a])
                    sp.sem_inc(sig("sp", "go"), 1)
                    sp.wait_ge(sig(tag, "copiedV"), n * 3 + (3, 5)[a])
                    sp.sem_inc(sig("sp", "go"), 1)
                    sp.dma_start(g_d.rearrange("(r n) c -> n r c", r=NREL)[bass.ds(n * PR + a * P, P), :, :],
                                 gout[:, a, :, :]).then_inc(sig(tag, f"stored{a}"), 16)

            def store_x1(n):
                sp.wait_ge(sig("n2", "x1"), n + 1)
                sp.sem_inc(sig("sp", "go"), 1)
                sp.dma_start(pairview(x1_d, n * PR), uu[:, :, :]).then_inc(sig("n2", "x1stored"), 16)

            def load_xv(b, r0):
                sp.dma_start(xt[:, b, :, :], pairview(x_d, r0)).then_inc(sig("n2", f"tile{b}"), 16)
                sp.dma_start(vt[:, b, :, :], pairview(v_d, r0)).then_inc(sig("n2", f"tile{b}"), 16)

            def n2_moves(n, b, more=True):
                store_x1(n + 1)
                if more:
                    load_xv(1 - b, n * PR + 3 * PR)
                store_gated("n2", n)

            for b in range(2):
                load_xv(b, PR * b)
            store_x1(0)
            load_xv(0, 2 * PR)
            with sp.Fori(0, HALF - 1) as i:
                for b in range(2):
                    n2_moves(i * 2 + b, b)
            n2_moves(PAIRS - 3, 0, more=False)
            n2_moves(PAIRS - 2, 1, more=False)
            store_gated("n2", PAIRS - 1)
            sp.wait_ge(sig("n2", "x1stored"), 16 + 16 * PAIRS)
            for a in range(2):
                sp.wait_ge(sig("n2", f"stored{a}"), 16 + 16 * PAIRS)
            for b in range(2):
                sp.wait_ge(sig("n2", f"tile{b}"), 32 * (HALF + 1 - b))
            barrier(sp, "sp")
            layer_params(1, root2, bias2, gw2, gb2)
            barrier(sp, "sp")
            with sp.Fori(0, PAIRS) as i:
                store_gated("n3", i)
            for a in range(2):
                sp.wait_ge(sig("n3", f"stored{a}"), 16 + 16 * PAIRS)
            barrier(sp, "sp")
            with sp.Fori(0, PAIRS) as i:
                sp.wait_ge(sig("l2", "residual"), i + 1)
                sp.dma_start(xt[:, 0, :, :], pairview(x1_d, i * PR)).then_inc(sig("l2", "x1"), 16)
            barrier(sp, "sp")
            with sp.Fori(0, PAIRS - 1) as n:
                sp.wait_ge(sig("n4", "ready"), n + 1)
                sp.dma_start(pairview(out, n * PR), qr[:, bass.ds(n * 2, 2), :]).then_inc(sig("n4", "stored"), 16)
            sp.wait_ge(sig("n4", "ready"), PAIRS)
            last = N - (PAIRS - 1) * PR
            sp.dma_start(out[N - last:N, :], qr[0:last, (PAIRS - 1) * 2, :]).then_inc(sig("n4", "stored"), 16)
            sp.wait_ge(sig("n4", "stored"), 16 * PAIRS)

        @block.gpsimd
        def _(pool):
            seq = Steps(pool, sem("pool_steps"))
            seq(nc.gpsimd.memset(ident[:, :], 0.0))
            for t, pat, mult in ((iotaj[:, :], [[1, P]], 0), (npid[:, :], [[1, 1]], -1), (scol[:, :], [[P, SG]], 1), (iotac, [[1, CHUNKS]], 0)):
                seq(nc.gpsimd.iota(t, pat, base=0, channel_multiplier=mult, allow_small_or_imprecise_dtypes=True))
            seq.settle()
            pool.affine_select(out=ident[:, :], in_=ident[:, :], compare_op=ALU.not_equal, fill=1.0, base=0,
                               pattern=[[-1, P]], channel_multiplier=1).then_inc(sig("pre", "constants"), 1)
            pool.wait_ge(sig("idx", "chunks"), 1)
            for g in range(SG):
                pool.indirect_dma_start(out=recs[:, g, :], out_offset=None, in_=rec_d[:, :],
                                        in_offset=bass.IndirectOffsetOnAxis(ap=chunk_i[:, g:g + 1], axis=0)).then_inc(sig("idx", "records"), 16)
            pool.wait_ge(sig("idx", "records"), 16 * SG)
            barrier(pool, "pool")
            barrier(pool, "pool")

            def gather_loop(tag, table):
                with pool.Fori(0, TURNS) as i:
                    for u in range(RING):
                        pool.wait_ge(sig(tag, "staged"), i * RING + (u + 1))
                        pool.sem_inc(sig("pool", "go"), 1)
                        for k in range(QUAD):
                            pool.indirect_dma_start(out=gbuf[:, u * QUAD + k, 0:D], out_offset=None, in_=table[:, :],
                                                    in_offset=bass.IndirectOffsetOnAxis(ap=stage[:, u, k:k + 1], axis=0)
                                                    ).then_inc(sig(tag, f"gathered{u}"), 16)
                barrier(pool, "pool")

            gather_loop("a", k_d)
            end_stage(pool, "pool")
            gather_loop("b", v_d)
            barrier(pool, "pool")
            gather_loop("l1", g_d)
            barrier(pool, "pool")
            gather_loop("l2", g_d)

        @block.tensor
        def _(pe):
            product = nc.tensor.matmul
            pe.sem_inc(sig("w", "product"), 2)
            pe.sem_inc(sig("a", "expanded"), RING)
            pe.wait_ge(sig("idx", "pd"), 1)
            for a in range(2):
                for c in range(2):
                    last = product(ps[:, 4 + 2 * a + c, 0:H2], ones[:, :], pd[:, a, c * H2:(c + 1) * H2], start=True, stop=True)
            last.then_inc(sig("idx", "pd_everywhere"), 1)
            pe.wait_ge(sig("pre", "constants"), 1)
            pe.wait_ge(sig("idx", "rows"), 1)
            for g in range(SG):
                nc.tensor.transpose(psf[0:1, g * P:(g + 1) * P], tilec[:, g:g + 1], ident[:, :])
                nc.tensor.transpose(psf[0:1, 1024 + g * P:1024 + (g + 1) * P], key[:, g, 0:1], ident[:, :])
                last = nc.tensor.transpose(psf[0:1, 2048 + g * P:2048 + (g + 1) * P], key[:, g, P - 1:P], ident[:, :])
            last.then_inc(sig("idx", "edges_T"), 1)
            pe.wait_ge(sig("idx", "crow"), 1)
            for g in range(SG):
                product(ps[:, 6, g:g + 1], crow[0:1, g * P:(g + 1) * P], ones[0:1, 0:1], start=True, stop=True)
                last = product(ps[:, 6, 8 + g:9 + g], crow[0:1, g * P + 1:(g + 1) * P + 1], ones[0:1, 0:1], start=True, stop=True)
            last.then_inc(sig("idx", "ccol"), 1)
            for a, v in enumerate((loc_row[:, :, 0:P], srcf, combf)):
                for g in range(SG):
                    last = nc.tensor.transpose(psf[:, a * 1024 + g * P:a * 1024 + (g + 1) * P], v[:, g, :], ident[:, :])
                last.then_inc(sig("idx", "transposed"), 1)
            pe.wait_ge(sig("pre", "qcols"), 1)
            for c0, c1 in ((0, 512), (512, 3 * D)):
                for k in range(2):
                    last = product(psf[:, 1024 + c0:1024 + c1], mTs[0][:, k, 0, :], wbig[:, k, c0:c1], start=(k == 0), stop=(k == 1))
            last.then_inc(sig("pre", "qproduct"), 1)
            barrier(pe, "pe")

            def transpose_pair(source, bank):
                for a in range(2):
                    for k in range(2):
                        last = nc.tensor.transpose(ps[:, bank, (a * 2 + k) * P:(a * 2 + k + 1) * P], source[:, a, k * P:(k + 1) * P], ident[:, :])
                return last

            def n1_transpose(m, b):
                pe.wait_ge(sig("n1", "h"), m + 1)
                transpose_pair(hh, 0).then_inc(sig("n1", "T"), 1)

            def n1_product(n, b, between=None):
                pe.wait_ge(sig("n1", "Tc"), n + 1)
                for a in range(2):
                    if a and between:
                        between()
                    pe.wait_ge(sig("n1", "used"), n * 2 + (a + 1))
                    for c0, c1, bank in ((0, 512, 1 + 2 * a), (512, 768, 2 + 2 * a)):
                        for k in range(2):
                            last = product(ps[:, bank, 0:c1 - c0], mTs[b][:, a, k, :], wbig[:, k, c0:c1], start=(k == 0), stop=(k == 1))
                    last.then_inc(sig("n1", "qkv"), 1)

            n1_transpose(0, 0)
            with pe.Fori(0, HALF) as i:
                for b in range(2):
                    n = i * 2 + b
                    n1_product(n, b, lambda: n1_transpose(n + 1, 1 - b))
            n1_product(PAIRS - 1, 0)
            barrier(pe, "pe")

            def a_turn(i, l):
                for u in range(RING):
                    b = u % 2
                    _, tile_of = nc.values_load_multi_w_load_instructions(
                        trow[0:1, bass.ds(i * BODY + u * QUAD, QUAD)], engines=(pe.engine,), min_val=0, max_val=TILES - 1,
                        skip_runtime_bounds_check_because="clamped when made")
                    pe.wait_ge(sig("a", "onehot"), i * RING + (u + 1))
                    pe.wait_ge(sig("a", "multiplied"), i * RING + (u + 1))
                    for k in range(QUAD):
                        product(ps[:, 2 * b + k // 2, (k % 2) * D:(k % 2 + 1) * D], ohT[u][:, k, 0:P],
                                qr[:, bass.ds(tile_of[k], 1), :].rearrange("p a c -> p (a c)"), start=True, stop=True)
                        last = product(ps[:, 4 + b, k * HD:(k + 1) * HD], ohT[u][0:NTYPE, k, P:2 * P], rel[:, :], start=True, stop=True)
                    last.then_inc(sig("a", "expanded"), 1)
                    if l is not None and u < 2:
                        pe.wait_ge(sig("w", f"basis{u}"), i * 64 + 64)
                        pe.wait_ge(sig("w", "copied"), i * 2 + (u + 1))
                        product(ps[0:4 * NREL, 6 + u, :], att[:, l, :], bas[u], start=True, stop=True).then_inc(sig("w", "product"), 1)

            pe.wait_ge(sig("pre", "att"), 16 * 8)
            for l in range(2):
                with pe.Fori(l * WTURNS, (l + 1) * WTURNS) as i:
                    a_turn(i, l)
            with pe.Fori(2 * WTURNS, TURNS) as i:
                a_turn(i, None)
            barrier(pe, "pe")

            for g in range(SG):
                if g >= 2:
                    pe.wait_ge(sig("m", "copied"), g - 1)
                for h in range(HEADS):
                    last = nc.tensor.transpose(ps[:, g % 2, h * P:(h + 1) * P], sc[:, g * P:(g + 1) * P, h], ident[:, :])
                last.then_inc(sig("m", "transposed"), 1)
            for r in range(2):
                pe.wait_ge(sig("m", "last"), r + 1)
                for g in range(SG):
                    nc.tensor.transpose(psf[0:HEADS, 1024 + g * P:1024 + (g + 1) * P], lcol[:, g, :], ident[:, :])
                    last = nc.tensor.transpose(psf[0:HEADS, 2048 + g * P:2048 + (g + 1) * P], gmc[:, r, g, :], ident[:, :])
                last.then_inc(sig("m", "last_T"), 1)
                pe.wait_ge(sig("m", "carry"), r + 1)
                for g in range(SG):
                    last = nc.tensor.transpose(ps[:, 7, g * HEADS:(g + 1) * HEADS], carry[:, g * P + r:(g + 1) * P + r], ident[0:HEADS, 0:HEADS])
                last.then_inc(sig("m", "carry_T"), 1)
            pe.wait_ge(sig("m", "exp"), 1)
            for g in range(SG):
                if g >= 2:
                    pe.wait_ge(sig("m", "back"), g - 1)
                for h in range(HEADS):
                    last = nc.tensor.transpose(ps[:, g % 2, h * P:(h + 1) * P], sx[0][:, h, g, :], ident[:, :])
                last.then_inc(sig("m", "back_T"), 1)
            barrier(pe, "pe")

            def seg_loop(tag):
                if tag != "b":
                    pe.wait_ge(sig(tag, "ones"), 1)
                with pe.Fori(0, TURNS) as i:
                    for u in range(RING):
                        pe.wait_ge(sig(tag, "onehot"), i * RING + (u + 1))
                        if tag == "b":
                            pe.wait_ge(sig(tag, "weighted"), i * RING + (u + 1))
                        if tag != "b":
                            pe.wait_ge(sig(tag, f"gathered{u}"), i * 64 + 64)
                        for k in range(QUAD):
                            pe.wait_ge(sig(tag, "added"), i * BODY + (u * QUAD + k + 1))
                            product(ps[:, 4 * (u % 2) + k, 0:AW], oh[:, u % 2, k, :], gbuf[:, u * QUAD + k, :], start=True, stop=True
                                    ).then_inc(sig(tag, "sum"), 1)
                barrier(pe, "pe")

            def h_transpose(tag, m):
                pe.wait_ge(sig(tag, "h"), m + 1)
                transpose_pair(hh, 0).then_inc(sig(tag, "hT"), 1)

            def gated(tag, n, b, between=None):
                pe.wait_ge(sig(tag, "hTc"), n + 1)
                pe.wait_ge(sig(tag, "rootused"), n + 1)
                for a in range(2):
                    for k in range(2):
                        last = product(ps[:, 1 + a, 0:D + NREL], hTs[b][:, a, k, :], wroot[:, k, :], start=(k == 0), stop=(k == 1))
                last.then_inc(sig(tag, "root"), 1)
                for j in range(6):
                    a, c = j // 3, j % 3
                    if j % 2:
                        pe.wait_ge(sig(tag, "copiedA"), n * 3 + ((j + 3) // 2))
                    else:
                        pe.wait_ge(sig(tag, "copiedV"), n * 3 + (j // 2 + 1))
                    for k in range(2):
                        last = product(ps[:, 3 + c, :], hTs[b][:, a, k, :], wbig[:, k, c * 512:(c + 1) * 512], start=(k == 0), stop=(k == 1))
                    last.then_inc(sig(tag, "xw"), 1)
                    if j == 3 and between:
                        between()

            seg_loop("b")
            def n2_transpose(m):
                pe.wait_ge(sig("n2", "operand"), m + 1)
                transpose_pair(mm, 6).then_inc(sig("n2", "T"), 1)

            def n2_out(m):
                pe.wait_ge(sig("n2", "Tc"), m + 1)
                for a in range(2):
                    for k in range(2):
                        last = product(ps[:, 7, a * D:(a + 1) * D], mTs[0][:, a, k, :], wo[:, k, :], start=(k == 0), stop=(k == 1))
                last.then_inc(sig("n2", "o"), 1)

            def n2_turn(n, b, more=True):
                n2_out(n + 1)
                gated("n2", n, b, (lambda: n2_transpose(n + 2)) if more else None)
                h_transpose("n2", n + 1)

            n2_transpose(0)
            n2_out(0)
            n2_transpose(1)
            h_transpose("n2", 0)
            with pe.Fori(0, HALF - 1) as i:
                for b in range(2):
                    n2_turn(i * 2 + b, b)
            n2_turn(PAIRS - 3, 0)
            n2_turn(PAIRS - 2, 1, more=False)
            gated("n2", PAIRS - 1, 0)
            barrier(pe, "pe")
            seg_loop("l1")
            h_transpose("n3", 0)
            with pe.Fori(0, HALF) as i:
                for b in range(2):
                    n = i * 2 + b
                    gated("n3", n, b, lambda: h_transpose("n3", n + 1))
            gated("n3", PAIRS - 1, 0)
            barrier(pe, "pe")
            seg_loop("l2")

        @block.scalar
        def _(act):
            A = nc.scalar.activation
            act.sem_inc(sig("w", "copied"), 2)
            for b in range(2):
                act.sem_inc(sig("w", f"stored{b}"), 16)
            act.sem_inc(sig("a", "rowfree"), 2)
            for tag in ("n2", "n3"):
                act.sem_inc(sig(tag, "copiedA"), 2)
            barrier(act, "act")

            def normalise(stage, n, what, out3, in3, func):
                deviation(stage, n, what)
                return normalised(stage, n, what, out3, in3, func)

            def deviation(stage, n, what):
                act.wait_ge(sig(stage, f"{what}_var"), n + 1)
                A(sd[:, :], mv[:, :, 1], ACT.Sqrt, bias=epsc[:, :]).then_inc(sig(stage, f"{what}_sd"), 1)

            def normalised(stage, n, what, out3, in3, func):
                act.wait_ge(sig(stage, f"{what}_scale"), n + 1)
                for a in range(2):
                    last = A(out3[:, a, :], in3[:, a, :], func, bias=nm[:, a:a + 1], scale=rs[:, a:a + 1])
                return last

            def n1_pair(m, b):
                normalise("n1", m, "x", hh, xt[:, b, :, :], ACT.Relu).then_inc(sig("n1", "h"), 1)
                act.wait_ge(sig("n1", "T"), m + 1)
                if b is not None:
                    A(mTs[b][:, :, :, :].rearrange("p a k c -> p (a k c)"), ps[:, 0, :], ACT.Copy).then_inc(sig("n1", "Tc"), 1)

            with act.Fori(0, HALF) as i:
                for b in range(2):
                    n = i * 2 + b
                    n1_pair(n, b)
            n1_pair(PAIRS - 1, 0)
            barrier(act, "act")

            def stage_indices(tag, index, done, unit, i, u):
                if u >= 2:
                    act.wait_ge(done, i * (RING * unit) + (u - 1) * unit)
                nc.scalar.activation(stage[:, u % RING, :], index[:, bass.ds(i * BODY + u * QUAD, QUAD)], ACT.Copy).then_inc(sig(tag, "staged"), 1)

            def one_hots(i, u):
                b = u % 2
                act.wait_ge(sig("a", f"row{b}"), i * 32 + (u // 2 + 1) * 16)
                act.wait_ge(sig("a", "expanded"), i * RING + (u + 1))
                A(ohT[u % RING], bcr[b], ACT.Square, bias=npid[:, :]).then_inc(sig("a", "rowfree"), 1)
                act.wait_ge(sig("a", "rowfree"), i * RING + (u + 3))
                A(ohT[u % RING], ohT[u % RING], ACT.Relu, bias=1.0, scale=-1.0).then_inc(sig("a", "onehot"), 1)

            for u in range(2):
                stage_indices("a", si, None, 1, 0, u)
            for u in range(2):
                one_hots(0, u)

            def a_turn(i, l, last=False):
                for u in range(RING):
                    stage_indices("a", si, sig("a", "scored"), 1, i, u + 2)
                    if not last or u + 2 < RING:
                        one_hots(i, u + 2)
                    if l is not None and u >= 2:
                        b, copied = u - 2, sig("w", "copied")
                        act.wait_ge(sig("w", "product"), i * 2 + (b + 3))
                        act.wait_ge(sig("w", f"stored{b}"), i * 16 + 16)
                        A(wout[b], ps[0:4 * NREL, 6 + b, :], ACT.Copy).then_inc(copied, 1)
                        act.wait_ge(copied, i * 2 + (b + 3))
                        act.dma_start(w_d[l][:, bass.ds((i - l * WTURNS) * (2 * WP) + b * WP, WP)], wout[b]).then_inc(sig("w", f"stored{b}"), 16)

            for l in range(2):
                with act.Fori(l * WTURNS, (l + 1) * WTURNS) as i:
                    a_turn(i, l)
            with act.Fori(2 * WTURNS, TURNS - 1) as i:
                a_turn(i, None)
            a_turn(TURNS - 1, None, last=True)
            for b in range(2):
                act.wait_ge(sig("w", f"stored{b}"), 16 + 16 * 2 * WTURNS)
            barrier(act, "act")

            for g in range(SG):
                if g == 0:
                    for u in range(2):
                        stage_indices("b", si, None, QUAD, 0, u)
                act.wait_ge(sig("m", "transposed"), g + 1)
                A(sx[0][:, :, g, :], ps[:, g % 2, :].rearrange("p (h c) -> p h c", h=HEADS), ACT.Copy).then_inc(sig("m", "copied"), 1)
            act.wait_ge(sig("m", "shifted"), 1)
            A(accf[:, 0:SG * 512], accf[:, 0:SG * 512], ACT.Exp).then_inc(sig("m", "exp"), 1)
            for g in range(SG):
                act.wait_ge(sig("m", "back_T"), g + 1)
                A(sc[:, g * P:(g + 1) * P, :].rearrange("p s h -> p h s"), ps[:, g % 2, :].rearrange("p (h c) -> p h c", h=HEADS),
                  ACT.Copy).then_inc(sig("m", "back"), 1)
            barrier(act, "act")

            def seg_loop(tag, index):
                added = sig(tag, "added")
                if tag != "b":
                    for u in range(2):
                        stage_indices(tag, index, None, QUAD, 0, u)
                with act.Fori(0, TURNS) as i:
                    for u in range(RING):
                        stage_indices(tag, index, added, QUAD, i, u + 2)
                        act.wait_ge(added, i * BODY + (u + 1) * QUAD)
                        for k in range(QUAD):
                            last = A(oh[:, u % 2, k, :], iotaj[:, :], ACT.Square, scale=-1.0, bias=dl[:, bass.ds(i * BODY + u * QUAD + k, 1)])
                        last.then_inc(sig(tag, "squared"), 1)
                        act.wait_ge(sig(tag, "squared"), i * RING + (u + 1))
                        A(oh[:, u % 2, :, :], oh[:, u % 2, :, :], ACT.Relu, bias=1.0, scale=-1.0).then_inc(sig(tag, "onehot"), 1)
                barrier(act, "act")

            seg_loop("b", si)

            def h_copy(tag, b):
                A(hTs[b][:, :, :, :].rearrange("p a k c -> p (a k c)"), ps[:, 0, :], ACT.Copy).then_inc(sig(tag, "hTc"), 1)

            def gate_of(tag, n):
                act.wait_ge(sig(tag, "root"), n + 1)
                act.wait_ge(sig(tag, "copiedV"), n * 3 + 2)
                act.wait_ge(sig(tag, "copiedA"), n * 3 + 2)
                A(gate[:, :, :], ps[:, 1:3, D:D + NREL], ACT.Sigmoid, bias=gb[:, :]).then_inc(sig(tag, "gate"), 1)
                act.wait_ge(sig(tag, "gate"), n + 1)

            def scaled(tag, n, j):
                a, c = j // 3, j % 3
                act.wait_ge(sig(tag, "xw"), n * 6 + (j + 1))
                if j in (0, 4):
                    act.wait_ge(sig(tag, f"stored{a}"), n * 16 + 16)
                for e in range(2):
                    r = 2 * c + e
                    last = A(gout[:, a, r, :], ps[:, 3 + c, e * D:(e + 1) * D], ACT.Copy, scale=gate[:, a, r:r + 1])
                last.then_inc(sig(tag, "copiedA"), 1)

            def n2_copy(m):
                act.wait_ge(sig("n2", "T"), m + 1)
                A(mTs[0][:, :, :, :].rearrange("p a k c -> p (a k c)"), ps[:, 6, :], ACT.Copy).then_inc(sig("n2", "Tc"), 1)

            def n2_h0(m, b):
                normalised("n2", m, "x", h0, xt[:, b, :, :], ACT.Relu).then_inc(sig("n2", "h0"), 1)

            def n2_middle(m, b):
                normalise("n2", m, "u", vt[:, b, :, :], uu, ACT.Identity).then_inc(sig("n2", "un"), 1)

            def n2_last(m, b):
                normalise("n2", m, "y", hh, uu, ACT.Relu).then_inc(sig("n2", "h"), 1)

            def n2_hT(m, b):
                act.wait_ge(sig("n2", "hT"), m + 1)
                h_copy("n2", b)

            def n2_turn(n, b, more=True):
                gate_of("n2", n)
                scaled("n2", n, 0)
                n2_middle(n + 1, 1 - b)
                scaled("n2", n, 2)
                if more:
                    n2_copy(n + 2)
                n2_last(n + 1, 1 - b)
                if more:
                    deviation("n2", n + 2, "x")
                n2_hT(n + 1, 1 - b)
                if more:
                    n2_h0(n + 2, b)
                scaled("n2", n, 4)

            deviation("n2", 0, "x")
            n2_h0(0, 0)
            n2_copy(0)
            n2_middle(0, 0)
            n2_last(0, 0)
            deviation("n2", 1, "x")
            n2_h0(1, 1)
            n2_copy(1)
            n2_hT(0, 0)
            with act.Fori(0, HALF - 1) as i:
                for b in range(2):
                    n2_turn(i * 2 + b, b)
            n2_turn(PAIRS - 3, 0)
            n2_turn(PAIRS - 2, 1, more=False)
            gate_of("n2", PAIRS - 1)
            for j in (0, 2, 4):
                scaled("n2", PAIRS - 1, j)
            barrier(act, "act")
            seg_loop("l1", ci)
            act.wait_ge(sig("n3", "hT"), 1)
            h_copy("n3", 0)
            with act.Fori(0, HALF) as i:
                for b in range(2):
                    n = i * 2 + b
                    gate_of("n3", n)
                    scaled("n3", n, 0)
                    scaled("n3", n, 2)
                    act.wait_ge(sig("n3", "hT"), n + 2)
                    h_copy("n3", 1 - b)
                    scaled("n3", n, 4)
            gate_of("n3", PAIRS - 1)
            for j in (0, 2, 4):
                scaled("n3", PAIRS - 1, j)
            barrier(act, "act")
            seg_loop("l2", ci)

        @block.vector
        def _(dve):
            V = nc.vector
            seq = Steps(dve, sem("dve_steps"))
            dve.sem_inc(sig("a", "scored"), 2)
            dve.sem_inc(sig("a", "multiplied"), 2)
            for tag in ("b", "l1", "l2"):
                dve.sem_inc(sig(tag, "added"), 2 * QUAD)
            dve.sem_inc(sig("n1", "used"), 2)
            for tag in ("n2", "n3"):
                dve.sem_inc(sig(tag, "rootused"), 1)
                dve.sem_inc(sig(tag, "copiedV"), 2)
            V.memset(att[:, :, :], 0.0).then_inc(sig("pre", "att0"), 1)
            V.memset(zpad, 0.0).then_inc(sig("pre", "pads"), 1)
            V.memset(dpad[:, 0:P], PAD_DST).then_inc(sig("pre", "pads"), 1)
            V.memset(dpad[:, P:2 * P], 0).then_inc(sig("pre", "pads"), 1)
            seq(V.memset(epsc[:, :], EPS))
            seq(V.memset(ones[:, :], 1.0))
            seq(V.memset(zrow, 0.0))
            dve.wait_ge(sig("pre", "lohi"), 32)
            seq.then(V.tensor_scalar(lohi_i, lohi_i, 7, None, ALU.arith_shift_right))
            seq.then(V.tensor_copy(lohi, lohi_i))
            lo, hi = lohi[:, 0:CHUNKS], lohi[:, CHUNKS:2 * CHUNKS]
            seq.then(V.scalar_tensor_tensor(ncount, hi, 1.0, lo, ALU.add, ALU.subtract))
            seq.then(V.tensor_tensor_scan(hi, ncount, zrow, 0.0, ALU.add, ALU.add))
            seq.then(V.tensor_tensor(pd[:, 0, :], hi, ncount, ALU.subtract))
            V.tensor_tensor(pd[:, 1, :], lo, pd[:, 0, :], ALU.subtract).then_inc(sig("idx", "pd"), 1)
            dve.wait_ge(sig("idx", "pd_everywhere"), 1)
            seq.then(V.tensor_copy(pdb[:, :, :].rearrange("p a (c n) -> p a c n", c=2), ps[:, 4:8, 0:H2].rearrange("p (a c) n -> p a c n", a=2)))
            dve.wait_ge(sig("pre", "constants"), 1)
            for g in range(SG):
                seq.then(V.tensor_scalar(junk, pdb[:, 0, :], scol[:, g:g + 1], None, ALU.is_le, ALU.add, accum_out=cnt[:, g:g + 1]))
            seq.then(V.tensor_scalar(cnt[:, :], cnt[:, :], -1.0, None, ALU.add))
            for g in range(SG):
                seq.then(V.scalar_tensor_tensor(junk, iotac, cnt[:, g:g + 1], pdb[:, 1, :], ALU.is_equal, ALU.mult, accum_out=dsel[:, g:g + 1]))
            V.tensor_copy(chunk_i[:, :], cnt[:, :]).then_inc(sig("idx", "chunks"), 1)
            seq.then(V.tensor_tensor(dsel[:, :], dsel[:, :], scol[:, :], ALU.add))
            seq.then(V.tensor_scalar(tilec[:, :], dsel[:, :], float(TILES - 1), None, ALU.min))
            seq.then(V.tensor_scalar(inr[:, :], dsel[:, :], float(P), None, ALU.mult))
            dve.wait_ge(sig("idx", "records"), 16 * SG)
            seq.then(V.tensor_copy(srcf, recs[:, :, 0:P]))
            seq.then(V.tensor_tensor(loc_row[:, :, 0:P], srcf, inr[:, :, None].to_broadcast([P, SG, P]), ALU.subtract))
            seq.then(V.tensor_scalar(key, loc_row[:, :, 0:P], 0.0, None, ALU.is_ge))
            seq.then(V.scalar_tensor_tensor(key, loc_row[:, :, 0:P], float(P), key, ALU.is_lt, ALU.mult))
            seq.then(V.scalar_tensor_tensor(key, srcf, 1.0, key, ALU.add, ALU.mult))
            seq.then(V.tensor_copy(combf, recs[:, :, 2 * P:3 * P]))
            seq.then(V.tensor_copy(srcf, recs[:, :, P:2 * P]))
            seq.then(V.scalar_tensor_tensor(combf, combf, float(ROWS), srcf, ALU.mult, ALU.add))
            V.tensor_copy(loc_row[:, :, P:2 * P], recs[:, :, 3 * P:4 * P]).then_inc(sig("idx", "rows"), 1)
            seq.then(V.tensor_tensor(rsx[:, :, 1:P], key[:, :, 1:P], key[:, :, 0:P - 1], ALU.not_equal))
            seq.then(V.tensor_scalar(rsx[:, :, 1:P], rsx[:, :, 1:P], -BIG, None, ALU.mult))
            dve.wait_ge(sig("idx", "edges_T"), 1)
            seq(V.tensor_copy(trow[:, :], psf[0:1, 0:SP_]))
            seq.then(V.tensor_copy(krow, psf[0:1, 1024:3072].rearrange("p (a c) -> p a c", a=2)[:, :, 0:SP_]))
            seq(V.memset(crow[:, 0:1], -BIG))
            seq(V.memset(crow[:, SP_:SP_ + 1], -BIG))
            seq.then(V.tensor_tensor(crow[:, 1:SP_], krow[:, 0, 1:SP_], krow[:, 1, 0:SP_ - 1], ALU.not_equal))
            V.tensor_scalar(crow[:, 1:SP_], crow[:, 1:SP_], -BIG, None, ALU.mult).then_inc(sig("idx", "crow"), 1)
            dve.wait_ge(sig("idx", "ccol"), 1)
            seq(V.tensor_copy(rsx[:, :, 0:1], ps[:, 6, 0:SG][:, :, None]))
            seq.then(V.tensor_copy(rsx[:, :, P:P + 1], ps[:, 6, 8:8 + SG][:, :, None]))
            for r in range(2):
                seq.then(V.tensor_reduce(inr[:, :], rsx[:, :, r:P + r], AX, ALU.min))
                seq.then(V.tensor_copy(gmc[:, r, :, :], inr[:, :, None].to_broadcast([P, SG, HEADS])))
            for a, t in enumerate((dl, si, ci)):
                dve.wait_ge(sig("idx", "transposed"), a + 1)
                seq(V.tensor_copy(t[:, :], psf[:, a * 1024:a * 1024 + SP_]))
            dve.wait_ge(sig("pre", "params"), 16 * 12)
            for t, f in ((wbig[:, :, 0:D], HD ** -0.5), (bqkv[:, 0:D], HD ** -0.5), (rel[:, :], 0.2), (qcol[:, :], 0.1)):
                seq(V.tensor_scalar(t, t, f, None, ALU.mult))
            seq.settle()
            V.tensor_copy(mTs[0][:, :, 0, :], qcol[:, :, None].to_broadcast([P, 2, P])).then_inc(sig("pre", "qcols"), 1)
            dve.wait_ge(sig("pre", "qproduct"), 1)
            seq.then(V.tensor_tensor(bqkv[:, :], bqkv[:, :], psf[:, 1024:1024 + 3 * D], ALU.add))
            barrier(dve, "dve")

            def moments(stage, n, what, in3):
                statistics(stage, what, in3)
                scales(stage, n, what)

            def statistics(stage, what, in3):
                for a in range(2):
                    seq(V.bn_stats(st6[:, a, :], in3[:, a, :]))
                seq.settle()
                dve.sem_inc(sig("dve", "go"), 1)
                seq(V.bn_aggr(mv[:, 0, :], st6[:, 0, :]))
                V.bn_aggr(mv[:, 1, :], st6[:, 1, :]).then_inc(sig(stage, f"{what}_var"), 1)

            def scales(stage, n, what):
                dve.wait_ge(sig(stage, f"{what}_sd"), n + 1)
                seq.then(V.reciprocal(rs[:, :], sd[:, :]))
                V.scalar_tensor_tensor(nm[:, :], mv[:, :, 0], -1.0, rs[:, :], ALU.mult, ALU.mult).then_inc(sig(stage, f"{what}_scale"), 1)

            bc2 = lambda v: v[:, None, :].to_broadcast([P, 2, D])

            def n1_moments(i, m, b):
                dve.wait_ge(sig("n1", f"tile{b}"), i * 16 + 16)
                moments("n1", m, "x", xt[:, b, :, :])

            def n1_finish(n, between=None):
                for a in range(2):
                    if a and between:
                        between()
                    dve.wait_ge(sig("n1", f"stored{a}"), n * 32 + 32)
                    dve.wait_ge(sig("n1", "qkv"), n * 2 + (a + 1))
                    seq(V.tensor_tensor(qr[:, bass.ds(n * 2 + a, 1), :].rearrange("p a c -> p (a c)"), ps[:, 1 + 2 * a, 0:D], bqkv[:, 0:D], ALU.add))
                    seq(V.tensor_tensor(kvo[:, a, 0:D], ps[:, 1 + 2 * a, D:2 * D], bqkv[:, D:2 * D], ALU.add))
                    V.tensor_tensor(kvo[:, a, D:2 * D], ps[:, 2 + 2 * a, 0:D], bqkv[:, 2 * D:3 * D], ALU.add).then_inc(sig("n1", "used"), 1)

            n1_moments(0, 0, 0)
            n1_moments(0, 1, 1)
            with dve.Fori(0, HALF - 1) as i:
                seq.enter(i, 2 * 8)
                for b in range(2):
                    n = i * 2 + b
                    n1_finish(n, lambda: n1_moments(i + 1, n + 2, b))
            seq.leave(HALF - 1)
            n1_finish(PAIRS - 3, lambda: n1_moments(HALF, PAIRS - 1, 0))
            n1_finish(PAIRS - 2)
            n1_finish(PAIRS - 1)
            seq.settle()
            dve.wait_ge(sig("n1", "used"), 2 + 2 * PAIRS)
            barrier(dve, "dve")

            seq.then(V.memset(sc[:, STEPS:SP_, :], 0.0))
            added, weighed = sig("a", "relation_added"), sig("a", "multiplied")

            def keys(u):
                return gbuf[:, u * QUAD:(u + 1) * QUAD, 0:D]

            def add_relation(i, u):
                b, k4 = u % 2, keys(u).rearrange("p k (h d) -> p k h d", h=HEADS)
                dve.wait_ge(sig("a", f"gathered{u}"), i * 64 + 64)
                dve.wait_ge(sig("a", "expanded"), i * RING + (u + 1 + RING))
                V.tensor_tensor(k4, k4, ps[:, 4 + b, 0:QUAD * HD].rearrange("p (k d) -> p k d", k=QUAD)[:, :, None, :]
                                .to_broadcast([P, QUAD, HEADS, HD]), ALU.add).then_inc(added, 1)

            def times_q(i, u):
                b = u % 2
                dve.wait_ge(added, i * RING + (u + 1))
                V.tensor_tensor(keys(u), keys(u), psf[:, b * 1024:(b + 1) * 1024].rearrange("p (k c) -> p k c", k=QUAD),
                                ALU.mult).then_inc(weighed, 1)

            def head_sums(i, u):
                dve.wait_ge(weighed, i * RING + (u + 3))
                V.tensor_reduce(sc[:, bass.ds(i * BODY + u * QUAD, QUAD), :], keys(u).rearrange("p k (h d) -> p k h d", h=HEADS),
                                AX, ALU.add).then_inc(sig("a", "scored"), 1)

            def a_turn(i, last):
                for u in range(RING):
                    if last and u == RING - 1:
                        head_sums(i, u)
                        continue
                    i1, u1 = i + (u + 1) // RING, (u + 1) % RING
                    add_relation(i1, u1)
                    head_sums(i, u)
                    times_q(i1, u1)

            add_relation(0, 0)
            times_q(0, 0)
            with dve.Fori(0, TURNS - 1) as i:
                a_turn(i, False)
            a_turn(TURNS - 1, True)
            dve.wait_ge(sig("a", "scored"), 2 + RING * TURNS)
            barrier(dve, "dve")

            def scans(r, carried):
                for g in range(SG):
                    for h in range(HEADS):
                        first = ccol[:, g, h:h + 1] if carried else -BIG
                        if r == 0:
                            seq(V.tensor_tensor_scan(sx[1][:, h, g, :], rsx[:, g, 0:P], sx[0][:, h, g, :], first, ALU.add, ALU.max))
                        else:
                            seq(V.tensor_tensor_scan(sx[2][:, h, g, ::-1], rsx[:, g, P:0:-1], sx[1][:, h, g, ::-1], first, ALU.add, ALU.max))
                seq.settle()

            dve.wait_ge(sig("m", "copied"), SG)
            for r in range(2):
                scans(r, False)
                end = P - 1 if r == 0 else 0
                V.tensor_copy(lcol[:, :, :], sx[1 + r][:, :, :, end].rearrange("p h g -> p g h")).then_inc(sig("m", "last"), 1)
                dve.wait_ge(sig("m", "last_T"), r + 1)
                seq(V.tensor_copy(ltrow, psf[0:HEADS, 1024:1024 + SP_]))
                seq(V.tensor_copy(grow, psf[0:HEADS, 2048:2048 + SP_]))
                seq.then(V.memset(carry[:, (0 if r == 0 else SP_):(1 if r == 0 else SP_ + 1)], -BIG))
                if r == 0:
                    V.tensor_tensor_scan(carry[:, 1:SP_ + 1], grow, ltrow, -BIG, ALU.add, ALU.max).then_inc(sig("m", "carry"), 1)
                else:
                    V.tensor_tensor_scan(carry[:, 0:SP_][:, ::-1], grow[:, ::-1], ltrow[:, ::-1], -BIG, ALU.add, ALU.max).then_inc(sig("m", "carry"), 1)
                dve.wait_ge(sig("m", "carry_T"), r + 1)
                seq.then(V.tensor_copy(ccol[:, :, :], ps[:, 7, 0:SG * HEADS].rearrange("p (g h) -> p g h", h=HEADS)))
                scans(r, True)
            V.tensor_tensor(accf[:, 0:SG * 512], accf[:, 0:SG * 512], accf[:, 2 * SG * 512:3 * SG * 512], ALU.subtract).then_inc(sig("m", "shifted"), 1)
            dve.wait_ge(sig("m", "shifted"), 1)
            seq.then(V.memset(accf[:, SG * 512:], 0.0))
            barrier(dve, "dve")

            def gate_columns(l, k):
                dve.wait_ge(sig(f"g{l}", "loaded"), 8 * 16)
                w6 = wbig[:, k, :].rearrange("p (r o) -> p r o", r=NREL)
                for r0, r1, room in ((0, 4, xt), (4, NREL, vt)):
                    part = room[:, :, :, :].rearrange("p b a c -> p (b a) c")[:, 0:r1 - r0, :]
                    seq.then(V.tensor_tensor(part, w6[:, r0:r1, :], vecs[:, 4, :][:, None, :].to_broadcast([P, r1 - r0, D]), ALU.mult))
                    seq.then(V.tensor_reduce(wroot[:, k, D + r0:D + r1], part, AX, ALU.add))

            def seg_loop(tag):
                if tag != "b":
                    V.memset(gbuf[:, :, D:AW], 1.0).then_inc(sig(tag, "ones"), 1)
                seq.then(V.memset(accf[:, 0:SG * 512] if tag == "b" else accf, 0.0))
                added, total = sig(tag, "added"), sig(tag, "sum")

                def weight(i, u):
                    at = bass.ds(i * BODY + u * QUAD, QUAD)
                    dve.wait_ge(sig(tag, f"gathered{u}"), i * 64 + 64)
                    v4 = gbuf[:, u * QUAD:(u + 1) * QUAD, 0:D].rearrange("p k (h d) -> p k h d", h=HEADS)
                    V.tensor_tensor(v4, v4, sc[:, at, :][:, :, :, None].to_broadcast([P, QUAD, HEADS, HD]), ALU.mult)
                    V.tensor_copy(gbuf[:, u * QUAD:(u + 1) * QUAD, D:AW], sc[:, at, :]).then_inc(sig(tag, "weighted"), 1)

                def add(i, u):
                    _, tile_of = nc.values_load_multi_w_load_instructions(
                        trow[0:1, bass.ds(i * BODY + u * QUAD, QUAD)], engines=(dve.engine,), min_val=0, max_val=TILES - 1,
                        skip_runtime_bounds_check_because="clamped when made")
                    for k in range(QUAD):
                        at = acc[:, bass.ds(tile_of[k], 1), :].rearrange("p a c -> p (a c)")
                        dve.wait_ge(total, i * BODY + (u * QUAD + k + 1))
                        dve.wait_ge(added, i * BODY + (2 * QUAD + u * QUAD + k))
                        V.tensor_tensor(at, ps[:, 4 * (u % 2) + k, 0:AW], at, ALU.add).then_inc(added, 1)

                def turn(i, last):
                    for u in range(RING):
                        if tag == "b" and not (last and u == RING - 1):
                            weight(i + (u + 1) // RING, (u + 1) % RING)
                        add(i, u)

                if tag == "b":
                    weight(0, 0)
                def residual(i):
                    at = qr[:, bass.ds(i * 2, 2), :]
                    dve.wait_ge(sig("l2", "x1"), i * 16 + 16)
                    V.tensor_tensor(at, at, xt[:, 0, :, :], ALU.add).then_inc(sig("l2", "residual"), 1)

                with dve.Fori(0, PAIRS) as i:
                    turn(i, False)
                    if tag == "l2":
                        residual(i)
                if tag == "l2":
                    stops = (PAIRS, TURNS - 1)
                else:
                    stops = (PAIRS, PAIRS + 12, TURNS - 1)
                for k, (start, stop) in enumerate(zip(stops, stops[1:])):
                    if tag != "l2":
                        gate_columns(0 if tag == "b" else 1, k)
                    with dve.Fori(start, stop) as i:
                        turn(i, False)
                turn(TURNS - 1, True)
                dve.wait_ge(added, 2 * QUAD + STEPS)
                barrier(dve, "dve")

            def root_of(tag, n):
                dve.wait_ge(sig(tag, "root"), n + 1)
                dve.wait_ge(sig(tag, "gate"), n + 1)
                V.tensor_tensor(qr[:, bass.ds(n * 2, 2), :], ps[:, 1:3, 0:D], bc2(vecs[:, 3, :]), ALU.add).then_inc(sig(tag, "rootused"), 1)

            def scaled(tag, n, j):
                a, c = j // 3, j % 3
                dve.wait_ge(sig(tag, "xw"), n * 6 + (j + 1))
                if j in (1, 3):
                    dve.wait_ge(sig(tag, f"stored{a}"), n * 16 + 16)
                V.tensor_tensor(gout[:, a, 2 * c:2 * c + 2, :], ps[:, 3 + c, :].rearrange("p (e o) -> p e o", e=2),
                                gate[:, a, 2 * c:2 * c + 2][:, :, None].to_broadcast([P, 2, D]), ALU.mult).then_inc(sig(tag, "copiedV"), 1)

            seg_loop("b")

            def n2_messages(i, n, b):
                v2 = vt[:, b, :, :]
                a2 = acc[:, bass.ds(n * 2, 2), 0:D].rearrange("p a (h d) -> p a h d", h=HEADS)
                w2 = acc[:, bass.ds(n * 2, 2), D:AW]
                wide = lambda t: t[:, :, :, None].to_broadcast([P, 2, HEADS, HD])
                dve.wait_ge(sig("n2", f"tile{b}"), i * 32 + 32)
                if not (isinstance(n, int) and n == 0):
                    dve.wait_ge(sig("n2", "T"), n)
                seq(V.tensor_scalar(zer[:, :, :], w2, 0.0, None, ALU.is_equal))
                seq.then(V.tensor_scalar(den[:, :, :], w2, 1e-30, None, ALU.max))
                seq.then(V.reciprocal(den[:, :, :], den[:, :, :]))
                m4 = mm[:, :, :].rearrange("p a (h d) -> p a h d", h=HEADS)
                v4 = v2.rearrange("p a (h d) -> p a h d", h=HEADS)
                seq(V.tensor_tensor(m4, a2, wide(den[:, :, :]), ALU.mult))
                seq.then(V.tensor_tensor(v4, v4, wide(zer[:, :, :]), ALU.mult))
                V.tensor_tensor(mm[:, :, :], mm[:, :, :], v2, ALU.add).then_inc(sig("n2", "operand"), 1)

            def n2_residual(n):
                dve.wait_ge(sig("n2", "o"), n + 1)
                dve.wait_ge(sig("n2", "x1stored"), n * 16 + 16)
                seq.then(V.tensor_tensor(uu[:, :, :], ps[:, 7, :].rearrange("p (a c) -> p a c", a=2), bc2(vecs[:, 0, :]), ALU.add))
                dve.wait_ge(sig("n2", "h0"), n + 1)
                seq.then(V.tensor_tensor(uu[:, :, :], uu[:, :, :], h0[:, :, :], ALU.add))
                statistics("n2", "u", uu)

            def n2_norm(n, b):
                x2, v2 = xt[:, b, :, :], vt[:, b, :, :]
                scales("n2", n, "u")
                dve.wait_ge(sig("n2", "un"), n + 1)
                seq.then(V.tensor_tensor(v2, v2, bc2(vecs[:, 1, :]), ALU.mult))
                seq.then(V.tensor_tensor(v2, v2, bc2(vecs[:, 2, :]), ALU.add))
                V.tensor_tensor(uu[:, :, :], x2, v2, ALU.add).then_inc(sig("n2", "x1"), 1)

            def n2_x(n, b):
                moments("n2", n, "x", xt[:, b, :, :])

            def n2_y(n):
                dve.wait_ge(sig("n2", "x1"), n + 1)
                moments("n2", n, "y", uu)

            def n2_turn(i, n, b, more=True):
                if more:
                    n2_messages(i + 1, n + 2, b)
                n2_residual(n + 1)
                root_of("n2", n)
                scaled("n2", n, 1)
                n2_norm(n + 1, 1 - b)
                n2_y(n + 1)
                if more:
                    n2_x(n + 2, b)
                scaled("n2", n, 3)
                scaled("n2", n, 5)

            n2_messages(0, 0, 0)
            n2_x(0, 0)
            n2_residual(0)
            n2_norm(0, 0)
            n2_y(0)
            n2_messages(0, 1, 1)
            n2_x(1, 1)
            with dve.Fori(0, HALF - 1) as i:
                seq.enter(i, 2 * 21)
                for b in range(2):
                    n2_turn(i, i * 2 + b, b)
            seq.leave(HALF - 1)
            n2_turn(HALF - 1, PAIRS - 3, 0)
            n2_turn(HALF - 1, PAIRS - 2, 1, more=False)
            root_of("n2", PAIRS - 1)
            for j in (1, 3, 5):
                scaled("n2", PAIRS - 1, j)
            seq.settle()
            dve.wait_ge(sig("n2", "copiedV"), 2 + 3 * PAIRS)
            barrier(dve, "dve")
            seg_loop("l1")

            def mean_plus_root(n, hh):
                seq.then(V.tensor_scalar(den[:, :, 0:1], acc[:, bass.ds(n * 2, 2), D:D + 1], 1.0, None, ALU.max))
                seq.then(V.reciprocal(den[:, :, 1:2], den[:, :, 0:1]))
                for a in range(2):
                    at = bass.ds(n * 2 + a, 1)
                    seq(V.scalar_tensor_tensor(hh[:, a, :], acc[:, at, 0:D].rearrange("p a c -> p (a c)"), den[:, a, 1:2],
                                               qr[:, at, :].rearrange("p a c -> p (a c)"), ALU.mult, ALU.add))
                seq.settle()

            def n3_h(m):
                if isinstance(m, int):
                    mean_plus_root(m, hh)
                else:
                    dve.wait_ge(sig("n3", "hT"), m)
                    mean_plus_root(m, hh)
                V.tensor_scalar(hh[:, :, :], hh[:, :, :], 0.0, None, ALU.max).then_inc(sig("n3", "h"), 1)

            n3_h(0)
            with dve.Fori(0, PAIRS - 1) as n:
                seq.enter(n, 4)
                n3_h(n + 1)
                root_of("n3", n)
                for j in (1, 3, 5):
                    scaled("n3", n, j)
            seq.leave(PAIRS - 1)
            root_of("n3", PAIRS - 1)
            for j in (1, 3, 5):
                scaled("n3", PAIRS - 1, j)
            dve.wait_ge(sig("n3", "copiedV"), 2 + 3 * PAIRS)
            barrier(dve, "dve")
            seg_loop("l2")

            dve.wait_ge(sig("l2", "residual"), 1 + PAIRS)
            seq.then(V.tensor_scalar(inv[:, :, None], acc[:, :, D:D + 1], 1.0, None, ALU.max))
            seq.then(V.reciprocal(inv[:, :], inv[:, :]))

            def n4_mean(m):
                at = acc[:, bass.ds(m * 2, 2), 0:D]
                V.tensor_tensor(at, at, inv[:, bass.ds(m * 2, 2)][:, :, None].to_broadcast([P, 2, D]), ALU.mult).then_inc(sig("n4", "mean"), 1)

            def n4_sum(n):
                at = bass.ds(n * 2, 2)
                dve.wait_ge(sig("n4", "mean"), n + 1)
                V.tensor_tensor(qr[:, at, :], qr[:, at, :], acc[:, at, 0:D], ALU.add).then_inc(sig("n4", "ready"), 1)

            n4_mean(0)
            with dve.Fori(0, PAIRS - 1) as n:
                n4_mean(n + 1)
                n4_sum(n)
            n4_sum(PAIRS - 1)


_INS = ['x', 'src', 'dst', 'edge_type_6', 'edge_type_64'] + ['L0_gnn_' + n for n in (
    'query_emb', 'Wq', 'bq', 'Wk', 'bk', 'Wv', 'bv', 'rel_w', 'Wo', 'bo', 'gamma', 'beta')] + [
    'L1_gnn_' + n for n in ('basis1', 'att1', 'root1', 'bias1', 'gate_w1', 'gate_b1',
                            'basis2', 'att2', 'root2', 'bias2', 'gate_w2', 'gate_b2')]


def kernel(**inputs):
    import numpy as _np
    import concourse.bacc as _bacc
    from concourse import mybir as _mybir
    from concourse.bass_utils import run_bass_kernel_spmd as _run

    nc = _bacc.Bacc("TRN2", target_bir_lowering=False, num_devices=1)
    arrays, args = {}, []
    for name in _INS:
        a = _np.ascontiguousarray(inputs[name])
        arrays[f"in_{name}"] = a
        args.append(nc.dram_tensor(f"in_{name}", a.shape, _mybir.dt.from_np(a.dtype), kind="ExternalInput").ap())
    o = nc.dram_tensor("out", (N, D), _mybir.dt.float32, kind="ExternalOutput").ap()
    build(nc, *args, o)
    r = _run(nc, [arrays], core_ids=[0])
    return r.results[0]["out"]
```
